# Optimizing a Trainium2 kernel written in Bass

```python
import numpy as np
import jax
import jax.numpy as jnp

def _softmax(x, axis=-1):
    return jax.nn.softmax(x, axis=axis)

def _gelu(x):
    return jax.nn.gelu(x, approximate=True)

def _silu(x):
    return jax.nn.silu(x)

def _sigmoid(x):
    return jax.nn.sigmoid(x)

def _layernorm(x, axis=-1, eps=1e-05):
    m = jnp.mean(x, axis=axis, keepdims=True)
    v = jnp.var(x, axis=axis, keepdims=True)
    return (x - m) / jnp.sqrt(v + eps)

def _scatter_add(tgt, idx, src, axis=0):
    return tgt.at[idx].add(src)

def _segment_sum(src, seg, n):
    return jax.ops.segment_sum(src, seg, n)
kernel_name = 'mk_decoder_postln_d1_seqx_r8_474e57'

def setup_inputs(seed: int=0):
    np.random.seed(seed)
    _w = jnp.asarray

    def _rec_inputs():
        import jax
        import jax.numpy as jnp
        _rk = jax.random.key(seed)
        x = -0.0005207 + 1.001 * jax.random.normal(jax.random.fold_in(_rk, 1), (8, 128, 512), jnp.float32)
        _lenS = 128 - jax.random.randint(jax.random.fold_in(_rk, 7), (8,), 0, max(1, 128 // 4) + 1, jnp.int32)
        _lenS2 = 128 - jax.random.randint(jax.random.fold_in(_rk, 8), (8,), 0, max(1, 128 // 4) + 1, jnp.int32)
        _ctx_4096P = jax.random.normal(jax.random.fold_in(_rk, 11), (8, 16, 512), jnp.float32)
        _ctx_4096c = jax.random.dirichlet(jax.random.fold_in(_rk, 511), 0.3 * jnp.ones((16,), jnp.float32), (8, 128))
        _ctx_4096t = jnp.einsum('bsk,bkd->bsd', _ctx_4096c, _ctx_4096P)
        _ctx_4096t = _ctx_4096t * jax.lax.rsqrt(jnp.mean(jnp.square(_ctx_4096t)) + 1e-12) * 0.953939
        ctx_4096 = -0.00010331 + 0.999899 * (_ctx_4096t + 0.3 * jax.random.normal(jax.random.fold_in(_rk, 611), (8, 128, 512), jnp.float32))
        return (x, ctx_4096)
    x, ctx_4096 = _rec_inputs()

    def _L0_attn_setup():
        import jax, jax.numpy as jnp
        import numpy as np
        import math
        B, T, D_IN, D_OUT = (2, 256, 512, 512)
        N_HEADS, N_KV = (32, 8)
        HEAD_DIM = D_OUT // N_HEADS
        GROUP_SIZE = N_HEADS // N_KV
        ROPE_BASE = 500000.0
        CTX = 256

        def _rope_tables(head_dim, base, seq_len):
            inv_freq = 1.0 / base ** (jnp.arange(0, head_dim, 2, dtype=jnp.float32) / head_dim)
            t = jnp.arange(seq_len, dtype=jnp.float32)
            freqs = jnp.einsum('i,j->ij', t, inv_freq)
            return (jnp.cos(freqs), jnp.sin(freqs))

        def _apply_rope(x, cos, sin):
            x1, x2 = jnp.split(x, 2, axis=-1)
            c = cos[None, None]
            s = sin[None, None]
            return jnp.concatenate([x1 * c - x2 * s, x1 * s + x2 * c], axis=-1)
        key = jax.random.key(seed)
        ks = jax.random.split(key, 5)
        scale = 0.02
        return {'x': jax.random.normal(ks[0], (B, T, D_IN), dtype=jnp.float32), 'Wq': jax.random.normal(ks[1], (D_IN, D_OUT), dtype=jnp.float32) * scale, 'Wk': jax.random.normal(ks[2], (D_IN, N_KV * HEAD_DIM), dtype=jnp.float32) * scale, 'Wv': jax.random.normal(ks[3], (D_IN, N_KV * HEAD_DIM), dtype=jnp.float32) * scale, 'Wo': jax.random.normal(ks[4], (D_OUT, D_OUT), dtype=jnp.float32) * scale}
    _L0_attn_all = _L0_attn_setup()
    _L0_attn_in = {k: v for k, v in _L0_attn_all.items() if k in ('Wq', 'Wk', 'Wv', 'Wo')}
    del _L0_attn_all

    def _L0_xattn_setup():
        import jax, jax.numpy as jnp
        import numpy as np
        import math
        HIDDEN = 512
        N_HEADS = 32
        HEAD_DIM = 128
        N_KV_HEADS = 4
        N_GROUPS = N_HEADS // N_KV_HEADS
        key = jax.random.key(seed)
        ks = jax.random.split(key, 6)
        B, NL, S = (8, 64, 512)
        latents = jax.random.normal(ks[0], (B, NL, HIDDEN), dtype=jnp.float32)
        context = jax.random.normal(ks[1], (B, S, HIDDEN), dtype=jnp.float32)
        scale = 1.0 / math.sqrt(HIDDEN)
        Wq = jax.random.normal(ks[2], (HIDDEN, N_HEADS * HEAD_DIM), dtype=jnp.float32) * scale
        Wk = jax.random.normal(ks[3], (HIDDEN, N_KV_HEADS * HEAD_DIM), dtype=jnp.float32) * scale
        Wv = jax.random.normal(ks[4], (HIDDEN, N_KV_HEADS * HEAD_DIM), dtype=jnp.float32) * scale
        Wo = jax.random.normal(ks[5], (N_HEADS * HEAD_DIM, HIDDEN), dtype=jnp.float32) * scale
        return {'latents': latents, 'context': context, 'Wq': Wq, 'Wk': Wk, 'Wv': Wv, 'Wo': Wo}
    _L0_xattn_all = _L0_xattn_setup()
    _L0_xattn_in = {k: v for k, v in _L0_xattn_all.items() if k in ('Wq', 'Wk', 'Wv', 'Wo')}
    del _L0_xattn_all

    def _L0_ffn_setup():
        import jax, jax.numpy as jnp
        import numpy as np
        B, S, D_IN, D_OUT = (2, 256, 512, 512)
        E, K, R = (8, 2, 16)
        SCALING = 32.0 / 16.0
        key = jax.random.key(seed)
        ks = jax.random.split(key, 6)
        x = jax.random.normal(ks[0], (B, S, D_IN), dtype=jnp.float32)
        gate_w = jax.random.normal(ks[1], (E, D_IN), dtype=jnp.float32) * 0.02
        base_w = jax.random.normal(ks[2], (D_OUT, D_IN), dtype=jnp.float32) * 0.02
        base_b = jax.random.normal(ks[3], (D_OUT,), dtype=jnp.float32) * 0.02
        lora_A = jax.random.normal(ks[4], (E, R, D_IN), dtype=jnp.float32) * 0.02
        lora_B = jax.random.normal(ks[5], (E, D_OUT, R), dtype=jnp.float32) * 0.02
        return {'x': x, 'gate_w': gate_w, 'base_w': base_w, 'base_b': base_b, 'lora_A': lora_A, 'lora_B': lora_B}
    _L0_ffn_all = _L0_ffn_setup()
    _L0_ffn_in = {k: v for k, v in _L0_ffn_all.items() if k in ('gate_w', 'base_w', 'base_b', 'lora_A', 'lora_B')}
    del _L0_ffn_all
    return {'x': x, 'ctx_4096': ctx_4096, 'L0_attn_Wq': _L0_attn_in['Wq'], 'L0_attn_Wk': _L0_attn_in['Wk'], 'L0_attn_Wv': _L0_attn_in['Wv'], 'L0_attn_Wo': _L0_attn_in['Wo'], 'L0_xattn_Wq': _L0_xattn_in['Wq'], 'L0_xattn_Wk': _L0_xattn_in['Wk'], 'L0_xattn_Wv': _L0_xattn_in['Wv'], 'L0_xattn_Wo': _L0_xattn_in['Wo'], 'L0_ffn_gate_w': _L0_ffn_in['gate_w'], 'L0_ffn_base_w': _L0_ffn_in['base_w'], 'L0_ffn_base_b': _L0_ffn_in['base_b'], 'L0_ffn_lora_A': _L0_ffn_in['lora_A'], 'L0_ffn_lora_B': _L0_ffn_in['lora_B']}

def reference(x, ctx_4096, L0_attn_Wq, L0_attn_Wk, L0_attn_Wv, L0_attn_Wo, L0_xattn_Wq, L0_xattn_Wk, L0_xattn_Wv, L0_xattn_Wo, L0_ffn_gate_w, L0_ffn_base_w, L0_ffn_base_b, L0_ffn_lora_A, L0_ffn_lora_B):
    import jax
    import jax.numpy as jnp

    def _L0_attn_ref(x, Wq, Wk, Wv, Wo):
        import jax, jax.numpy as jnp
        import numpy as np
        import math
        B, T, D_IN, D_OUT = (2, 256, 512, 512)
        N_HEADS, N_KV = (32, 8)
        HEAD_DIM = D_OUT // N_HEADS
        GROUP_SIZE = N_HEADS // N_KV
        ROPE_BASE = 500000.0
        CTX = 256

        def _rope_tables(head_dim, base, seq_len):
            inv_freq = 1.0 / base ** (jnp.arange(0, head_dim, 2, dtype=jnp.float32) / head_dim)
            t = jnp.arange(seq_len, dtype=jnp.float32)
            freqs = jnp.einsum('i,j->ij', t, inv_freq)
            return (jnp.cos(freqs), jnp.sin(freqs))

        def _apply_rope(x, cos, sin):
            x1, x2 = jnp.split(x, 2, axis=-1)
            c = cos[None, None]
            s = sin[None, None]
            return jnp.concatenate([x1 * c - x2 * s, x1 * s + x2 * c], axis=-1)
        b, t, _ = x.shape
        cos, sin = _rope_tables(HEAD_DIM, ROPE_BASE, t)
        q = (x @ Wq).reshape(b, t, N_HEADS, HEAD_DIM).transpose(0, 2, 1, 3)
        k = (x @ Wk).reshape(b, t, N_KV, HEAD_DIM).transpose(0, 2, 1, 3)
        v = (x @ Wv).reshape(b, t, N_KV, HEAD_DIM).transpose(0, 2, 1, 3)
        q = _apply_rope(q, cos, sin)
        k = _apply_rope(k, cos, sin)
        k_h = jnp.repeat(k, GROUP_SIZE, axis=1)
        v_h = jnp.repeat(v, GROUP_SIZE, axis=1)
        scores = jnp.einsum('bhqd,bhkd->bhqk', q, k_h) / math.sqrt(HEAD_DIM)
        causal = jnp.triu(jnp.ones((t, t), dtype=bool), k=1)
        scores = jnp.where(causal[None, None], jnp.finfo(scores.dtype).min, scores)
        attn = jax.nn.softmax(scores, axis=-1)
        ctx = jnp.einsum('bhqk,bhkd->bhqd', attn, v_h)
        ctx = ctx.transpose(0, 2, 1, 3).reshape(b, t, D_OUT)
        return ctx @ Wo

    def _L0_xattn_ref(latents, context, Wq, Wk, Wv, Wo):
        import jax, jax.numpy as jnp
        import numpy as np
        import math
        HIDDEN = 512
        N_HEADS = 32
        HEAD_DIM = 128
        N_KV_HEADS = 4
        N_GROUPS = N_HEADS // N_KV_HEADS
        b, q_len, _ = latents.shape
        kv_len = q_len + context.shape[1]
        hidden_states = jnp.concatenate([context, latents], axis=1)
        q = (latents @ Wq).reshape(b, q_len, N_KV_HEADS, N_GROUPS, HEAD_DIM)
        k = (hidden_states @ Wk).reshape(b, kv_len, N_KV_HEADS, HEAD_DIM)
        v = (hidden_states @ Wv).reshape(b, kv_len, N_KV_HEADS, HEAD_DIM)
        scale = 1.0 / math.sqrt(HEAD_DIM)
        scores = jnp.einsum('bqhgd,bkhd->bhgqk', q, k) * scale
        attn = jax.nn.softmax(scores.astype(jnp.float32), axis=-1).astype(q.dtype)
        out = jnp.einsum('bhgqk,bkhd->bqhgd', attn, v)
        out = out.reshape(b, q_len, N_HEADS * HEAD_DIM)
        return out @ Wo

    def _L0_ffn_ref(x, gate_w, base_w, base_b, lora_A, lora_B):
        import jax, jax.numpy as jnp
        import numpy as np
        B, S, D_IN, D_OUT = (2, 256, 512, 512)
        E, K, R = (8, 2, 16)
        SCALING = 32.0 / 16.0
        gate_logits = jnp.einsum('bsd,ed->bse', x, gate_w)
        weights, selected = jax.lax.top_k(gate_logits, K)
        weights = jax.nn.softmax(weights.astype(jnp.float32), axis=2).astype(x.dtype)
        result = jnp.einsum('bsd,od->bso', x, base_w) + base_b
        w_full = jnp.sum(jax.nn.one_hot(selected, E, dtype=x.dtype) * weights[..., None], axis=2)
        low = jnp.einsum('bsd,erd->ebsr', x, lora_A)
        lora_out = jnp.einsum('ebsr,eor,bse->bso', low, lora_B, w_full)
        result = result + SCALING * lora_out
        return result
    x = _layernorm(x + _L0_attn_ref(x, L0_attn_Wq, L0_attn_Wk, L0_attn_Wv, L0_attn_Wo), axis=-1)
    x = _layernorm(x + _L0_xattn_ref(x, ctx_4096, L0_xattn_Wq, L0_xattn_Wk, L0_xattn_Wv, L0_xattn_Wo), axis=-1)
    x = _layernorm(x + _L0_ffn_ref(x, L0_ffn_gate_w, L0_ffn_base_w, L0_ffn_base_b, L0_ffn_lora_A, L0_ffn_lora_B), axis=-1)
    return x

_drawn_inputs = setup_inputs


def setup_inputs(seed=0):
    import zlib

    import numpy as np

    out = dict(_drawn_inputs(seed))
    spreads = {}
    factors = {'L0_attn_Wq': 7.965, 'L0_attn_Wk': 7.669, 'L0_ffn_base_b': 3.303}
    for name, (base, spread) in spreads.items():
        noise = np.random.default_rng([zlib.crc32(name.encode()), seed]).standard_normal(out[name].shape)
        drawn = base * np.exp(spread * noise) if base else spread * noise
        out[name] = jnp.asarray(drawn.astype(out[name].dtype))
    for name, factor in factors.items():
        out[name] = (out[name] * factor).astype(out[name].dtype)
    return out
```

```python
from contextlib import ExitStack

import concourse.bass as bass
from concourse import mybir

F32 = mybir.dt.float32
F32R = mybir.dt.float32r
BF16 = mybir.dt.bfloat16
I32 = mybir.dt.int32
U32 = mybir.dt.uint32
ALU = mybir.AluOpType
ACT = mybir.ActivationFunctionType
AX_X = mybir.AxisListType.X

P = 128
B, T, D = 8, 128, 512
C = D // P
H, KV, HD = 32, 8, 16
GS = H // KV
HALF = HD // 2
KD = KV * HD
UN = 4
UH = H // UN
VW = HD + 2
XH, XG, XD = 32, 4, 128
XHG = XH // XG
PAIRS = XHG // 2
XSCALE = float(XD) ** -0.5
KEYS = 2 * T
E, R, TOPK = 8, 16, 2
ER = E * R
SCALING = 2.0
EPS = 1e-5
GUESS = float(0x5F3759DF - (3 << 23) + (1 << 23) - (1 << 31))

C_COS, C_SIN, C_NSIN, C_IOTA = 0, HD, HD + HALF, HD + 2 * HALF
C_N = C_IOTA + E


def post_ln_decoder(nc, x, context, sa_wq, sa_wk, sa_wv, sa_wo, xa_wq, xa_wk, xa_wv, xa_wo,
                    gate_w, base_w, base_b, lora_a, lora_b, table, mask, out, UPTO=3, LOOPS=False):
    with ExitStack() as ctx:
        def sbuf(name, shape, dt=F32, scope=ctx):
            return scope.enter_context(nc.sbuf_tensor(name, shape, dt))

        def sem(name):
            return ctx.enter_context(nc.semaphore(name))

        bank = [ctx.enter_context(nc.psum_tensor(f"bank{i}", [P, 512], F32)) for i in range(6)]
        score_banks = ctx.enter_context(nc.psum_tensor("score_banks", [P, 2, 512], F32))

        y = sbuf("y", [P, B, D])
        x1h = sbuf("x1h", [P, C, B * T], F32R)
        x1l = sbuf("x1l", [P, C, B * T], F32R)
        ident = sbuf("ident", [P, P])
        identb = sbuf("identb", [P, P], BF16)
        consts = sbuf("consts", [P, C_N])
        one = sbuf("one", [P, 1])
        maskb = sbuf("maskb", [P, P], BF16)
        maskf = sbuf("maskf", [P, P])
        stats = sbuf("stats", [P, B, 6])
        meanvar = sbuf("meanvar", [P, B, 2])
        newton = sbuf("newton", [P, 5, B])

        xwq_raw = sbuf("xwq_raw", [P, C, 2 * XD])
        xwo_raw = sbuf("xwo_raw", [P, 2, D])
        xwkv_raw = sbuf("xwkv_raw", [P, C, 2 * XD])

        pa = ExitStack()
        wqh = sbuf("wqh", [P, C, D], F32R, pa)
        wql = sbuf("wql", [P, C, D], F32R, pa)
        wkvh = sbuf("wkvh", [P, C, 2 * KD], F32R, pa)
        wkvl = sbuf("wkvl", [P, C, 2 * KD], F32R, pa)
        woh = sbuf("woh", [P, C, D], F32R, pa)
        wol = sbuf("wol", [P, C, D], F32R, pa)
        wraw = sbuf("wraw", [P, C * (2 * D + 2 * KD)], F32, pa)
        wq_raw = wraw[:, 0:C * D].rearrange("p (c n) -> p c n", c=C)
        wkv_raw = wraw[:, C * D:C * (D + 2 * KD)].rearrange("p (c n) -> p c n", c=C)
        wo_raw = wraw[:, C * (D + 2 * KD):].rearrange("p (c n) -> p c n", c=C)
        xin = sbuf("xin", [P, D], F32, pa)
        xth = sbuf("xth", [P, C, T], F32R, pa)
        xtl = sbuf("xtl", [P, C, T], F32R, pa)
        rot1 = sbuf("rot1", [P, H + KV, HD], F32, pa)
        rot2 = sbuf("rot2", [P, H + KV, HD], F32, pa)
        roped = sbuf("roped", [P, H + KV, HD], F32, pa)
        qs = sbuf("qs", [P, H, 2, 2, HD], F32R, pa)
        ks = sbuf("ks", [P, KV, 4, 2, HD], F32R, pa)
        qt = sbuf("qt", [P, H // 2, T], F32R, pa)
        kt = sbuf("kt", [P, KV, T], F32R, pa)
        vnext = sbuf("vnext", [P, KV, HD], F32, pa)
        vaug = sbuf("vaug", [P, KV, VW], F32, pa)
        probs = sbuf("probs", [P, 2, UH, T], F32, pa)
        pt = sbuf("pt", [P, UH, T], F32, pa)
        nmax = sbuf("nmax", [P, 2, 2, UH], F32, pa)
        rsum = sbuf("rsum", [P, UH], F32, pa)
        attn = sbuf("attn", [P, D], F32, pa)
        ath = sbuf("ath", [P, C, T], F32R, pa)
        atl = sbuf("atl", [P, C, T], F32R, pa)
        xpre = sbuf("xpre", [P, D], F32, pa)
        xnorm = sbuf("xnorm", [P, D], F32, pa)
        pa.close()

        pb = ExitStack()
        cx_raw = sbuf("cx_raw", [P, 2, D], F32, pb)
        cxh = sbuf("cxh", [P, C, B * T], F32R, pb)
        cxl = sbuf("cxl", [P, C, B * T], F32R, pb)
        kh = sbuf("kh", [P, B, KEYS], F32R, pb)
        kl = sbuf("kl", [P, B, KEYS], F32R, pb)
        vh = sbuf("vh", [P, B, 2, XD], F32R, pb)
        vl = sbuf("vl", [P, B, 2, XD], F32R, pb)
        vfm = sbuf("vfm", [P, 2, 4 * T], F32, pb)
        xwqh = sbuf("xwqh", [P, 2, C, 2 * XD], F32R, pb)
        xwql = sbuf("xwql", [P, 2, C, 2 * XD], F32R, pb)
        xwoh = sbuf("xwoh", [P, 2, 2, D], F32R, pb)
        xwol = sbuf("xwol", [P, 2, 2, D], F32R, pb)
        xwkvh = sbuf("xwkvh", [P, C, 2 * XD], F32R, pb)
        xwkvl = sbuf("xwkvl", [P, C, 2 * XD], F32R, pb)
        xqh = sbuf("xqh", [P, 2, 2, 4 * T], F32R, pb)
        xql = sbuf("xql", [P, 2, 2, 4 * T], F32R, pb)
        xp = sbuf("xp", [P, 2, 2, KEYS], F32, pb)
        xpth = sbuf("xpth", [P, 2, 2 * T], F32R, pb)
        xptl = sbuf("xptl", [P, 2, 2 * T], F32R, pb)
        xoh = sbuf("xoh", [P, 2 * T], F32R, pb)
        xol = sbuf("xol", [P, 2 * T], F32R, pb)
        xmax = sbuf("xmax", [P, 2, 2, 2], F32, pb)
        xsum = sbuf("xsum", [P, 2, 2, 2], F32, pb)
        pb.close()

        pc = ExitStack()
        gate_raw = sbuf("gate_raw", [E, D], F32, pc)
        bias = sbuf("bias", [P, D], F32, pc)
        bwh = sbuf("bwh", [P, C, D], F32R, pc)
        bwl = sbuf("bwl", [P, C, D], F32R, pc)
        agh = sbuf("agh", [P, C, ER + E], F32R, pc)
        agl = sbuf("agl", [P, C, ER + E], F32R, pc)
        lbh = sbuf("lbh", [P, D], F32R, pc)
        lbl = sbuf("lbl", [P, D], F32R, pc)
        x2 = sbuf("x2", [P, 2, D], F32, pc)
        lowg = sbuf("lowg", [P, B, ER + E], F32, pc)
        wlow = sbuf("wlow", [P, B, ER], F32, pc)
        lwh = sbuf("lwh", [P, 2, P], F32R, pc)
        lwl = sbuf("lwl", [P, 2, P], F32R, pc)
        top = sbuf("top", [P, B, 8], F32, pc)
        topi = sbuf("topi", [P, B, 8], U32, pc)
        topf = sbuf("topf", [P, B, TOPK], F32, pc)
        share = sbuf("share", [P, 4, B], F32, pc)
        gates = sbuf("gates", [P, TOPK, B, E], F32, pc)
        pc.close()
        base_raw = (xwq_raw[:].rearrange("p c n -> p (c n)"), xwo_raw[:].rearrange("p c n -> p (c n)"))
        lora_raw = xwkv_raw[:].rearrange("p c n -> p (c n)")
        la_raw, lb_raw = lora_raw[:, 0:D], lora_raw[:, D:2 * D]

        consts_in = sem("consts_in")
        ident_made = sem("ident_made")
        wq_in, wkv_in, wo_in = sem("wq_in"), sem("wkv_in"), sem("wo_in")
        w_hi, w_lo = sem("w_hi"), sem("w_lo")
        x_in, xres_in = sem("x_in"), sem("xres_in")
        xt_ready, xt_hi, xt_split = sem("xt_ready"), sem("xt_hi"), sem("xt_split")
        q_ready, kv_ready = sem("q_ready"), sem("kv_ready")
        roped_q, roped_k, q_hi, k_hi, q_lo, k_lo = (sem(n) for n in ("roped_q", "roped_k", "q_hi", "k_hi", "q_lo", "k_lo"))
        v_copied, v_set = sem("v_copied"), sem("v_set")
        stack_ready, stack_act, stack_dve = sem("stack_ready"), sem("stack_act"), sem("stack_dve")
        scores_ready, max_ready, exp_done = sem("scores_ready"), sem("max_ready"), sem("exp_done")
        pt_ready, pt_copied = sem("pt_ready"), sem("pt_copied")
        pv_ready, attn_set = sem("pv_ready"), sem("attn_set")
        at_ready, at_hi, at_split = sem("at_ready"), sem("at_hi"), sem("at_split")
        proj_ready, y_added, normed, y_set = sem("proj_ready"), sem("y_added"), sem("normed"), sem("y_set")
        x1_ready, x1_hi, x1_split = sem("x1_ready"), sem("x1_hi"), sem("x1_split")
        dve_chain = sem("dve_chain")
        xwq_in, xwo_in, xwkv_in = sem("xwq_in"), sem("xwo_in"), sem("xwkv_in")
        xw_hi, xwq_split, xwo_split, xwkv_split = sem("xw_hi"), sem("xwq_split"), sem("xwo_split"), sem("xwkv_split")
        cx_in = (sem("cx_in0"), sem("cx_in1"))
        cx_ready, cx_hi, cx_split = sem("cx_ready"), sem("cx_hi"), sem("cx_split")
        kv_done, xk_hi, xk_split = sem("kv_done"), sem("xk_hi"), sem("xk_split")
        vfm_copied, vt_ready, xv_hi, xv_split = sem("vfm_copied"), sem("vt_ready"), sem("xv_hi"), sem("xv_split")
        xq_done, xq_hi, xq_split = sem("xq_done"), sem("xq_hi"), sem("xq_split")
        xs_done, xmax_ready, xexp_done, xp_normed = sem("xs_done"), sem("xmax_ready"), sem("xexp_done"), sem("xp_normed")
        xpt_ready, xpt_hi, xpt_split = sem("xpt_ready"), sem("xpt_hi"), sem("xpt_split")
        xo_ready, xo_hi, xo_split = sem("xo_ready"), sem("xo_hi"), sem("xo_split")
        xy_ready, xy_added = sem("xy_ready"), sem("xy_added")
        base_in, lora_in, bias_in = sem("base_in"), sem("lora_in"), sem("bias_in")
        fw_ready, fw_hi, fw_split = sem("fw_ready"), sem("fw_hi"), sem("fw_split")
        x2_normed, x2_ready, x2_hi, x2_split, x2_kept = (sem(n) for n in ("x2_normed", "x2_ready", "x2_hi", "x2_split", "x2_kept"))
        ag_ready, ag_copied = sem("ag_ready"), sem("ag_copied")
        top_ready, top_exp, wlow_set = sem("top_ready"), sem("top_exp"), sem("wlow_set")
        lw_ready, lw_hi, lw_split = sem("lw_ready"), sem("lw_hi"), sem("lw_split")
        ff_ready, ff_added, out_set = sem("ff_ready"), sem("ff_added"), sem("out_set")
        stored = sem("stored")
        block = ctx.enter_context(nc.Block())

        TM, QB, KVB, CT, TP = bank[0], bank[1], bank[2], bank[3], (bank[4], bank[5])
        SC = score_banks
        XQ, XT, XO, XY = (bank[0], bank[1]), bank[2], bank[3], (bank[4], bank[5])

        FW = bank[0:4]
        FX, FG, FY = (bank[0], bank[1]), (bank[2], bank[3]), (SC[:, 0, :], SC[:, 1, :], bank[4][:], bank[5][:])

        NU = PAIRS * B
        NQ = 4 * PAIRS
        NKV = 4

        def block_of(blk):
            return blk % 2, blk // 2
        STACK = (QB, KVB, TM)

        def loop(eng, first, end, body):
            if LOOPS:
                with eng.Fori(first, end) as i:
                    body(i)
            else:
                for i in range(first, end):
                    body(i)

        def chunked(ap):
            return ap[:, :].rearrange("p (c n) -> p c n", c=C)

        def tile(ap, b):
            return ap[b:b + 1, :, :].rearrange("o t n -> (o t) n")

        @block.sync
        def _(sp):
            sp.dma_start(xin[:], tile(x, 0)).then_inc(x_in, 16)
            sp.dma_start(wq_raw, sa_wq.rearrange("(c p) n -> p c n", p=P)).then_inc(wq_in, 16)
            sp.dma_start(consts[:], table).then_inc(consts_in, 16)
            sp.dma_start(maskf[:], mask).then_inc(consts_in, 16)
            sp.dma_start(wkv_raw[:, :, 0:KD], sa_wk.rearrange("(c p) n -> p c n", p=P)).then_inc(wkv_in, 16)
            sp.dma_start(wkv_raw[:, :, KD:], sa_wv.rearrange("(c p) n -> p c n", p=P)).then_inc(wkv_in, 16)
            sp.dma_start(wo_raw, sa_wo.rearrange("(c p) n -> p c n", p=P)).then_inc(wo_in, 16)
            sp.dma_start(y[:], x.rearrange("b t n -> t b n")).then_inc(xres_in, 16)
            for b in range(1, B):
                sp.wait_ge(xt_ready, b)
                sp.dma_start(xin[:], tile(x, b)).then_inc(x_in, 16)

            def load_pair(pair):
                sp.dma_start(xwq_raw[:], xa_wq.rearrange("(c p) n -> p c n", p=P)[:, :, bass.ds(pair * 2 * XD, 2 * XD)])\
                  .then_inc(xwq_in, 16)
                sp.dma_start(xwo_raw[:], xa_wo.rearrange("(h d) n -> d h n", d=XD)[:, bass.ds(pair * 2, 2), :])\
                  .then_inc(xwo_in, 16)

            def load_kv(g):
                for j, w in enumerate((xa_wk, xa_wv)):
                    sp.dma_start(xwkv_raw[:, :, j * XD:(j + 1) * XD],
                                 w.rearrange("(c p) n -> p c n", p=P)[:, :, bass.ds(g * XD, XD)]).then_inc(xwkv_in, 16)

            if UPTO >= 2:
                load_kv(0)
                load_pair(0)
                sp.wait_ge(x1_split, B)
                sp.wait_ge(y_set, B)
                for b in range(B):
                    if b >= 2:
                        sp.wait_ge(cx_ready, b - 1)
                    sp.dma_start(cx_raw[:, b % 2, :], tile(context, b)).then_inc(cx_in[b % 2], 16)

                def pair_loads(g, pairs):
                    for p in pairs:
                        sp.wait_ge(xwo_split, g * PAIRS + p)
                        load_pair(g * PAIRS + p)

                def sp_group(g):
                    pair_loads(g, range(1, PAIRS))
                    sp.wait_ge(xwkv_split, g + 1)
                    load_kv(g + 1)
                    pair_loads(g, [PAIRS])

                loop(sp, 0, XG - 1, sp_group)
                pair_loads(XG - 1, range(1, PAIRS))
            if UPTO == 3:
                sp.wait_ge(xwo_split, XG * PAIRS)
                for i, raw in enumerate(base_raw):
                    sp.dma_start(raw.rearrange("p (c n) -> p c n", c=2),
                                 base_w[2 * i * P:2 * (i + 1) * P, :].rearrange("(c p) n -> p c n", p=P)).then_inc(base_in, 16)
                sp.dma_start(la_raw, lora_a.rearrange("e r n -> (e r) n")).then_inc(lora_in, 16)
                for c in range(C):
                    sp.dma_start(lb_raw[:, c * ER:(c + 1) * ER].rearrange("p (e r) -> p e r", e=E),
                                 lora_b[:, c * P:(c + 1) * P, :].rearrange("e p r -> p e r")).then_inc(lora_in, 16)
                sp.wait_ge(xy_added, XG * NU)
                sp.dma_start(gate_raw[:], gate_w).then_inc(bias_in, 16)
                sp.dma_start(bias[:], base_b.rearrange("(o n) -> o n", o=1).to_broadcast([P, D])).then_inc(bias_in, 16)
                for b in range(B):
                    sp.wait_ge(out_set, b + 1)
                    sp.dma_start(tile(out, b), y[:, b, :]).then_inc(stored, 16)
                sp.wait_ge(stored, 16 * B)
            if UPTO == 2:
                sp.wait_ge(xy_added, XG * NU)
                sp.dma_start(out.rearrange("b t n -> t b n"), y[:]).then_inc(stored, 16)
                sp.wait_ge(stored, 16)
            if UPTO == 1:
                sp.wait_ge(y_set, B)
                sp.dma_start(out.rearrange("b t n -> t b n"), y[:]).then_inc(stored, 16)
                sp.wait_ge(stored, 16)

        @block.gpsimd
        def _(pool):
            pool.memset(ident[:], 0.0).then_inc(ident_made, 1)
            pool.memset(vaug[:], 0.0).then_inc(ident_made, 1)
            pool.memset(one[:], 1.0).then_inc(ident_made, 1)
            pool.wait_ge(ident_made, 3)
            pool.affine_select(out=ident[:], in_=ident[:], compare_op=ALU.not_equal, fill=1.0, base=0,
                               pattern=[[-1, P]], channel_multiplier=1).then_inc(ident_made, 1)
            pool.memset(vaug[:, :, HD:HD + 1], 1.0).then_inc(ident_made, 1)
            pool.wait_ge(ident_made, 5)
            pool.tensor_copy(identb[:], ident[:]).then_inc(ident_made, 1)

            def low_parts(b):
                pool.wait_ge(q_hi, b + 1)
                pool.tensor_tensor(qs[:, :, 1, :, :], roped[:, 0:H, :].unsqueeze(2).to_broadcast([P, H, 2, HD]),
                                   qs[:, :, 0, :, :].bitcast(F32), ALU.subtract).then_inc(q_lo, 1)
                pool.wait_ge(k_hi, b + 1)
                pool.tensor_tensor(ks[:, :, :, 1, :], roped[:, H:, :].unsqueeze(2).to_broadcast([P, KV, 4, HD]),
                                   ks[:, :, :, 0, :].bitcast(F32), ALU.subtract).then_inc(k_lo, 1)

            def set_v(b):
                if b >= 1:
                    pool.wait_ge(pv_ready, UN * b)
                pool.wait_ge(v_copied, b + 1)
                pool.tensor_copy(vaug[:, :, 0:HD], vnext[:]).then_inc(v_set, 1)

            def keep_norm(b):
                pool.wait_ge(normed, b + 1)
                pool.tensor_copy(y[:, b, :], xnorm[:]).then_inc(y_set, 1)

            low_parts(0)
            set_v(0)
            for b in range(B):
                if b + 1 < B:
                    low_parts(b + 1)
                    set_v(b + 1)
                if b >= 1:
                    keep_norm(b - 1)
            keep_norm(B - 1)
            if UPTO < 2:
                return

            def split(raw, hi, lo, done):
                pool.tensor_tensor(hi, raw, one[:].unsqueeze(2).to_broadcast(raw.shape), ALU.mult).then_inc(xw_hi, 1)
                hi_count[0] += 1
                pool.wait_ge(xw_hi, hi_base[0] + hi_count[0])
                pool.tensor_tensor(lo, raw, hi.bitcast(F32), ALU.subtract).then_inc(done, 1)

            hi_base, hi_count = [0], [0]

            def split_kv(g):
                pool.wait_ge(xwkv_in, 32 * g + 32)
                split(xwkv_raw[:], xwkvh[:], xwkvl[:], xwkv_split)

            def split_pair(g, p):
                pair = g * PAIRS + p
                pool.wait_ge(xwq_in, 16 * pair + 16)
                split(xwq_raw[:], xwqh[:, p % 2], xwql[:, p % 2], xwq_split)
                pool.wait_ge(xwo_in, 16 * pair + 16)
                split(xwo_raw[:], xwoh[:, p % 2], xwol[:, p % 2], xwo_split)

            def late_pairs(g):
                for p in (2, 3):
                    pool.wait_ge(xq_done, g * NQ + 4 * (p - 1))
                    pool.wait_ge(xy_ready, g * NU + B * (p - 1))
                    split_pair(g, p)

            def pool_group(g):
                hi_base[0], hi_count[0] = 5 + g * 9, 0
                late_pairs(g)
                pool.wait_ge(kv_done, g * 2 * NKV + 2 * NKV)
                split_kv(g + 1)
                for p in (0, 1):
                    pool.wait_ge(xq_done, g * NQ + 4 * (p + 3))
                    pool.wait_ge(xy_ready, g * NU + B * (p + 3))
                    split_pair(g + 1, p)

            pool.wait_ge(x1_split, B)
            split_kv(0)
            split_pair(0, 0)
            split_pair(0, 1)
            loop(pool, 0, XG - 1, pool_group)
            hi_base[0], hi_count[0] = 5 + (XG - 1) * 9, 0
            late_pairs(XG - 1)
            if UPTO < 3:
                return

            pool.wait_ge(bias_in, 32)
            for b in range(B):
                pool.wait_ge(x2_normed, b + 1)
                pool.tensor_tensor(y[:, b, :], x2[:, b % 2, :], bias[:], ALU.add).then_inc(x2_kept, 1)

        @block.tensor
        def _(pe):
            def three_passes(o, pairs, n):
                last = None
                for i, ((lh, ll), (rh, rl)) in enumerate(pairs):
                    pe.matmul(o, ll, rh, start=(i == 0), stop=False)
                    pe.matmul(o, lh, rl, start=False, stop=False)
                    last = pe.matmul(o, lh, rh, start=False, stop=(i == n - 1))
                return last

            def transpose4(dst, srcs):
                for j, s in enumerate(srcs):
                    last = pe.transpose(dst[:, j * P:(j + 1) * P], s, ident[:])
                return last

            def x_transpose(b):
                pe.wait_ge(x_in, 16 * (b + 1))
                if b >= 1:
                    pe.wait_ge(stack_act, 3 * b - 2)
                transpose4(QB, [xin[:, c * P:(c + 1) * P] for c in range(C)]).then_inc(xt_ready, 1)

            def project_q(b):
                pe.wait_ge(xt_split, b + 1)
                three_passes(QB[:], [((xth[:, c, :], xtl[:, c, :]), (wqh[:, c, :], wql[:, c, :])) for c in range(C)],
                             C).then_inc(q_ready, 1)

            def project_kv(b):
                if b >= 1:
                    pe.wait_ge(stack_act, 3 * b - 1)
                three_passes(KVB[:, 0:2 * KD],
                             [((xth[:, c, :], xtl[:, c, :]), (wkvh[:, c, :], wkvl[:, c, :])) for c in range(C)],
                             C).then_inc(kv_ready, 1)

            def stack_transpose(b):
                qf = qs[:].bitcast(F32).rearrange("p (j h) a e d -> p j (h a e d)", h=2)
                kf = ks[:].bitcast(F32).rearrange("p g a e d -> p g (a e d)")
                blocks = [qf[:, j, :] for j in range(H // 2)] + [kf[:, g, :] for g in range(KV)]
                for g in range(6):
                    if g == 0:
                        pe.wait_ge(q_lo, b + 1)
                    if g == 1:
                        pe.wait_ge(roped_k, b + 1)
                    if g == 2 and b == 1:
                        pe.wait_ge(stack_act, 3)
                    if g == 2 and b >= 2:
                        pe.wait_ge(y_added, b - 1)
                    if g == 4:
                        pe.wait_ge(k_lo, b + 1)
                    if g >= 3:
                        pe.wait_ge(stack_dve, 3 * b + g - 2)
                    transpose4(STACK[g % 3], blocks[4 * g:4 * g + 4]).then_inc(stack_ready, 1)

            def scores(n):
                b, k = n // UN, n % UN
                if k == 0:
                    pe.wait_ge(stack_act, 3 * b + 3)
                    pe.wait_ge(stack_dve, 3 * b + 3)
                if n >= 1:
                    pe.wait_ge(exp_done, n)
                for odd in range(2):
                    pe.matmul(SC[:, odd, :], identb[:], maskb[:].unsqueeze(1).to_broadcast([P, 4, T]),
                              start=True, stop=False, skip_group_check=True)
                for i in range(UH // 2):
                    for odd in range(2):
                        h = UH * k + 2 * i + odd
                        rows = slice(64 * odd, 64 * odd + 64)
                        last = pe.matmul(SC[:, odd, i * T:(i + 1) * T], qt[rows, h // 2, :], kt[rows, h // GS, :],
                                         start=False, stop=True, skip_group_check=True)
                last.then_inc(scores_ready, 1)

            def probs_transpose(n):
                pe.wait_ge(exp_done, n + 1)
                for g in range(2):
                    if n >= 1:
                        pe.wait_ge(pt_copied, 2 * n - 1 + g)
                    transpose4(TP[g], [probs[:, n % 2, 4 * g + j, :] for j in range(4)]).then_inc(pt_ready, 1)

            def weigh_values(n):
                b, k = n // UN, n % UN
                pe.wait_ge(pt_copied, 2 * n + 2)
                if k == 0:
                    pe.wait_ge(v_set, b + 1)
                if n >= 1:
                    pe.wait_ge(attn_set, n)
                for s in range(UH):
                    h = UH * k + 2 * (s % 4) + s // 4
                    last = pe.matmul(CT[:, s * VW:(s + 1) * VW], pt[:, s, :], vaug[:, h // GS, :],
                                     start=True, stop=True)
                last.then_inc(pv_ready, 1)

            def attn_transpose(b):
                pe.wait_ge(attn_set, UN * (b + 1))
                if b == 0:
                    pe.wait_ge(stack_act, 6)
                else:
                    pe.wait_ge(x1_split, b)
                transpose4(TM, [attn[:, c * P:(c + 1) * P] for c in range(C)]).then_inc(at_ready, 1)

            def project_out(b):
                pe.wait_ge(at_split, b + 1)
                three_passes(TM[:], [((ath[:, c, :], atl[:, c, :]), (woh[:, c, :], wol[:, c, :])) for c in range(C)],
                             C).then_inc(proj_ready, 1)

            def norm_transpose(b):
                pe.wait_ge(normed, b + 1)
                if b + 2 < B:
                    pe.wait_ge(stack_act, 3 * b + 9)
                transpose4(TM, [xnorm[:, c * P:(c + 1) * P] for c in range(C)]).then_inc(x1_ready, 1)

            pe.wait_ge(ident_made, 6)
            x_transpose(0)
            pe.wait_ge(w_lo, 1)
            project_q(0)
            pe.wait_ge(w_lo, 2)
            project_kv(0)
            stack_transpose(0)
            x_transpose(1)
            scores(0)
            for b in range(B):
                n = UN * b
                scores(n + 1)
                probs_transpose(n)
                if b >= 2:
                    norm_transpose(b - 2)
                if b + 1 < B:
                    project_q(b + 1)
                if b >= 1:
                    attn_transpose(b - 1)
                weigh_values(n)

                scores(n + 2)
                probs_transpose(n + 1)
                if b + 1 < B:
                    project_kv(b + 1)
                if b == 1:
                    pe.wait_ge(w_lo, 3)
                if b >= 1:
                    project_out(b - 1)
                weigh_values(n + 1)

                scores(n + 3)
                probs_transpose(n + 2)
                if b + 1 < B:
                    stack_transpose(b + 1)
                weigh_values(n + 2)

                if b + 1 < B:
                    scores(n + 4)
                probs_transpose(n + 3)
                if b + 2 < B:
                    x_transpose(b + 2)
                weigh_values(n + 3)
            norm_transpose(B - 2)
            attn_transpose(B - 1)
            project_out(B - 1)
            norm_transpose(B - 1)
            if UPTO < 2:
                return

            pe.wait_ge(x1_split, B)
            for b in range(B):
                pe.wait_ge(cx_in[b % 2], 16 * (b // 2 + 1))
                if b >= 2:
                    pe.wait_ge(cx_split, b - 1)
                transpose4(XT if b % 2 == 0 else XO, [cx_raw[:, b % 2, c * P:(c + 1) * P] for c in range(C)])\
                    .then_inc(cx_ready, 1)
            pe.wait_ge(cx_split, B)

            def passes(lh, ll, rh, rl):
                return [(ll, rh), (lh, rl), (lh, rh)]

            def run(o, ops, first=True, last=True):
                for i, (l, r) in enumerate(ops):
                    mm = pe.matmul(o, l, r, start=(first and i == 0), stop=(last and i == len(ops) - 1),
                                   skip_group_check=True)
                return mm

            def project_block(g, blk, j):
                src, half = block_of(blk)
                sh, sl = ((cxh, cxl), (x1h, x1l))[src]
                cols, toks = slice(j * XD, (j + 1) * XD), slice(half * 4 * T, (half + 1) * 4 * T)
                if blk >= 1:
                    pe.wait_ge((xk_split, vfm_copied)[j], g * NKV + blk)
                ops = []
                for c in range(C):
                    ops += passes(xwkvh[:, c, cols], xwkvl[:, c, cols], sh[:, c, toks], sl[:, c, toks])
                run(XQ[j][:], ops).then_inc(kv_done, 1)

            def values_transpose(g, blk):
                pe.wait_ge(vfm_copied, g * NKV + blk + 1)
                if blk >= 1:
                    pe.wait_ge(xv_split, g * NKV + blk)
                transpose4(XT, [vfm[:, blk % 2, t * T:(t + 1) * T] for t in range(4)]).then_inc(vt_ready, 1)

            def project_queries(g, part):
                h, quarter = part // 4, part % 4
                j = quarter // 2
                toks = slice((h % 2) * 4 * T, (h % 2 + 1) * 4 * T)
                w = (h // 2) % 2
                if quarter == 0 and h % 2 == 0:
                    pe.wait_ge(xwq_split, g * PAIRS + h // 2 + 1)
                if quarter % 2 == 0:
                    if h >= 1:
                        pe.wait_ge(xq_split, g * NQ + 2 * (h - 1) + j + 1)
                    else:
                        pe.wait_ge((xk_split, vfm_copied)[j], g * NKV + NKV)
                ops = []
                for c in range(C):
                    cols = slice(j * XD, (j + 1) * XD)
                    ops += passes(xwqh[:, w, c, cols], xwql[:, w, c, cols], x1h[:, c, toks], x1l[:, c, toks])
                n = len(ops) // 2
                if quarter % 2 == 0:
                    run(XQ[j][:], ops[:n], last=False)
                else:
                    run(XQ[j][:], ops[n:], first=False).then_inc(xq_done, 1)

            def cross_scores(g, u):
                b, h = u % B, u // 4
                toks = slice((u % 4) * T, (u % 4 + 1) * T)
                if u % 4 == 0:
                    pe.wait_ge(xq_split, g * NQ + 2 * h + 2)
                if u == 0:
                    pe.wait_ge(xk_split, g * NKV + NKV)
                if u >= 2:
                    pe.wait_ge(xexp_done, g * NU + u - 1)
                for j in range(2):
                    mm = run(SC[:, u % 2, j * KEYS:(j + 1) * KEYS],
                             passes(xqh[:, h % 2, j, toks], xql[:, h % 2, j, toks], kh[:, b, :], kl[:, b, :]))
                mm.then_inc(xs_done, 1)

            def cross_transpose(g, u):
                pe.wait_ge(xp_normed, g * NU + u + 1)
                if u >= 1:
                    pe.wait_ge(xpt_split, g * NU + u)
                else:
                    pe.wait_ge(xv_split, g * NKV + NKV)
                transpose4(XT, [xp[:, u % 2, j, c * T:(c + 1) * T] for c in range(2) for j in range(2)])\
                    .then_inc(xpt_ready, 1)

            def cross_values(g, u):
                pe.wait_ge(xpt_split, g * NU + u + 1)
                if u >= 1:
                    pe.wait_ge(xo_split, g * NU + u)
                ops = []
                for c in range(2):
                    ops += passes(vh[:, u % B, c, :], vl[:, u % B, c, :], xpth[:, c, :], xptl[:, c, :])
                run(XO[:, 0:2 * T], ops).then_inc(xo_ready, 1)

            def cross_out(g, u):
                w = (u // B) % 2
                pe.wait_ge(xo_split, g * NU + u + 1)
                if u % B == 0:
                    pe.wait_ge(xwo_split, g * PAIRS + u // B + 1)
                if u >= 2:
                    pe.wait_ge(xy_added, g * NU + u - 1)
                ops = []
                for j in range(2):
                    cols = slice(j * T, (j + 1) * T)
                    ops += passes(xoh[:, cols], xol[:, cols], xwoh[:, w, j, :], xwol[:, w, j, :])
                run(XY[u % 2][:], ops).then_inc(xy_ready, 1)

            def pe_group(g):
                pe.wait_ge(xwkv_split, g + 1)
                for blk in range(NKV):
                    project_block(g, blk, 0)
                    if blk >= 1:
                        values_transpose(g, blk - 1)
                    project_block(g, blk, 1)
                project_queries(g, 0)
                project_queries(g, 1)
                values_transpose(g, NKV - 1)
                for part in range(2, 5):
                    project_queries(g, part)
                cross_scores(g, 0)
                for u in range(NU):
                    if u + 1 < NU:
                        cross_scores(g, u + 1)
                    cross_transpose(g, u)
                    if u + 5 < 2 * NQ:
                        project_queries(g, u + 5)
                    if u >= 1:
                        cross_out(g, u - 1)
                    cross_values(g, u)
                cross_out(g, NU - 1)
                pe.wait_ge(xy_added, g * NU + NU)

            loop(pe, 0, XG, pe_group)
            if UPTO < 3:
                return

            groups = [[base_raw[oc // 2][:, (oc % 2) * D + c * P:(oc % 2) * D + (c + 1) * P] for oc in range(C)]
                      for c in range(C)]
            groups.append([lb_raw[:, c * P:(c + 1) * P] for c in range(C)])
            groups.append([la_raw[:, c * P:(c + 1) * P] for c in range(C)])
            pe.wait_ge(base_in, 32)
            for i, srcs in enumerate(groups):
                if i == 4:
                    pe.wait_ge(lora_in, 16 * (C + 1))
                if i >= 4:
                    pe.wait_ge(fw_split, i - 3)
                transpose4(FW[i % 4], srcs).then_inc(fw_ready, 1)
            pe.wait_ge(bias_in, 32)
            pe.wait_ge(fw_split, 3)
            for c in range(C):
                mm = pe.transpose(FW[2][:, c * E:(c + 1) * E], gate_raw[:, c * P:(c + 1) * P], ident[0:E, 0:E])
            mm.then_inc(fw_ready, 1)

            def x2_transpose(b):
                pe.wait_ge(x2_normed, b + 1)
                if b >= 2:
                    pe.wait_ge(x2_split, b - 1)
                else:
                    pe.wait_ge(fw_split, 5 + b)
                transpose4(FX[b % 2], [x2[:, b % 2, c * P:(c + 1) * P] for c in range(C)]).then_inc(x2_ready, 1)

            def tile_passes(b, wh, wl):
                toks = slice(b * T, (b + 1) * T)
                ops = []
                for c in range(C):
                    ops += passes(x1h[:, c, toks], x1l[:, c, toks], wh[:, c, :], wl[:, c, :])
                return ops

            def low_and_gate(b):
                pe.wait_ge(x2_split, b + 1)
                if b == 0:
                    pe.wait_ge(fw_split, 7)
                if b >= 2:
                    pe.wait_ge(ag_copied, b - 1)
                run(FG[b % 2][:, 0:ER + E], tile_passes(b, agh, agl)).then_inc(ag_ready, 1)

            def base(b):
                if b >= 4:
                    pe.wait_ge(ff_added, b - 3)
                run(FY[b % 4], tile_passes(b, bwh, bwl), last=False)

            def low_transpose(b):
                pe.wait_ge(wlow_set, 1)
                if b >= 2:
                    pe.wait_ge(lw_split, b - 1)
                pe.transpose(FX[b % 2][:, 0:P], wlow[:, b, :], ident[:]).then_inc(lw_ready, 1)

            def lora(b):
                pe.wait_ge(lw_split, b + 1)
                run(FY[b % 4], passes(lwh[:, b % 2, :], lwl[:, b % 2, :], lbh[:], lbl[:]), first=False)\
                    .then_inc(ff_ready, 1)

            x2_transpose(0)
            for b in range(B):
                if b + 1 < B:
                    x2_transpose(b + 1)
                low_and_gate(b)
            for b in range(3):
                base(b)
            low_transpose(0)
            for b in range(B):
                if b + 1 < B:
                    low_transpose(b + 1)
                if b + 3 < B:
                    base(b + 3)
                lora(b)

        @block.scalar
        def _(act):
            def copy(o, i):
                return act.activation(o, i, ACT.Copy)

            def split_weights(n, raw, hi, loaded, count):
                act.wait_ge(loaded, count)
                copy(hi[:], raw).then_inc(w_hi, 1)

            def x_high(b):
                act.wait_ge(xt_ready, b + 1)
                copy(xth[:], chunked(QB)).then_inc(xt_hi, 1)

            def stack_high(b):
                act.wait_ge(roped_q, b + 1)
                copy(qs[:, :, 0, :, :], roped[:, 0:H, :].unsqueeze(2).to_broadcast([P, H, 2, HD])).then_inc(q_hi, 1)
                act.wait_ge(roped_k, b + 1)
                copy(ks[:, :, :, 0, :], roped[:, H:, :].unsqueeze(2).to_broadcast([P, KV, 4, HD])).then_inc(k_hi, 1)

            def copy_v(b):
                act.wait_ge(kv_ready, b + 1)
                if b >= 1:
                    act.wait_ge(v_set, b)
                copy(vnext[:], KVB[:, KD:2 * KD].rearrange("p (g d) -> p g d", g=KV)).then_inc(v_copied, 1)

            def stack_copy(b):
                for g, dst in ((3, qt[:, 12:16, :]), (4, kt[:, 0:4, :]), (5, kt[:, 4:8, :])):
                    act.wait_ge(stack_ready, 6 * b + g + 1)
                    copy(dst, chunked(STACK[g % 3])).then_inc(stack_act, 1)

            def exponentials(n):
                act.wait_ge(max_ready, n + 1)
                if n >= 2:
                    act.wait_ge(pt_ready, 2 * (n - 1))
                for s in range(UH):
                    last = act.activation(probs[:, n % 2, s, :], SC[:, s // 4, (s % 4) * T:(s % 4 + 1) * T], ACT.Exp,
                                          bias=nmax[:, n % 2, 1, s:s + 1], scale=HD ** -0.5)
                last.then_inc(exp_done, 1)

            def pt_copy(n):
                for g in range(2):
                    act.wait_ge(pt_ready, 2 * n + g + 1)
                    copy(pt[:, 4 * g:4 * g + 4, :], chunked(TP[g])).then_inc(pt_copied, 1)

            def attn_high(b):
                act.wait_ge(at_ready, b + 1)
                copy(ath[:], chunked(TM)).then_inc(at_hi, 1)

            def norm_high(b):
                act.wait_ge(x1_ready, b + 1)
                copy(x1h[:, :, b * T:(b + 1) * T], chunked(TM)).then_inc(x1_hi, 1)

            x_high(0)
            split_weights(0, wq_raw, wqh, wq_in, 16)
            split_weights(1, wkv_raw, wkvh, wkv_in, 32)
            act.wait_ge(consts_in, 32)
            copy(maskb[:], maskf[:]).then_inc(w_hi, 1)
            copy_v(0)
            stack_high(0)
            split_weights(2, wo_raw, woh, wo_in, 16)
            stack_copy(0)
            x_high(1)
            exponentials(0)
            for b in range(B):
                n = UN * b
                pt_copy(n)
                if b >= 2:
                    norm_high(b - 2)
                exponentials(n + 1)

                if b >= 1:
                    attn_high(b - 1)
                pt_copy(n + 1)
                exponentials(n + 2)
                if b + 1 < B:
                    copy_v(b + 1)
                    stack_high(b + 1)

                pt_copy(n + 2)
                exponentials(n + 3)
                if b + 1 < B:
                    stack_copy(b + 1)

                pt_copy(n + 3)
                if b + 2 < B:
                    x_high(b + 2)
                if b + 1 < B:
                    exponentials(n + 4)
            norm_high(B - 2)
            attn_high(B - 1)
            norm_high(B - 1)
            if UPTO < 2:
                return

            act.wait_ge(x1_split, B)
            for b in range(B):
                act.wait_ge(cx_ready, b + 1)
                copy(cxh[:, :, b * T:(b + 1) * T], chunked(XT if b % 2 == 0 else XO)).then_inc(cx_hi, 1)

            def keys_high(g, blk):
                src, half = block_of(blk)
                act.wait_ge(kv_done, g * 2 * NKV + 2 * blk + 1)
                copy(kh[:, 4 * half:4 * half + 4, src * T:(src + 1) * T], chunked(XQ[0])).then_inc(xk_hi, 1)

            def values_copy(g, blk):
                act.wait_ge(kv_done, g * 2 * NKV + 2 * blk + 2)
                if blk >= 2:
                    act.wait_ge(vt_ready, g * NKV + blk - 1)
                copy(vfm[:, blk % 2, :], XQ[1][:]).then_inc(vfm_copied, 1)

            def values_high(g, blk):
                src, half = block_of(blk)
                act.wait_ge(vt_ready, g * NKV + blk + 1)
                copy(vh[:, 4 * half:4 * half + 4, src, :], chunked(XT)).then_inc(xv_hi, 1)

            def queries_high(g, h, j):
                act.wait_ge(xq_done, g * NQ + 2 * h + j + 1)
                copy(xqh[:, h % 2, j, :], XQ[j][:]).then_inc(xq_hi, 1)

            def cross_exp(g, u):
                act.wait_ge(xmax_ready, g * NU + u + 1)
                if u >= 2:
                    act.wait_ge(xpt_ready, g * NU + u - 1)
                for j in range(2):
                    last = act.activation(xp[:, u % 2, j, :], SC[:, u % 2, j * KEYS:(j + 1) * KEYS], ACT.Exp,
                                          bias=xmax[:, u % 2, 1, j:j + 1], scale=XSCALE,
                                          accum_out=xsum[:, u % 2, 0, j:j + 1])
                last.then_inc(xexp_done, 1)

            def cross_pt_high(g, u):
                act.wait_ge(xpt_ready, g * NU + u + 1)
                copy(xpth[:], XT[:].rearrange("p (c n) -> p c n", c=2)).then_inc(xpt_hi, 1)

            def cross_o_high(g, u):
                act.wait_ge(xo_ready, g * NU + u + 1)
                copy(xoh[:], XO[:, 0:2 * T]).then_inc(xo_hi, 1)

            def act_group(g):
                for blk in range(NKV):
                    keys_high(g, blk)
                    if blk >= 1:
                        values_high(g, blk - 1)
                    values_copy(g, blk)
                queries_high(g, 0, 0)
                values_high(g, NKV - 1)
                queries_high(g, 0, 1)
                cross_exp(g, 0)
                for u in range(NU):
                    cross_pt_high(g, u)
                    if u + 1 < NU:
                        cross_exp(g, u + 1)
                    if u + 5 < 2 * NQ and (u + 5) % 2 == 1:
                        queries_high(g, (u + 5) // 4, (u + 5) % 4 // 2)
                    cross_o_high(g, u)

            loop(act, 0, XG, act_group)
            if UPTO < 3:
                return

            act.wait_ge(xy_added, XG * NU)
            for i in range(7):
                act.wait_ge(fw_ready, i + 1)
                if i < 4:
                    copy(bwh[:, i, :], FW[i % 4][:]).then_inc(fw_hi, 1)
                elif i == 4:
                    copy(lbh[:], FW[0][:]).then_inc(fw_hi, 1)
                elif i == 5:
                    copy(agh[:, :, 0:ER], chunked(FW[1])).then_inc(fw_hi, 1)
                else:
                    copy(agh[:, :, ER:], FW[2][:, 0:C * E].rearrange("p (c e) -> p c e", c=C)).then_inc(fw_hi, 1)

            def x2_high(b):
                act.wait_ge(x2_ready, b + 1)
                copy(x1h[:, :, b * T:(b + 1) * T], chunked(FX[b % 2])).then_inc(x2_hi, 1)

            x2_high(0)
            for b in range(B):
                if b + 1 < B:
                    x2_high(b + 1)
                act.wait_ge(ag_ready, b + 1)
                copy(lowg[:, b, :], FG[b % 2][:, 0:ER + E]).then_inc(ag_copied, 1)
            act.wait_ge(top_ready, 1)
            act.activation(share[:, 1, :], share[:, 0, :], ACT.Exp).then_inc(top_exp, 1)
            for b in range(B):
                act.wait_ge(lw_ready, b + 1)
                if b >= 2:
                    act.wait_ge(ff_ready, b - 1)
                copy(lwh[:, b % 2, :], FX[b % 2][:, 0:P]).then_inc(lw_hi, 1)

        @block.vector
        def _(dve):
            chain, links = [0], [0]

            def link(ins):
                chain[0] += 1
                ins.then_inc(dve_chain, 1)
                dve.wait_ge(dve_chain, links[0] + chain[0])

            def low(o, whole, high):
                return dve.tensor_tensor(o, whole, high.bitcast(F32), ALU.subtract)

            def x_low(b):
                dve.wait_ge(xt_hi, b + 1)
                low(xtl[:], chunked(QB), xth[:]).then_inc(xt_split, 1)

            def rope(b, src, lo, hi, ready, done, others):
                heads = hi - lo
                v = src.rearrange("p (h d) -> p h d", h=heads)
                cos = consts[:, C_COS:C_COS + HD].unsqueeze(1).to_broadcast([P, heads, HD])
                nsin = consts[:, C_NSIN:C_NSIN + HALF].unsqueeze(1).to_broadcast([P, heads, HALF])
                sin = consts[:, C_SIN:C_SIN + HALF].unsqueeze(1).to_broadcast([P, heads, HALF])
                dve.wait_ge(ready, b + 1)
                for s in others:
                    if b >= 1:
                        dve.wait_ge(s, b)
                dve.tensor_tensor(rot1[:, lo:hi, :], v, cos, ALU.mult)
                dve.tensor_tensor(rot2[:, lo:hi, 0:HALF], v[:, :, HALF:], nsin, ALU.mult)
                link(dve.tensor_tensor(rot2[:, lo:hi, HALF:], v[:, :, 0:HALF], sin, ALU.mult))
                dve.tensor_tensor(roped[:, lo:hi, :], rot1[:, lo:hi, :], rot2[:, lo:hi, :], ALU.add).then_inc(done, 1)

            def rope_q(b):
                rope(b, QB[:], 0, H, q_ready, roped_q, (q_lo,))

            def rope_k(b):
                dve.wait_ge(v_copied, b + 1)
                rope(b, KVB[:, 0:KD], H, H + KV, kv_ready, roped_k, (k_lo,))

            def stack_copy(b):
                for g in range(3):
                    dve.wait_ge(stack_ready, 6 * b + g + 1)
                    dve.tensor_copy(qt[:, 4 * g:4 * g + 4, :], chunked(STACK[g])).then_inc(stack_dve, 1)

            def maxima(n):
                dve.wait_ge(scores_ready, n + 1)
                if n >= 2:
                    dve.wait_ge(exp_done, n - 1)
                link(dve.tensor_reduce(nmax[:, n % 2, 0, :].rearrange("p (o i) -> p o i", o=2),
                                       SC[:].rearrange("p o (i t) -> p o i t", i=4), AX_X, ALU.max))
                dve.tensor_scalar(nmax[:, n % 2, 1, :], nmax[:, n % 2, 0, :], -HD ** -0.5, None,
                                  ALU.mult).then_inc(max_ready, 1)

            def set_attn(n):
                k = n % UN
                dve.wait_ge(pv_ready, n + 1)
                pv = CT[:, 0:UH * VW].rearrange("p (s v) -> p s v", s=UH)
                link(dve.reciprocal(rsum[:], pv[:, :, HD]))
                for odd in range(2):
                    o = attn[:, k * UH * HD:(k + 1) * UH * HD].rearrange("p (i o d) -> p o i d", o=2, d=HD)[:, odd]
                    last = dve.tensor_tensor(o, pv[:, 4 * odd:4 * odd + 4, 0:HD],
                                             rsum[:, 4 * odd:4 * odd + 4].unsqueeze(2).to_broadcast([P, 4, HD]), ALU.mult)
                last.then_inc(attn_set, 1)

            def attn_low(b):
                dve.wait_ge(at_hi, b + 1)
                low(atl[:], chunked(TM), ath[:]).then_inc(at_split, 1)

            def add_residual(b):
                dve.wait_ge(proj_ready, b + 1)
                dve.tensor_tensor(xpre[:], TM[:], y[:, b, :], ALU.add).then_inc(y_added, 1)

            def rsqrt(n, var):
                a, r = newton[:, 3, 0:n], newton[:, 4, 0:n]
                for i, s in enumerate((4.0, 16.0, 64.0)):
                    last = dve.tensor_scalar(newton[:, i, 0:n], var, EPS, s, ALU.add, ALU.mult)
                link(last)
                link(dve.tensor_scalar(a.bitcast(I32), newton[:, 0, 0:n].bitcast(I32), 1, None, ALU.logical_shift_right))
                link(dve.tensor_scalar(r.bitcast(I32), a.bitcast(I32), -1.0, GUESS, ALU.mult, ALU.add))
                for i in (2, 1, 0):
                    if n == 1:
                        link(dve.scalar_tensor_tensor(a, r, newton[:, i, 0:1], r, ALU.mult, ALU.mult))
                    else:
                        link(dve.tensor_tensor(a, r, r, ALU.mult))
                        link(dve.tensor_tensor(a, a, newton[:, i, 0:n], ALU.mult))
                    link(dve.scalar_tensor_tensor(r, a, -3.0, r, ALU.add, ALU.mult))
                return r

            def layer_norm(b):
                dve.wait_ge(y_added, b + 1)
                link(dve.bn_stats(stats[:, 0, :], xpre[:]))
                link(dve.bn_aggr(meanvar[:, 0, :], stats[:, 0, :]))
                r = rsqrt(1, meanvar[:, 0, 1:2])
                if b >= 1:
                    dve.wait_ge(x1_ready, b)
                    dve.wait_ge(y_set, b)
                dve.tensor_scalar(xnorm[:], xpre[:], meanvar[:, 0, 0:1], r, ALU.subtract, ALU.mult).then_inc(normed, 1)

            def norm_low(b):
                dve.wait_ge(x1_hi, b + 1)
                s = slice(b * T, (b + 1) * T)
                low(x1l[:, :, s], chunked(TM), x1h[:, :, s]).then_inc(x1_split, 1)

            def weights_low(n, raw, hi, lo):
                dve.wait_ge(w_hi, n)
                low(lo[:], raw, hi[:]).then_inc(w_lo, 1)

            x_low(0)
            weights_low(1, wq_raw, wqh, wql)
            weights_low(2, wkv_raw, wkvh, wkvl)
            dve.wait_ge(consts_in, 32)
            rope_q(0)
            rope_k(0)
            stack_copy(0)
            x_low(1)
            maxima(0)
            dve.wait_ge(xres_in, 16)
            for b in range(B):
                n = UN * b
                if b >= 1:
                    set_attn(n - 1)
                maxima(n + 1)
                if b >= 2:
                    norm_low(b - 2)
                if b == 0:
                    weights_low(4, wo_raw, woh, wol)

                set_attn(n)
                if b >= 1:
                    attn_low(b - 1)
                maxima(n + 2)
                if b + 1 < B:
                    rope_q(b + 1)
                    rope_k(b + 1)

                set_attn(n + 1)
                if b >= 1:
                    add_residual(b - 1)
                maxima(n + 3)
                if b + 1 < B:
                    stack_copy(b + 1)

                set_attn(n + 2)
                if b + 1 < B:
                    maxima(n + 4)
                if b + 2 < B:
                    x_low(b + 2)
                if b >= 1:
                    layer_norm(b - 1)
            set_attn(UN * B - 1)
            norm_low(B - 2)
            attn_low(B - 1)
            add_residual(B - 1)
            layer_norm(B - 1)
            norm_low(B - 1)
            if UPTO < 2:
                return

            dve.wait_ge(y_set, B)
            for b in range(B):
                dve.wait_ge(cx_hi, b + 1)
                s = slice(b * T, (b + 1) * T)
                low(cxl[:, :, s], chunked(XT if b % 2 == 0 else XO), cxh[:, :, s]).then_inc(cx_split, 1)

            def keys_low(g, blk):
                src, half = block_of(blk)
                dve.wait_ge(xk_hi, g * NKV + blk + 1)
                at = (slice(None), slice(4 * half, 4 * half + 4), slice(src * T, (src + 1) * T))
                low(kl[at], chunked(XQ[0]), kh[at]).then_inc(xk_split, 1)

            def values_low(g, blk):
                src, half = block_of(blk)
                dve.wait_ge(xv_hi, g * NKV + blk + 1)
                at = (slice(None), slice(4 * half, 4 * half + 4), src)
                low(vl[at], chunked(XT), vh[at]).then_inc(xv_split, 1)

            def queries_low(g, h, j):
                dve.wait_ge(xq_hi, g * NQ + 2 * h + j + 1)
                low(xql[:, h % 2, j, :], XQ[j][:], xqh[:, h % 2, j, :]).then_inc(xq_split, 1)

            def cross_max(g, u):
                dve.wait_ge(xs_done, g * NU + u + 1)
                if u >= 2:
                    dve.wait_ge(xexp_done, g * NU + u - 1)
                link(dve.tensor_reduce(xmax[:, u % 2, 0, :], SC[:, u % 2, :].rearrange("p (j k) -> p j k", j=2),
                                       AX_X, ALU.max))
                dve.tensor_scalar(xmax[:, u % 2, 1, :], xmax[:, u % 2, 0, :], -XSCALE, None, ALU.mult)\
                   .then_inc(xmax_ready, 1)

            def cross_norm(g, u):
                dve.wait_ge(xexp_done, g * NU + u + 1)
                link(dve.reciprocal(xsum[:, u % 2, 1, :], xsum[:, u % 2, 0, :]))
                for j in range(2):
                    last = dve.tensor_scalar(xp[:, u % 2, j, :], xp[:, u % 2, j, :], xsum[:, u % 2, 1, j:j + 1], None,
                                             ALU.mult)
                last.then_inc(xp_normed, 1)

            def cross_pt_low(g, u):
                dve.wait_ge(xpt_hi, g * NU + u + 1)
                low(xptl[:], XT[:].rearrange("p (c n) -> p c n", c=2), xpth[:]).then_inc(xpt_split, 1)

            def cross_o_low(g, u):
                dve.wait_ge(xo_hi, g * NU + u + 1)
                low(xol[:], XO[:, 0:2 * T], xoh[:]).then_inc(xo_split, 1)

            def cross_add(g, u):
                dve.wait_ge(xy_ready, g * NU + u + 1)
                dve.tensor_tensor(y[:, u % B, :], XY[u % 2][:], y[:, u % B, :], ALU.add).then_inc(xy_added, 1)

            chain_base = chain[0]

            def dve_group(g):
                links[0] = chain_base + g * 2 * NU
                chain[0] = 0
                for blk in range(NKV):
                    keys_low(g, blk)
                    if blk >= 1:
                        values_low(g, blk - 1)
                queries_low(g, 0, 0)
                values_low(g, NKV - 1)
                queries_low(g, 0, 1)
                cross_max(g, 0)
                cross_norm(g, 0)
                for u in range(NU):
                    if u + 1 < NU:
                        cross_max(g, u + 1)
                    cross_pt_low(g, u)
                    if u + 1 < NU:
                        cross_norm(g, u + 1)
                    if u + 5 < 2 * NQ and (u + 5) % 2 == 1:
                        queries_low(g, (u + 5) // 4, (u + 5) % 4 // 2)
                    if u >= 1:
                        cross_add(g, u - 1)
                    cross_o_low(g, u)
                cross_add(g, NU - 1)

            loop(dve, 0, XG, dve_group)
            links[0], chain[0] = chain_base + XG * 2 * NU, 0
            if UPTO < 3:
                return

            dve.wait_ge(xy_added, XG * NU)
            for b in range(B):
                last = dve.bn_stats(stats[:, b, :], y[:, b, :])
            link(last)
            for b in range(B):
                last = dve.bn_aggr(meanvar[:, b, :], stats[:, b, :])
            link(last)
            scale = rsqrt(B, meanvar[:, :, 1])

            def x2_norm(b):
                if b >= 2:
                    dve.wait_ge(x2_ready, b - 1)
                    dve.wait_ge(x2_kept, b - 1)
                dve.tensor_scalar(x2[:, b % 2, :], y[:, b, :], meanvar[:, b, 0:1], scale[:, b:b + 1],
                                  ALU.subtract, ALU.mult).then_inc(x2_normed, 1)

            def x2_low(b):
                dve.wait_ge(x2_hi, b + 1)
                s = slice(b * T, (b + 1) * T)
                low(x1l[:, :, s], chunked(FX[b % 2]), x1h[:, :, s]).then_inc(x2_split, 1)

            x2_norm(0)
            x2_norm(1)
            for i in range(7):
                dve.wait_ge(fw_hi, i + 1)
                if i < 4:
                    low(bwl[:, i, :], FW[i % 4][:], bwh[:, i, :]).then_inc(fw_split, 1)
                elif i == 4:
                    low(lbl[:], FW[0][:], lbh[:]).then_inc(fw_split, 1)
                elif i == 5:
                    low(agl[:, :, 0:ER], chunked(FW[1]), agh[:, :, 0:ER]).then_inc(fw_split, 1)
                else:
                    low(agl[:, :, ER:], FW[2][:, 0:C * E].rearrange("p (c e) -> p c e", c=C),
                        agh[:, :, ER:]).then_inc(fw_split, 1)
            for b in range(B):
                x2_low(b)
                if b + 2 < B:
                    x2_norm(b + 2)

            dve.wait_ge(ag_copied, B)
            for b in range(B):
                last = dve.max(top[:, b, :], lowg[:, b, ER:])
            link(last)
            dve.tensor_tensor(share[:, 0, :], top[:, :, 1], top[:, :, 0], ALU.subtract).then_inc(top_ready, 1)
            for b in range(B):
                last = dve.max_index(topi[:, b, :], top[:, b, :], lowg[:, b, ER:])
            link(last)
            link(dve.tensor_copy(topf[:], topi[:, :, 0:TOPK]))
            dve.wait_ge(top_exp, 1)
            link(dve.tensor_scalar(share[:, 2, :], share[:, 1, :], 1.0, 1.0 / SCALING, ALU.add, ALU.mult))
            link(dve.reciprocal(share[:, 2, :], share[:, 2, :]))
            link(dve.tensor_tensor(share[:, 3, :], share[:, 1, :], share[:, 2, :], ALU.mult))
            iota = consts[:, C_IOTA:C_IOTA + E].unsqueeze(1).to_broadcast([P, B, E])
            for i in range(TOPK):
                link(dve.tensor_tensor(gates[:, i], iota, topf[:, :, i].unsqueeze(2).to_broadcast([P, B, E]), ALU.is_equal))
                link(dve.tensor_tensor(gates[:, i], gates[:, i], share[:, 2 + i, :].unsqueeze(2).to_broadcast([P, B, E]),
                                       ALU.mult))
            link(dve.tensor_tensor(gates[:, 0], gates[:, 0], gates[:, 1], ALU.add))
            for e in range(E):
                last = dve.tensor_tensor(wlow[:, :, e * R:(e + 1) * R], lowg[:, :, e * R:(e + 1) * R],
                                         gates[:, 0, :, e].unsqueeze(2).to_broadcast([P, B, R]), ALU.mult)
            last.then_inc(wlow_set, 1)

            def lw_low(b):
                dve.wait_ge(lw_hi, b + 1)
                low(lwl[:, b % 2, :], FX[b % 2][:, 0:P], lwh[:, b % 2, :]).then_inc(lw_split, 1)

            dve.wait_ge(x2_kept, B)
            lw_low(0)
            for b in range(B):
                if b + 1 < B:
                    lw_low(b + 1)
                dve.wait_ge(ff_ready, b + 1)
                dve.tensor_tensor(y[:, b, :], FY[b % 4], y[:, b, :], ALU.add).then_inc(ff_added, 1)
                dve.wait_ge(ff_added, b + 1)
                link(dve.bn_stats(stats[:, b, :], y[:, b, :]))
                last = dve.bn_aggr(meanvar[:, b, :], stats[:, b, :])
                if b % 4 == 3:
                    link(last)
                    scale = rsqrt(4, meanvar[:, b - 3:b + 1, 1])
                    for i in range(4):
                        t = b - 3 + i
                        dve.tensor_scalar(y[:, t, :], y[:, t, :], meanvar[:, t, 0:1], scale[:, i:i + 1],
                                          ALU.subtract, ALU.mult).then_inc(out_set, 1)


_NAMES = ["x", "ctx_4096", "L0_attn_Wq", "L0_attn_Wk", "L0_attn_Wv", "L0_attn_Wo", "L0_xattn_Wq", "L0_xattn_Wk",
          "L0_xattn_Wv", "L0_xattn_Wo", "L0_ffn_gate_w", "L0_ffn_base_w", "L0_ffn_base_b", "L0_ffn_lora_A",
          "L0_ffn_lora_B"]


def _tables(np):
    inv = (1.0 / np.float32(500000.0) ** (np.arange(0, HD, 2, dtype=np.float32) / np.float32(HD))).astype(np.float32)
    angle = np.arange(T, dtype=np.float32)[:, None] * inv[None, :]
    cos, sin = np.cos(angle), np.sin(angle)
    iota = np.broadcast_to(np.arange(E, dtype=np.float32), (T, E))
    table = np.concatenate([cos, cos, sin, -sin, iota], axis=1).astype(np.float32)
    row = np.arange(T)
    mask = np.where(row[None, :] > row[:, None], np.float32(-1e30), np.float32(0.0)).astype(np.float32)
    return np.ascontiguousarray(table), np.ascontiguousarray(mask)


def kernel(**inputs):
    import numpy as np
    import concourse.bacc as bacc
    from concourse.bass_utils import run_bass_kernel_spmd

    nc = bacc.Bacc("TRN2", target_bir_lowering=False, num_devices=1)
    arrays, args = {}, []
    table, mask = _tables(np)
    for name, a in [(n, inputs[n]) for n in _NAMES] + [("table", table), ("mask", mask)]:
        a = np.ascontiguousarray(a)
        arrays[f"in_{name}"] = a
        args.append(nc.dram_tensor(f"in_{name}", a.shape, F32, kind="ExternalInput").ap())
    o = nc.dram_tensor("out_0", (B, T, D), F32, kind="ExternalOutput").ap()
    post_ln_decoder(nc, *args, o, UPTO=3, LOOPS=True)
    r = run_bass_kernel_spmd(nc, [arrays], core_ids=[0])
    return r.results[0]["out_0"]
```

```python
from contextlib import ExitStack

import concourse.bass as bass
from concourse import mybir

F32 = mybir.dt.float32
F32R = mybir.dt.float32r
BF16 = mybir.dt.bfloat16
I32 = mybir.dt.int32
U32 = mybir.dt.uint32
ALU = mybir.AluOpType
ACT = mybir.ActivationFunctionType
AX_X = mybir.AxisListType.X

P = 128
B, T, D = 8, 128, 512
C = D // P
H, KV, HD = 32, 8, 16
GS = H // KV
HALF = HD // 2
KD = KV * HD
UN = 4
UH = H // UN
VW = HD + 2
XH, XG, XD = 32, 4, 128
XHG = XH // XG
PAIRS = XHG // 2
XSCALE = float(XD) ** -0.5
KEYS = 2 * T
E, R, TOPK = 8, 16, 2
ER = E * R
SCALING = 2.0
EPS = 1e-5
GUESS = float(0x5F3759DF - (3 << 23) + (1 << 23) - (1 << 31))

C_COS, C_SIN, C_NSIN, C_IOTA = 0, HD, HD + HALF, HD + 2 * HALF
C_N = C_IOTA + E


def post_ln_decoder(nc, x, context, sa_wq, sa_wk, sa_wv, sa_wo, xa_wq, xa_wk, xa_wv, xa_wo,
                    gate_w, base_w, base_b, lora_a, lora_b, table, mask, out):
    with ExitStack() as ctx:
        def sbuf(name, shape, dt=F32, scope=ctx):
            return scope.enter_context(nc.sbuf_tensor(name, shape, dt))

        def sem(name):
            return ctx.enter_context(nc.semaphore(name))

        bank = [ctx.enter_context(nc.psum_tensor(f"bank{i}", [P, 512], F32)) for i in range(6)]
        score_banks = ctx.enter_context(nc.psum_tensor("score_banks", [P, 2, 512], F32))

        y = sbuf("y", [P, B, D])
        x1h = sbuf("x1h", [P, C, B * T], F32R)
        x1l = sbuf("x1l", [P, C, B * T], F32R)
        ident = sbuf("ident", [P, P])
        identb = sbuf("identb", [P, P], BF16)
        consts = sbuf("consts", [P, C_N])
        one = sbuf("one", [P, 1])
        maskb = sbuf("maskb", [P, P], BF16)
        maskf = sbuf("maskf", [P, P])
        stats = sbuf("stats", [P, B, 6])
        meanvar = sbuf("meanvar", [P, B, 2])
        newton = sbuf("newton", [P, 5, B])

        xwq_raw = sbuf("xwq_raw", [P, C, 2 * XD])
        xwo_raw = sbuf("xwo_raw", [P, 2, D])
        xwkv_raw = sbuf("xwkv_raw", [P, C, 2 * XD])
        xwkvh = sbuf("xwkvh", [P, C, 2 * XD], F32R)
        xwkvl = sbuf("xwkvl", [P, C, 2 * XD], F32R)
        cx_raw = sbuf("cx_raw", [P, 2, D])
        vfm = sbuf("vfm", [P, 2, 4 * T])

        pa = ExitStack()
        wqh = sbuf("wqh", [P, C, D], F32R, pa)
        wql = sbuf("wql", [P, C, D], F32R, pa)
        wkvh = sbuf("wkvh", [P, C, 2 * KD], F32R, pa)
        wkvl = sbuf("wkvl", [P, C, 2 * KD], F32R, pa)
        wraw = sbuf("wraw", [P, C * (2 * D + 2 * KD)], F32, pa)
        wq_raw = wraw[:, 0:C * D].rearrange("p (c n) -> p c n", c=C)
        wkv_raw = wraw[:, C * D:C * (D + 2 * KD)].rearrange("p (c n) -> p c n", c=C)
        wo_raw = wraw[:, C * (D + 2 * KD):].rearrange("p (c n) -> p c n", c=C)
        xin = sbuf("xin", [P, D], F32, pa)
        xth = sbuf("xth", [P, C, T], F32R, pa)
        xtl = sbuf("xtl", [P, C, T], F32R, pa)
        rot1 = sbuf("rot1", [P, H + KV, HD], F32, pa)
        rot2 = sbuf("rot2", [P, H + KV, HD], F32, pa)
        roped = sbuf("roped", [P, H + KV, HD], F32, pa)
        qs = sbuf("qs", [P, H, 2, 2, HD], F32R, pa)
        ks = sbuf("ks", [P, KV, 4, 2, HD], F32R, pa)
        vnext = sbuf("vnext", [P, KV, HD], F32, pa)
        qt = sbuf("qt", [P, H // 2, T], F32R, pa)
        kt = sbuf("kt", [P, KV, T], F32R, pa)
        woh = sbuf("woh", [P, C, D], F32R, pa)
        wol = sbuf("wol", [P, C, D], F32R, pa)
        vaug = sbuf("vaug", [P, KV, VW], F32, pa)
        probs = sbuf("probs", [P, 2, UH, T], F32, pa)
        pt = sbuf("pt", [P, UH, T], F32, pa)
        nmax = sbuf("nmax", [P, 2, 2, UH], F32, pa)
        rsum = sbuf("rsum", [P, UH], F32, pa)
        attn = sbuf("attn", [P, 2, D], F32, pa)
        ath = sbuf("ath", [P, C, T], F32R, pa)
        atl = sbuf("atl", [P, C, T], F32R, pa)
        xpre = sbuf("xpre", [P, D], F32, pa)
        xnorm = sbuf("xnorm", [P, D], F32, pa)
        pa.close()

        pb = ExitStack()
        cxh = sbuf("cxh", [P, C, B * T], F32R, pb)
        cxl = sbuf("cxl", [P, C, B * T], F32R, pb)
        kh = sbuf("kh", [P, B, KEYS], F32R, pb)
        kl = sbuf("kl", [P, B, KEYS], F32R, pb)
        vh = sbuf("vh", [P, B, 2, XD], F32R, pb)
        vl = sbuf("vl", [P, B, 2, XD], F32R, pb)
        xwq = sbuf("xwq", [P, 2, 2, C, 2 * XD], F32R, pb)
        xwqh, xwql = xwq[:, :, 0], xwq[:, :, 1]
        xwoh = sbuf("xwoh", [P, 2, 2, D], F32R, pb)
        xwol = sbuf("xwol", [P, 2, 2, D], F32R, pb)
        xqh = sbuf("xqh", [P, 2, 2, 4 * T], F32R, pb)
        xql = sbuf("xql", [P, 2, 2, 4 * T], F32R, pb)
        xp = sbuf("xp", [P, 2, 2, KEYS], F32, pb)
        xpth = sbuf("xpth", [P, 2, 2 * T], F32R, pb)
        xptl = sbuf("xptl", [P, 2, 2 * T], F32R, pb)
        xoh = sbuf("xoh", [P, 2 * T], F32R, pb)
        xol = sbuf("xol", [P, 2 * T], F32R, pb)
        xmax = sbuf("xmax", [P, 2, 2, 2], F32, pb)
        xsum = sbuf("xsum", [P, 2, 2, 2], F32, pb)
        pb.close()

        pc = ExitStack()
        gate_raw = sbuf("gate_raw", [E, D], F32, pc)
        bias = sbuf("bias", [P, D], F32, pc)
        bwh = sbuf("bwh", [P, C, D], F32R, pc)
        bwl = sbuf("bwl", [P, C, D], F32R, pc)
        agh = sbuf("agh", [P, C, ER + E], F32R, pc)
        agl = sbuf("agl", [P, C, ER + E], F32R, pc)
        lbh = sbuf("lbh", [P, D], F32R, pc)
        lbl = sbuf("lbl", [P, D], F32R, pc)
        lwh = sbuf("lwh", [P, 2, P], F32R, pc)
        lwl = sbuf("lwl", [P, 2, P], F32R, pc)
        lowg = sbuf("lowg", [P, B, ER + E], F32, pc)
        wlow = sbuf("wlow", [P, B, ER], F32, pc)
        top = sbuf("top", [P, B, 8], F32, pc)
        topi = sbuf("topi", [P, B, 8], U32, pc)
        topf = sbuf("topf", [P, B, TOPK], F32, pc)
        share = sbuf("share", [P, 4, B], F32, pc)
        gates = sbuf("gates", [P, TOPK, B, E], F32, pc)
        pc.close()
        base_raw = (xwq_raw[:].rearrange("p c n -> p (c n)"), xwo_raw[:].rearrange("p c n -> p (c n)"))
        lora_raw = xwkv_raw[:].rearrange("p c n -> p (c n)")
        la_raw, lb_raw = lora_raw[:, 0:D], lora_raw[:, D:2 * D]

        consts_in = sem("consts_in")
        ident_made = sem("ident_made")
        wq_in, wkv_in, wo_in = sem("wq_in"), sem("wkv_in"), sem("wo_in")
        w_hi, w_lo, wq_hi, wq_split = sem("w_hi"), sem("w_lo"), sem("wq_hi"), sem("wq_split")
        x_in, xres_in = sem("x_in"), sem("xres_in")
        xt_ready, xt_hi, xt_split = sem("xt_ready"), sem("xt_hi"), sem("xt_split")
        q_ready, kv_ready = sem("q_ready"), sem("kv_ready")
        roped_q, roped_k, q_hi, k_hi, q_lo, k_lo = (sem(n) for n in ("roped_q", "roped_k", "q_hi", "k_hi", "q_lo", "k_lo"))
        v_copied, v_set = sem("v_copied"), sem("v_set")
        stack_ready, stack_act, stack_dve = sem("stack_ready"), sem("stack_act"), sem("stack_dve")
        scores_ready, max_ready, exp_done = sem("scores_ready"), sem("max_ready"), sem("exp_done")
        pt_ready, pt_copied = sem("pt_ready"), sem("pt_copied")
        pv_ready, attn_set = sem("pv_ready"), sem("attn_set")
        at_ready, at_hi, at_split = sem("at_ready"), sem("at_hi"), sem("at_split")
        proj_ready, y_added, normed, y_set = sem("proj_ready"), sem("y_added"), sem("normed"), sem("y_set")
        x1_ready, x1_hi, x1_split = sem("x1_ready"), sem("x1_hi"), sem("x1_split")
        dve_chain = sem("dve_chain")
        xwq_in, xwo_in, xwkv_in = sem("xwq_in"), sem("xwo_in"), sem("xwkv_in")
        xw_hi, xwq_split, xwo_split, xwkv_split = sem("xw_hi"), sem("xwq_split"), sem("xwo_split"), sem("xwkv_split")
        cx_in = (sem("cx_in0"), sem("cx_in1"))
        cx_ready, cx_hi, cx_split = sem("cx_ready"), sem("cx_hi"), sem("cx_split")
        k_done, v_done, xk_hi, xk_split = sem("k_done"), sem("v_done"), sem("xk_hi"), sem("xk_split")
        vfm_copied, vt_ready, xv_hi, xv_split = sem("vfm_copied"), sem("vt_ready"), sem("xv_hi"), sem("xv_split")
        xq_done, xq_hi, xq_split = sem("xq_done"), sem("xq_hi"), sem("xq_split")
        xs_done, xmax_ready, xexp_done, xp_normed = sem("xs_done"), sem("xmax_ready"), sem("xexp_done"), sem("xp_normed")
        xpt_ready, xpt_hi, xpt_split = sem("xpt_ready"), sem("xpt_hi"), sem("xpt_split")
        xo_ready, xo_hi, xo_split = sem("xo_ready"), sem("xo_hi"), sem("xo_split")
        xy_ready, xy_added = sem("xy_ready"), sem("xy_added")
        base_in, lora_in, gate_in, bias_in = sem("base_in"), sem("lora_in"), sem("gate_in"), sem("bias_in")
        fw_ready, fw_kept, fw_hi, fw_split = sem("fw_ready"), sem("fw_kept"), sem("fw_hi"), sem("fw_split")
        x2_normed, x2_ready, x2_hi, x2_split, x2_kept = (sem(n) for n in ("x2_normed", "x2_ready", "x2_hi", "x2_split", "x2_kept"))
        ag_ready, ag_copied = sem("ag_ready"), sem("ag_copied")
        top_ready, top_exp, wlow_set = sem("top_ready"), sem("top_exp"), sem("wlow_set")
        lw_ready, lw_hi, lw_split = sem("lw_ready"), sem("lw_hi"), sem("lw_split")
        ff_ready, ff_added, out_set = sem("ff_ready"), sem("ff_added"), sem("out_set")
        stored = sem("stored")
        block = ctx.enter_context(nc.Block())

        TM, QB, KVB, CT, TP = bank[0], bank[1], bank[2], bank[3], (bank[4], bank[5])
        SC = score_banks
        XQ, XT, XO, XY = (bank[1], bank[2]), bank[0], bank[3], (bank[4], bank[5])

        FX, FG, FY = (XQ[1], XQ[0]), (XT, XO), (SC[:, 0, :], SC[:, 1, :], bank[4][:], bank[5][:])

        NU = PAIRS * B
        NQ = 4 * PAIRS
        NKV = 4
        AHEAD = 5
        NF = C + 3
        HB = B // 2
        LATE = 2 * NQ - AHEAD
        KV_STEPS = {LATE: (("k", 0),), LATE + 1: (("v", 0),), LATE + 2: (("k", 1), ("t", 0)), LATE + 3: (("v", 1),),
                    LATE + 4: (("t", 1), ("k", 2))}
        KV_BANK = {("k", 0): XQ[0], ("k", 1): XQ[0], ("k", 2): XQ[0], ("k", 3): XQ[0],
                   ("v", 0): XQ[1], ("v", 1): XQ[0], ("v", 2): XQ[1], ("v", 3): XQ[1],
                   ("t", 0): XQ[1], ("t", 1): XQ[1], ("t", 2): XT, ("t", 3): XO}
        FW_STEPS = {LATE: (0,), LATE + 1: (1,), LATE + 2: (2, 3), LATE + 3: (4, 5), LATE + 4: (6,)}

        def first(g):
            return isinstance(g, int) and g == 0

        def block_of(blk):
            return blk % 2, blk // 2
        STACK = (QB, KVB, TM)

        def loop(eng, first, end, body):
            with eng.Fori(first, end) as i:
                body(i)

        def chunked(ap):
            return ap[:, :].rearrange("p (c n) -> p c n", c=C)

        def tile(ap, b):
            return ap[b:b + 1, :, :].rearrange("o t n -> (o t) n")

        @block.sync
        def _(sp):
            sp.dma_start(xin[:], tile(x, 0)).then_inc(x_in, 16)
            sp.dma_start(wq_raw, sa_wq.rearrange("(c p) n -> p c n", p=P)).then_inc(wq_in, 16)
            sp.dma_start(consts[:], table).then_inc(consts_in, 16)
            sp.dma_start(maskf[:], mask).then_inc(consts_in, 16)
            sp.dma_start(wkv_raw[:, :, 0:KD], sa_wk.rearrange("(c p) n -> p c n", p=P)).then_inc(wkv_in, 16)
            sp.dma_start(wkv_raw[:, :, KD:], sa_wv.rearrange("(c p) n -> p c n", p=P)).then_inc(wkv_in, 16)
            sp.dma_start(wo_raw, sa_wo.rearrange("(c p) n -> p c n", p=P)).then_inc(wo_in, 16)
            sp.dma_start(y[:], x.rearrange("b t n -> t b n")).then_inc(xres_in, 16)
            for b in range(1, B):
                sp.wait_ge(xt_ready, b)
                sp.dma_start(xin[:], tile(x, b)).then_inc(x_in, 16)

            def load_pair(pair):
                sp.dma_start(xwq_raw[:], xa_wq.rearrange("(c p) n -> p c n", p=P)[:, :, bass.ds(pair * 2 * XD, 2 * XD)])\
                  .then_inc(xwq_in, 16)
                sp.dma_start(xwo_raw[:], xa_wo.rearrange("(h d) n -> d h n", d=XD)[:, bass.ds(pair * 2, 2), :])\
                  .then_inc(xwo_in, 16)

            def load_kv(g):
                for j, w in enumerate((xa_wk, xa_wv)):
                    sp.dma_start(xwkv_raw[:, :, j * XD:(j + 1) * XD],
                                 w.rearrange("(c p) n -> p c n", p=P)[:, :, bass.ds(g * XD, XD)]).then_inc(xwkv_in, 16)

            load_kv(0)
            load_pair(0)
            for b in range(B):
                if b >= 2:
                    sp.wait_ge(cx_ready, b - 1)
                sp.dma_start(cx_raw[:, b % 2, :], tile(context, b)).then_inc(cx_in[b % 2], 16)

            def pair_loads(g, pairs):
                for p in pairs:
                    sp.wait_ge(xwo_split, g * PAIRS + p)
                    load_pair(g * PAIRS + p)

            def sp_group(g):
                sp.wait_ge(xwkv_split, g + 1)
                load_kv(g + 1)
                pair_loads(g, range(1, PAIRS + 1))

            loop(sp, 0, XG - 1, sp_group)
            sp.wait_ge(xwkv_split, XG)
            sp.dma_start(la_raw, lora_a.rearrange("e r n -> (e r) n")).then_inc(lora_in, 16)
            for c in range(C):
                sp.dma_start(lb_raw[:, c * ER:(c + 1) * ER].rearrange("p (e r) -> p e r", e=E),
                             lora_b[:, c * P:(c + 1) * P, :].rearrange("e p r -> p e r")).then_inc(lora_in, 16)
            sp.wait_ge(v_done, XG * NKV)
            sp.dma_start(gate_raw[:], gate_w).then_inc(gate_in, 16)
            sp.dma_start(bias[:], base_b.rearrange("(o n) -> o n", o=1).to_broadcast([P, D])).then_inc(bias_in, 16)
            pair_loads(XG - 1, range(1, PAIRS))
            sp.wait_ge(xwo_split, XG * PAIRS)
            for i, raw in enumerate(base_raw):
                sp.dma_start(raw.rearrange("p (c n) -> p c n", c=2),
                             base_w[2 * i * P:2 * (i + 1) * P, :].rearrange("(c p) n -> p c n", p=P)).then_inc(base_in, 16)
            for b in range(B):
                sp.wait_ge(out_set, b + 1)
                sp.dma_start(tile(out, b), y[:, b, :]).then_inc(stored, 16)
            sp.wait_ge(stored, 16 * B)

        @block.gpsimd
        def _(pool):
            pool.memset(ident[:], 0.0).then_inc(ident_made, 1)
            pool.memset(vaug[:], 0.0).then_inc(ident_made, 1)
            pool.memset(one[:], 1.0).then_inc(ident_made, 1)
            pool.wait_ge(ident_made, 3)
            pool.affine_select(out=ident[:], in_=ident[:], compare_op=ALU.not_equal, fill=1.0, base=0,
                               pattern=[[-1, P]], channel_multiplier=1).then_inc(ident_made, 1)
            pool.memset(vaug[:, :, HD:HD + 1], 1.0).then_inc(ident_made, 1)
            pool.wait_ge(ident_made, 5)
            pool.tensor_copy(identb[:], ident[:]).then_inc(ident_made, 1)

            def low_parts(b):
                pool.wait_ge(q_hi, b + 1)
                pool.tensor_tensor(qs[:, :, 1, :, :], roped[:, 0:H, :].unsqueeze(2).to_broadcast([P, H, 2, HD]),
                                   qs[:, :, 0, :, :].bitcast(F32), ALU.subtract).then_inc(q_lo, 1)
                pool.wait_ge(k_hi, b + 1)
                pool.tensor_tensor(ks[:, :, :, 1, :], roped[:, H:, :].unsqueeze(2).to_broadcast([P, KV, 4, HD]),
                                   ks[:, :, :, 0, :].bitcast(F32), ALU.subtract).then_inc(k_lo, 1)

            def set_v(b):
                if b >= 1:
                    pool.wait_ge(pv_ready, UN * b)
                pool.wait_ge(v_copied, b + 1)
                pool.tensor_copy(vaug[:, :, 0:HD], vnext[:]).then_inc(v_set, 1)

            def keep_norm(b):
                pool.wait_ge(normed, b + 1)
                pool.tensor_copy(y[:, b, :], xnorm[:]).then_inc(y_set, 1)

            def split(raw, hi, lo, done):
                pool.tensor_tensor(hi, raw, one[:].unsqueeze(2).to_broadcast(raw.shape), ALU.mult).then_inc(xw_hi, 1)
                hi_count[0] += 1
                pool.wait_ge(xw_hi, hi_base[0] + hi_count[0])
                pool.tensor_tensor(lo, raw, hi.bitcast(F32), ALU.subtract).then_inc(done, 1)

            hi_base, hi_count = [0], [0]

            def split_kv(g):
                pool.wait_ge(xwkv_in, 32 * g + 32)
                split(xwkv_raw[:], xwkvh[:], xwkvl[:], xwkv_split)

            def split_pair(g, p, free=None, between=None):
                pair = g * PAIRS + p
                if free:
                    pool.wait_ge(xq_done, free[0] * NQ + 4 * (free[1] + 1))
                pool.wait_ge(xwq_in, 16 * pair + 16)
                split(xwq_raw[:], xwqh[:, p % 2], xwql[:, p % 2], xwq_split)
                if between:
                    between()
                    pool.wait_ge(x1_split, B)
                if free:
                    pool.wait_ge(xy_ready, free[0] * NU + B * (free[1] + 1))
                pool.wait_ge(xwo_in, 16 * pair + 16)
                split(xwo_raw[:], xwoh[:, p % 2], xwol[:, p % 2], xwo_split)

            def pool_group(g):
                hi_base[0], hi_count[0] = 5 + g * 9, 0
                pool.wait_ge(v_done, g * NKV + NKV)
                split_kv(g + 1)
                for p in (2, 3):
                    split_pair(g, p, (g, p - 2))
                for p in (0, 1):
                    split_pair(g + 1, p, (g, p + 2))

            set_v(0)
            for b in range(B):
                if b + 1 < B:
                    low_parts(b + 1)
                    set_v(b + 1)
                if b == B - 1:
                    split_kv(0)
                if b >= 1:
                    keep_norm(b - 1)
            pool.wait_ge(scores_ready, UN * B)
            split_pair(0, 0, between=lambda: keep_norm(B - 1))
            split_pair(0, 1)
            loop(pool, 0, XG - 1, pool_group)
            hi_base[0], hi_count[0] = 5 + (XG - 1) * 9, 0
            for p in (2, 3):
                split_pair(XG - 1, p, (XG - 1, p - 2))

            for i in range(NF):
                whole = vfm[:, i % 2, :]
                pool.wait_ge(fw_hi, i + 1)
                pool.wait_ge(fw_kept, i + 1)
                if i < C:
                    o, w, hi = bwl[:, i, :], whole, bwh[:, i, :]
                elif i == C:
                    o, w, hi = lbl[:], whole, lbh[:]
                elif i == C + 1:
                    o, w, hi = agl[:, :, 0:ER], whole.rearrange("p (c n) -> p c n", c=C), agh[:, :, 0:ER]
                else:
                    o, w, hi = agl[:, :, ER:], whole[:, 0:C * E].rearrange("p (c e) -> p c e", c=C), agh[:, :, ER:]
                pool.tensor_tensor(o, w, hi.bitcast(F32), ALU.subtract).then_inc(fw_split, 1)

            pool.wait_ge(bias_in, 16)
            for b in range(B):
                pool.wait_ge(x2_ready, b + 1)
                pool.tensor_tensor(y[:, b, :], y[:, b, :], bias[:], ALU.add).then_inc(x2_kept, 1)

        @block.tensor
        def _(pe):
            def three_passes(o, pairs, n):
                last = None
                for i, ((lh, ll), (rh, rl)) in enumerate(pairs):
                    pe.matmul(o, ll, rh, start=(i == 0), stop=False)
                    pe.matmul(o, lh, rl, start=False, stop=False)
                    last = pe.matmul(o, lh, rh, start=False, stop=(i == n - 1))
                return last

            def transpose4(dst, srcs):
                for j, s in enumerate(srcs):
                    last = pe.transpose(dst[:, j * P:(j + 1) * P], s, ident[:])
                return last

            def x_transpose(b):
                pe.wait_ge(x_in, 16 * (b + 1))
                if b >= 1:
                    pe.wait_ge(stack_act, 3 * b - 2)
                transpose4(QB, [xin[:, c * P:(c + 1) * P] for c in range(C)]).then_inc(xt_ready, 1)

            def project_q(b):
                pe.wait_ge(xt_split, b + 1)
                for c in range(C):
                    if b == 0:
                        pe.wait_ge(wq_split, c + 1)
                    pe.matmul(QB[:], xtl[:, c, :], wqh[:, c, :], start=(c == 0), stop=False)
                    pe.matmul(QB[:], xth[:, c, :], wql[:, c, :], start=False, stop=False)
                    last = pe.matmul(QB[:], xth[:, c, :], wqh[:, c, :], start=False, stop=(c == C - 1))
                last.then_inc(q_ready, 1)

            def project_kv(b):
                if b >= 1:
                    pe.wait_ge(stack_act, 3 * b - 1)
                three_passes(KVB[:, 0:2 * KD],
                             [((xth[:, c, :], xtl[:, c, :]), (wkvh[:, c, :], wkvl[:, c, :])) for c in range(C)],
                             C).then_inc(kv_ready, 1)

            def stack_transpose(b, groups):
                qf = qs[:].bitcast(F32).rearrange("p (j h) a e d -> p j (h a e d)", h=2)
                kf = ks[:].bitcast(F32).rearrange("p g a e d -> p g (a e d)")
                blocks = [qf[:, j, :] for j in range(H // 2)] + [kf[:, g, :] for g in range(KV)]
                for g in groups:
                    if g == 0:
                        pe.wait_ge(q_lo, b + 1)
                    if g == 1:
                        pe.wait_ge(roped_k, b + 1)
                    if g == 2 and b == 1:
                        pe.wait_ge(stack_act, 3)
                    if g == 2 and b >= 2:
                        pe.wait_ge(y_added, b - 1)
                    if g == 4:
                        pe.wait_ge(k_lo, b + 1)
                    if g >= 3:
                        pe.wait_ge(stack_dve, 3 * b + g - 2)
                    transpose4(STACK[g % 3], blocks[4 * g:4 * g + 4]).then_inc(stack_ready, 1)

            def scores(n):
                b, k = n // UN, n % UN
                if k == 0:
                    pe.wait_ge(stack_act, 3 * b + 2)
                    pe.wait_ge(stack_dve, 3 * b + 3)
                if k == 2:
                    pe.wait_ge(stack_act, 3 * b + 3)
                if n >= 1:
                    pe.wait_ge(exp_done, n)
                for odd in range(2):
                    pe.matmul(SC[:, odd, :], identb[:], maskb[:].unsqueeze(1).to_broadcast([P, 4, T]),
                              start=True, stop=False, skip_group_check=True)
                for i in range(UH // 2):
                    for odd in range(2):
                        h = UH * k + 2 * i + odd
                        rows = slice(64 * odd, 64 * odd + 64)
                        last = pe.matmul(SC[:, odd, i * T:(i + 1) * T], qt[rows, h // 2, :], kt[rows, h // GS, :],
                                         start=False, stop=True, skip_group_check=True)
                last.then_inc(scores_ready, 1)

            def probs_transpose(n):
                pe.wait_ge(exp_done, n + 1)
                for g in range(2):
                    if n >= 1:
                        pe.wait_ge(pt_copied, 2 * n - 1 + g)
                    transpose4(TP[g], [probs[:, n % 2, 4 * g + j, :] for j in range(4)]).then_inc(pt_ready, 1)

            def weigh_values(n):
                b, k = n // UN, n % UN
                pe.wait_ge(pt_copied, 2 * n + 2)
                if k == 0:
                    pe.wait_ge(v_set, b + 1)
                if n >= 1:
                    pe.wait_ge(attn_set, n)
                for s in range(UH):
                    h = UH * k + 2 * (s % 4) + s // 4
                    last = pe.matmul(CT[:, s * VW:(s + 1) * VW], pt[:, s, :], vaug[:, h // GS, :],
                                     start=True, stop=True)
                last.then_inc(pv_ready, 1)

            def attn_transpose(b):
                pe.wait_ge(attn_set, UN * (b + 1))
                if b == 0:
                    pe.wait_ge(stack_act, 6)
                else:
                    pe.wait_ge(x1_split, b)
                transpose4(TM, [attn[:, b % 2, c * P:(c + 1) * P] for c in range(C)]).then_inc(at_ready, 1)

            def project_out(b):
                pe.wait_ge(at_split, b + 1)
                three_passes(TM[:], [((ath[:, c, :], atl[:, c, :]), (woh[:, c, :], wol[:, c, :])) for c in range(C)],
                             C).then_inc(proj_ready, 1)

            def norm_transpose(b):
                pe.wait_ge(normed, b + 1)
                if b + 2 < B:
                    pe.wait_ge(stack_act, 3 * b + 9)
                transpose4(TM, [xnorm[:, c * P:(c + 1) * P] for c in range(C)]).then_inc(x1_ready, 1)

            def cx_transpose(b):
                pe.wait_ge(cx_in[b % 2], 16 * (b // 2 + 1))
                if b < 2:
                    pe.wait_ge(stack_act, 3 * B - 2 + b)
                else:
                    pe.wait_ge(cx_split, b - 1)
                transpose4(XQ[b % 2], [cx_raw[:, b % 2, c * P:(c + 1) * P] for c in range(C)]).then_inc(cx_ready, 1)

            def passes(lh, ll, rh, rl):
                return [(ll, rh), (lh, rl), (lh, rh)]

            def run(o, ops, first=True, last=True):
                for i, (l, r) in enumerate(ops):
                    mm = pe.matmul(o, l, r, start=(first and i == 0), stop=(last and i == len(ops) - 1),
                                   skip_group_check=True)
                return mm

            def project_block(g, blk, j, bank_):
                src, half = block_of(blk)
                sh, sl = ((cxh, cxl), (x1h, x1l))[src]
                cols, toks = slice(j * XD, (j + 1) * XD), slice(half * 4 * T, (half + 1) * 4 * T)
                ops = []
                for c in range(C):
                    ops += passes(xwkvh[:, c, cols], xwkvl[:, c, cols], sh[:, c, toks], sl[:, c, toks])
                return run(bank_[:], ops)

            def kv_step(g, kind, blk):
                n, q = g * NKV, g * NQ
                if (kind, blk) == ("k", 0):
                    pe.wait_ge(xwkv_split, g + 1)
                if (kind, blk) in (("k", 0), ("v", 0)):
                    j = "kv".index(kind)
                    if first(g):
                        pe.wait_ge(cx_split, B - 1 + j)
                    else:
                        pe.wait_ge(xq_split, q - 1 + j)
                elif kind == "k":
                    pe.wait_ge(*{1: (xk_split, n + 1), 2: (vfm_copied, n + 2), 3: (xq_split, q + 1)}[blk])
                elif kind == "v":
                    pe.wait_ge(*{1: (xk_split, n + 2), 2: (xv_split, n + 2), 3: (xq_split, q + 2)}[blk])
                else:
                    pe.wait_ge(vfm_copied, n + blk + 1)
                    if blk % 2 == 1:
                        pe.wait_ge(xv_split, n + blk)
                    if blk == 2 and first(g):
                        pe.wait_ge(x1_split, B)
                if kind == "t":
                    transpose4(KV_BANK[kind, blk], [vfm[:, blk % 2, t * T:(t + 1) * T] for t in range(4)])\
                        .then_inc(vt_ready, 1)
                elif kind == "k":
                    project_block(g, blk, 0, KV_BANK[kind, blk]).then_inc(k_done, 1)
                else:
                    project_block(g, blk, 1, KV_BANK[kind, blk]).then_inc(v_done, 1)

            def project_queries(g, part):
                h, quarter = part // 4, part % 4
                j = quarter // 2
                toks = slice((h % 2) * 4 * T, (h % 2 + 1) * 4 * T)
                w = (h // 2) % 2
                if quarter == 0 and h % 2 == 0:
                    pe.wait_ge(xwq_split, g * PAIRS + h // 2 + 1)
                if quarter % 2 == 0:
                    if h >= 2:
                        pe.wait_ge(xq_split, g * NQ + 2 * (h - 1) + j + 1)
                    else:
                        pe.wait_ge((xk_split, vfm_copied)[j], g * NKV + 3 + h)
                ops = []
                for c in range(C):
                    cols = slice(j * XD, (j + 1) * XD)
                    ops += passes(xwqh[:, w, c, cols], xwql[:, w, c, cols], x1h[:, c, toks], x1l[:, c, toks])
                n = len(ops) // 2
                if quarter % 2 == 0:
                    run(XQ[j][:], ops[:n], last=False)
                else:
                    run(XQ[j][:], ops[n:], first=False).then_inc(xq_done, 1)

            def cross_scores(g, u):
                b, h = u % B, u // 4
                toks = slice((u % 4) * T, (u % 4 + 1) * T)
                if u % 4 == 0:
                    pe.wait_ge(xq_split, g * NQ + 2 * h + 2)
                if u in (0, 4):
                    pe.wait_ge(xk_split, g * NKV + (2 if u == 0 else NKV))
                if u >= 2:
                    pe.wait_ge(xexp_done, g * NU + u - 1)
                for j in range(2):
                    mm = run(SC[:, u % 2, j * KEYS:(j + 1) * KEYS],
                             passes(xqh[:, h % 2, j, toks], xql[:, h % 2, j, toks], kh[:, b, :], kl[:, b, :]))
                mm.then_inc(xs_done, 1)

            def cross_transpose(g, u):
                pe.wait_ge(xp_normed, g * NU + u + 1)
                if u >= 1:
                    pe.wait_ge(xpt_split, g * NU + u)
                else:
                    pe.wait_ge(xv_split, g * NKV + 3)
                transpose4(XT, [xp[:, u % 2, j, c * T:(c + 1) * T] for c in range(2) for j in range(2)])\
                    .then_inc(xpt_ready, 1)

            def cross_values(g, u):
                pe.wait_ge(xpt_split, g * NU + u + 1)
                if u >= 1:
                    pe.wait_ge(xo_split, g * NU + u)
                else:
                    pe.wait_ge(xv_split, g * NKV + NKV)
                ops = []
                for c in range(2):
                    ops += passes(vh[:, u % B, c, :], vl[:, u % B, c, :], xpth[:, c, :], xptl[:, c, :])
                run(XO[:, 0:2 * T], ops).then_inc(xo_ready, 1)

            def cross_out(g, u):
                w = (u // B) % 2
                pe.wait_ge(xo_split, g * NU + u + 1)
                if u % B == 0:
                    pe.wait_ge(xwo_split, g * PAIRS + u // B + 1)
                if u >= 2:
                    pe.wait_ge(xy_added, g * NU + u - 1)
                ops = []
                for j in range(2):
                    cols = slice(j * T, (j + 1) * T)
                    ops += passes(xoh[:, cols], xol[:, cols], xwoh[:, w, j, :], xwol[:, w, j, :])
                run(XY[u % 2][:], ops).then_inc(xy_ready, 1)

            def weights_transpose(i):
                if i < 2:
                    pe.wait_ge(xq_split, XG * NQ - 1 + i)
                else:
                    pe.wait_ge(fw_hi, i - 1)
                if i == 0:
                    pe.wait_ge(base_in, 32)
                if i == C:
                    pe.wait_ge(lora_in, 16 * (C + 1))
                if i < C:
                    srcs = [base_raw[oc // 2][:, (oc % 2) * D + i * P:(oc % 2) * D + (i + 1) * P] for oc in range(C)]
                elif i < C + 2:
                    srcs = [(lb_raw, la_raw)[i - C][:, c * P:(c + 1) * P] for c in range(C)]
                if i < C + 2:
                    transpose4(XQ[i % 2], srcs).then_inc(fw_ready, 1)
                    return
                pe.wait_ge(gate_in, 16)
                for c in range(C):
                    mm = pe.transpose(XQ[0][:, c * E:(c + 1) * E], gate_raw[:, c * P:(c + 1) * P], ident[0:E, 0:E])
                mm.then_inc(fw_ready, 1)

            def x2_transpose(b):
                pe.wait_ge(x2_normed, b + 1)
                if b >= 2:
                    pe.wait_ge(x2_split, b - 1)
                else:
                    pe.wait_ge(fw_hi, NF - 1 + b)
                transpose4(FX[b % 2], [y[:, b, c * P:(c + 1) * P] for c in range(C)]).then_inc(x2_ready, 1)

            def pe_units(g, last):
                for u in range(NU):
                    if u + 1 < NU:
                        cross_scores(g, u + 1)
                    cross_transpose(g, u)
                    if u < LATE:
                        project_queries(g, u + AHEAD)
                    elif last:
                        for i in FW_STEPS[u]:
                            weights_transpose(i)
                        if u == NU - 1:
                            x2_transpose(0)
                    else:
                        for kind, blk in KV_STEPS[u]:
                            kv_step(g + 1, kind, blk)
                    if u >= 1:
                        cross_out(g, u - 1)
                    cross_values(g, u)

            def rest_of_projections(g):
                project_queries(g, 0)
                project_queries(g, 1)
                kv_step(g, "t", 2)
                project_queries(g, 2)
                project_queries(g, 3)
                kv_step(g, "k", 3)
                cross_scores(g, 0)
                kv_step(g, "v", 3)
                project_queries(g, 4)
                kv_step(g, "t", 3)

            def pe_group(g):
                pe_units(g, last=False)
                kv_step(g + 1, "v", 2)
                cross_out(g, NU - 1)
                rest_of_projections(g + 1)
                pe.wait_ge(xy_added, g * NU + NU)

            pe.wait_ge(ident_made, 6)
            x_transpose(0)
            project_q(0)
            pe.wait_ge(w_lo, 1)
            project_kv(0)
            stack_transpose(0, range(5))
            x_transpose(1)
            stack_transpose(0, (5,))
            scores(0)
            project_q(1)
            for b in range(B):
                n = UN * b
                scores(n + 1)
                probs_transpose(n)
                if b + 1 < B:
                    if b >= 1:
                        project_q(b + 1)
                else:
                    cx_transpose(0)
                    cx_transpose(1)
                weigh_values(n)
                if b >= 2:
                    norm_transpose(b - 2)
                if b + 1 == B:
                    cx_transpose(2)

                scores(n + 2)
                probs_transpose(n + 1)
                if b >= 1:
                    attn_transpose(b - 1)
                if b + 1 < B:
                    project_kv(b + 1)
                else:
                    cx_transpose(3)
                if b == 1:
                    pe.wait_ge(w_lo, 2)
                if b >= 1:
                    project_out(b - 1)
                if b + 1 == B:
                    cx_transpose(4)
                    cx_transpose(5)
                weigh_values(n + 1)

                scores(n + 3)
                probs_transpose(n + 2)
                if b + 1 < B:
                    stack_transpose(b + 1, range(5))
                else:
                    cx_transpose(6)
                    cx_transpose(7)
                weigh_values(n + 2)

                if b + 1 < B:
                    scores(n + 4)
                probs_transpose(n + 3)
                if b + 1 < B:
                    stack_transpose(b + 1, (5,))
                if b + 2 < B:
                    x_transpose(b + 2)
                if b + 1 == B:
                    kv_step(0, "k", 0)
                weigh_values(n + 3)
            norm_transpose(B - 2)
            kv_step(0, "v", 0)
            attn_transpose(B - 1)
            kv_step(0, "k", 1)
            project_out(B - 1)
            kv_step(0, "t", 0)
            kv_step(0, "v", 1)
            kv_step(0, "t", 1)
            norm_transpose(B - 1)
            kv_step(0, "k", 2)
            kv_step(0, "v", 2)
            rest_of_projections(0)
            loop(pe, 0, XG - 1, pe_group)
            pe_units(XG - 1, last=True)

            def tile_passes(b, wh, wl):
                toks = slice(b * T, (b + 1) * T)
                ops = []
                for c in range(C):
                    ops += passes(x1h[:, c, toks], x1l[:, c, toks], wh[:, c, :], wl[:, c, :])
                return ops

            def low_and_gate(b):
                pe.wait_ge(x2_split, b + 1)
                if b == 0:
                    pe.wait_ge(fw_split, NF)
                if b >= 2:
                    pe.wait_ge(ag_copied, b - 1)
                run(FG[b % 2][:, 0:ER + E], tile_passes(b, agh, agl)).then_inc(ag_ready, 1)

            def base(b):
                if b >= 4:
                    pe.wait_ge(ff_added, b - 3)
                elif b >= 2:
                    pe.wait_ge(xy_added, XG * NU - 3 + b)
                run(FY[b % 4], tile_passes(b, bwh, bwl), last=False)

            def low_transpose(b):
                pe.wait_ge(wlow_set, b // HB + 1)
                if b >= 2:
                    pe.wait_ge(lw_split, b - 1)
                pe.transpose(FX[b % 2][:, 0:P], wlow[:, b, :], ident[:]).then_inc(lw_ready, 1)

            def lora(b):
                pe.wait_ge(lw_split, b + 1)
                run(FY[b % 4], passes(lwh[:, b % 2, :], lwl[:, b % 2, :], lbh[:], lbl[:]), first=False)\
                    .then_inc(ff_ready, 1)

            def rows_of(tiles):
                for b in tiles:
                    low_and_gate(b)
                    if b + 2 in tiles:
                        x2_transpose(b + 2)

            x2_transpose(1)
            cross_out(XG - 1, NU - 1)
            rows_of(range(HB))
            for b in range(HB - 1):
                base(b)
            x2_transpose(HB)
            x2_transpose(HB + 1)
            base(HB - 1)
            rows_of(range(HB, B))
            pe.wait_ge(x2_split, B)
            low_transpose(0)
            low_transpose(1)
            lora(0)
            low_transpose(2)
            lora(1)
            low_transpose(3)
            base(4)
            lora(2)
            base(5)
            lora(3)
            base(6)
            low_transpose(4)
            low_transpose(5)
            base(7)
            for b in range(HB, B):
                lora(b)
                if b + 2 < B:
                    low_transpose(b + 2)

        @block.scalar
        def _(act):
            def copy(o, i):
                return act.activation(o, i, ACT.Copy)

            def split_weights(n, raw, hi, loaded, count):
                act.wait_ge(loaded, count)
                copy(hi[:], raw).then_inc(w_hi, 1)

            def x_high(b):
                act.wait_ge(xt_ready, b + 1)
                copy(xth[:], chunked(QB)).then_inc(xt_hi, 1)

            def stack_high(b):
                act.wait_ge(roped_q, b + 1)
                copy(qs[:, :, 0, :, :], roped[:, 0:H, :].unsqueeze(2).to_broadcast([P, H, 2, HD])).then_inc(q_hi, 1)
                act.wait_ge(roped_k, b + 1)
                copy(ks[:, :, :, 0, :], roped[:, H:, :].unsqueeze(2).to_broadcast([P, KV, 4, HD])).then_inc(k_hi, 1)

            def copy_v(b):
                act.wait_ge(kv_ready, b + 1)
                if b >= 1:
                    act.wait_ge(v_set, b)
                copy(vnext[:], KVB[:, KD:2 * KD].rearrange("p (g d) -> p g d", g=KV)).then_inc(v_copied, 1)

            def stack_copy(b, groups):
                for g in groups:
                    dst = {3: qt[:, 12:16, :], 4: kt[:, 0:4, :], 5: kt[:, 4:8, :]}[g]
                    act.wait_ge(stack_ready, 6 * b + g + 1)
                    copy(dst, chunked(STACK[g % 3])).then_inc(stack_act, 1)

            def exponentials(n):
                act.wait_ge(max_ready, n + 1)
                if n >= 2:
                    act.wait_ge(pt_ready, 2 * (n - 1))
                for s in range(UH):
                    last = act.activation(probs[:, n % 2, s, :], SC[:, s // 4, (s % 4) * T:(s % 4 + 1) * T], ACT.Exp,
                                          bias=nmax[:, n % 2, 1, s:s + 1], scale=HD ** -0.5)
                last.then_inc(exp_done, 1)

            def pt_copy(n):
                for g in range(2):
                    act.wait_ge(pt_ready, 2 * n + g + 1)
                    copy(pt[:, 4 * g:4 * g + 4, :], chunked(TP[g])).then_inc(pt_copied, 1)

            def attn_high(b):
                act.wait_ge(at_ready, b + 1)
                copy(ath[:], chunked(TM)).then_inc(at_hi, 1)

            def norm_high(b):
                act.wait_ge(x1_ready, b + 1)
                copy(x1h[:, :, b * T:(b + 1) * T], chunked(TM)).then_inc(x1_hi, 1)

            def cx_high(b):
                act.wait_ge(cx_ready, b + 1)
                copy(cxh[:, :, b * T:(b + 1) * T], chunked(XQ[b % 2])).then_inc(cx_hi, 1)

            def keys_high(g, blk):
                src, half = block_of(blk)
                act.wait_ge(k_done, g * NKV + blk + 1)
                copy(kh[:, 4 * half:4 * half + 4, src * T:(src + 1) * T], chunked(KV_BANK["k", blk])).then_inc(xk_hi, 1)

            def values_copy(g, blk):
                act.wait_ge(v_done, g * NKV + blk + 1)
                if blk >= 2:
                    act.wait_ge(vt_ready, g * NKV + blk - 1)
                copy(vfm[:, blk % 2, :], KV_BANK["v", blk][:]).then_inc(vfm_copied, 1)

            def values_high(g, blk):
                src, half = block_of(blk)
                act.wait_ge(vt_ready, g * NKV + blk + 1)
                copy(vh[:, 4 * half:4 * half + 4, src, :], chunked(KV_BANK["t", blk])).then_inc(xv_hi, 1)

            def kv_step(g, kind, blk):
                {"k": keys_high, "v": values_copy, "t": values_high}[kind](g, blk)

            def queries_high(g, h, j):
                act.wait_ge(xq_done, g * NQ + 2 * h + j + 1)
                copy(xqh[:, h % 2, j, :], XQ[j][:]).then_inc(xq_hi, 1)

            def cross_exp(g, u):
                act.wait_ge(xmax_ready, g * NU + u + 1)
                if u >= 2:
                    act.wait_ge(xpt_ready, g * NU + u - 1)
                for j in range(2):
                    last = act.activation(xp[:, u % 2, j, :], SC[:, u % 2, j * KEYS:(j + 1) * KEYS], ACT.Exp,
                                          bias=xmax[:, u % 2, 1, j:j + 1], scale=XSCALE,
                                          accum_out=xsum[:, u % 2, 0, j:j + 1])
                last.then_inc(xexp_done, 1)

            def cross_pt_high(g, u):
                act.wait_ge(xpt_ready, g * NU + u + 1)
                copy(xpth[:], XT[:].rearrange("p (c n) -> p c n", c=2)).then_inc(xpt_hi, 1)

            def cross_o_high(g, u):
                act.wait_ge(xo_ready, g * NU + u + 1)
                copy(xoh[:], XO[:, 0:2 * T]).then_inc(xo_hi, 1)

            def weights_high(i):
                act.wait_ge(fw_ready, i + 1)
                if i >= 2:
                    act.wait_ge(fw_split, i - 1)
                wide = C * E if i == C + 2 else D
                copy(vfm[:, i % 2, 0:wide], XQ[i % 2][:, 0:wide]).then_inc(fw_kept, 1)
                if i < C:
                    copy(bwh[:, i, :], XQ[i % 2][:]).then_inc(fw_hi, 1)
                elif i == C:
                    copy(lbh[:], XQ[0][:]).then_inc(fw_hi, 1)
                elif i == C + 1:
                    copy(agh[:, :, 0:ER], chunked(XQ[1])).then_inc(fw_hi, 1)
                else:
                    copy(agh[:, :, ER:], XQ[0][:, 0:C * E].rearrange("p (c e) -> p c e", c=C)).then_inc(fw_hi, 1)

            def x2_high(b):
                act.wait_ge(x2_ready, b + 1)
                copy(x1h[:, :, b * T:(b + 1) * T], chunked(FX[b % 2])).then_inc(x2_hi, 1)

            def act_units(g, last):
                for u in range(NU):
                    cross_pt_high(g, u)
                    if u + 1 < NU:
                        cross_exp(g, u + 1)
                    if u >= LATE:
                        if last:
                            for i in FW_STEPS[u]:
                                weights_high(i)
                            if u == NU - 1:
                                x2_high(0)
                        else:
                            for kind, blk in KV_STEPS[u]:
                                kv_step(g + 1, kind, blk)
                    elif (u + AHEAD) % 2 == 1:
                        queries_high(g, (u + AHEAD) // 4, (u + AHEAD) % 4 // 2)
                    cross_o_high(g, u)

            def rest_of_projections(g):
                kv_step(g, "v", 2)
                queries_high(g, 0, 0)
                kv_step(g, "t", 2)
                queries_high(g, 0, 1)
                kv_step(g, "k", 3)
                cross_exp(g, 0)
                kv_step(g, "v", 3)
                kv_step(g, "t", 3)

            def act_group(g):
                act_units(g, last=False)
                rest_of_projections(g + 1)

            x_high(0)
            act.wait_ge(wq_in, 16)
            for c in range(C):
                copy(wqh[:, c, :], wq_raw[:, c, :]).then_inc(wq_hi, 1)
            split_weights(1, wkv_raw, wkvh, wkv_in, 32)
            act.wait_ge(consts_in, 32)
            copy(maskb[:], maskf[:]).then_inc(w_hi, 1)
            copy_v(0)
            stack_high(0)
            split_weights(2, wo_raw, woh, wo_in, 16)
            stack_copy(0, (3, 4))
            x_high(1)
            stack_copy(0, (5,))
            exponentials(0)
            for b in range(B):
                n = UN * b
                pt_copy(n)
                if b + 1 == B:
                    cx_high(0)
                exponentials(n + 1)
                if b + 1 == B:
                    cx_high(1)
                if b >= 2:
                    norm_high(b - 2)
                if b + 1 == B:
                    cx_high(2)

                pt_copy(n + 1)
                if b >= 1:
                    attn_high(b - 1)
                if b + 1 == B:
                    cx_high(3)
                exponentials(n + 2)
                if b + 1 < B:
                    copy_v(b + 1)
                    stack_high(b + 1)
                else:
                    cx_high(4)
                    cx_high(5)

                pt_copy(n + 2)
                exponentials(n + 3)
                if b + 1 < B:
                    stack_copy(b + 1, (3, 4))
                else:
                    cx_high(6)
                    cx_high(7)

                pt_copy(n + 3)
                if b + 1 < B:
                    exponentials(n + 4)
                    stack_copy(b + 1, (5,))
                if b + 2 < B:
                    x_high(b + 2)
            kv_step(0, "k", 0)
            norm_high(B - 2)
            kv_step(0, "v", 0)
            attn_high(B - 1)
            kv_step(0, "k", 1)
            kv_step(0, "t", 0)
            kv_step(0, "v", 1)
            kv_step(0, "t", 1)
            norm_high(B - 1)
            kv_step(0, "k", 2)
            rest_of_projections(0)
            loop(act, 0, XG - 1, act_group)
            act_units(XG - 1, last=True)

            def gates_of(half):
                act.wait_ge(top_ready, half + 1)
                s = slice(half * HB, (half + 1) * HB)
                act.activation(share[:, 1, s], share[:, 0, s], ACT.Exp).then_inc(top_exp, 1)

            for half in range(2):
                tiles = range(half * HB, (half + 1) * HB)
                if half == 1:
                    x2_high(tiles[0])
                x2_high(tiles[1])
                for b in tiles:
                    act.wait_ge(ag_ready, b + 1)
                    copy(lowg[:, b, :], FG[b % 2][:, 0:ER + E]).then_inc(ag_copied, 1)
                    if b + 2 in tiles:
                        x2_high(b + 2)
                if half == 0:
                    gates_of(half)
            for b in range(B):
                if b == HB:
                    gates_of(1)
                act.wait_ge(lw_ready, b + 1)
                if b >= 2:
                    act.wait_ge(ff_ready, b - 1)
                copy(lwh[:, b % 2, :], FX[b % 2][:, 0:P]).then_inc(lw_hi, 1)

        @block.vector
        def _(dve):
            chain, links = [0], [0]

            def link(ins):
                chain[0] += 1
                ins.then_inc(dve_chain, 1)
                dve.wait_ge(dve_chain, links[0] + chain[0])

            def low(o, whole, high):
                return dve.tensor_tensor(o, whole, high.bitcast(F32), ALU.subtract)

            def x_low(b):
                dve.wait_ge(xt_hi, b + 1)
                low(xtl[:], chunked(QB), xth[:]).then_inc(xt_split, 1)

            def rope(b, src, lo, hi, ready, done, others):
                heads = hi - lo
                v = src.rearrange("p (h d) -> p h d", h=heads)
                cos = consts[:, C_COS:C_COS + HD].unsqueeze(1).to_broadcast([P, heads, HD])
                nsin = consts[:, C_NSIN:C_NSIN + HALF].unsqueeze(1).to_broadcast([P, heads, HALF])
                sin = consts[:, C_SIN:C_SIN + HALF].unsqueeze(1).to_broadcast([P, heads, HALF])
                dve.wait_ge(ready, b + 1)
                for s in others:
                    if b >= 1:
                        dve.wait_ge(s, b)
                dve.tensor_tensor(rot1[:, lo:hi, :], v, cos, ALU.mult)
                dve.tensor_tensor(rot2[:, lo:hi, 0:HALF], v[:, :, HALF:], nsin, ALU.mult)
                link(dve.tensor_tensor(rot2[:, lo:hi, HALF:], v[:, :, 0:HALF], sin, ALU.mult))
                dve.tensor_tensor(roped[:, lo:hi, :], rot1[:, lo:hi, :], rot2[:, lo:hi, :], ALU.add).then_inc(done, 1)

            def rope_q(b):
                rope(b, QB[:], 0, H, q_ready, roped_q, (q_lo,))

            def rope_k(b):
                dve.wait_ge(v_copied, b + 1)
                rope(b, KVB[:, 0:KD], H, H + KV, kv_ready, roped_k, (k_lo,))

            def stack_copy(b):
                for g in range(3):
                    dve.wait_ge(stack_ready, 6 * b + g + 1)
                    dve.tensor_copy(qt[:, 4 * g:4 * g + 4, :], chunked(STACK[g])).then_inc(stack_dve, 1)

            def maxima(n):
                dve.wait_ge(scores_ready, n + 1)
                if n >= 2:
                    dve.wait_ge(exp_done, n - 1)
                link(dve.tensor_reduce(nmax[:, n % 2, 0, :].rearrange("p (o i) -> p o i", o=2),
                                       SC[:].rearrange("p o (i t) -> p o i t", i=4), AX_X, ALU.max))
                dve.tensor_scalar(nmax[:, n % 2, 1, :], nmax[:, n % 2, 0, :], -HD ** -0.5, None,
                                  ALU.mult).then_inc(max_ready, 1)

            def set_attn(n):
                k = n % UN
                dve.wait_ge(pv_ready, n + 1)
                pv = CT[:, 0:UH * VW].rearrange("p (s v) -> p s v", s=UH)
                link(dve.reciprocal(rsum[:], pv[:, :, HD]))
                for odd in range(2):
                    o = attn[:, n // UN % 2, k * UH * HD:(k + 1) * UH * HD].rearrange("p (i o d) -> p o i d", o=2, d=HD)[:, odd]
                    last = dve.tensor_tensor(o, pv[:, 4 * odd:4 * odd + 4, 0:HD],
                                             rsum[:, 4 * odd:4 * odd + 4].unsqueeze(2).to_broadcast([P, 4, HD]), ALU.mult)
                last.then_inc(attn_set, 1)

            def attn_low(b):
                dve.wait_ge(at_hi, b + 1)
                low(atl[:], chunked(TM), ath[:]).then_inc(at_split, 1)

            def add_residual(b):
                dve.wait_ge(proj_ready, b + 1)
                dve.tensor_tensor(xpre[:], TM[:], y[:, b, :], ALU.add).then_inc(y_added, 1)

            def rsqrt_guess(n, var):
                a, r = newton[:, 3, 0:n], newton[:, 4, 0:n]
                for i, s in enumerate((4.0, 16.0, 64.0)):
                    last = dve.tensor_scalar(newton[:, i, 0:n], var, EPS, s, ALU.add, ALU.mult)
                link(last)
                link(dve.tensor_scalar(a.bitcast(I32), newton[:, 0, 0:n].bitcast(I32), 1, None, ALU.logical_shift_right))
                link(dve.tensor_scalar(r.bitcast(I32), a.bitcast(I32), -1.0, GUESS, ALU.mult, ALU.add))

            def rsqrt_steps(n, steps):
                a, r = newton[:, 3, 0:n], newton[:, 4, 0:n]
                for i in steps:
                    if n == 1:
                        link(dve.scalar_tensor_tensor(a, r, newton[:, i, 0:1], r, ALU.mult, ALU.mult))
                    else:
                        link(dve.tensor_tensor(a, r, r, ALU.mult))
                        link(dve.tensor_tensor(a, a, newton[:, i, 0:n], ALU.mult))
                    link(dve.scalar_tensor_tensor(r, a, -3.0, r, ALU.add, ALU.mult))
                return r

            def rsqrt(n, var):
                rsqrt_guess(n, var)
                return rsqrt_steps(n, (2, 1, 0))

            def tile_moments(b):
                dve.wait_ge(y_added, b + 1)
                link(dve.bn_stats(stats[:, 0, :], xpre[:]))
                link(dve.bn_aggr(meanvar[:, 0, :], stats[:, 0, :]))

            def layer_norm(b):
                r = rsqrt(1, meanvar[:, 0, 1:2])
                if b >= 1:
                    dve.wait_ge(x1_ready, b)
                    dve.wait_ge(y_set, b)
                dve.tensor_scalar(xnorm[:], xpre[:], meanvar[:, 0, 0:1], r, ALU.subtract, ALU.mult).then_inc(normed, 1)

            def norm_low(b):
                dve.wait_ge(x1_hi, b + 1)
                s = slice(b * T, (b + 1) * T)
                low(x1l[:, :, s], chunked(TM), x1h[:, :, s]).then_inc(x1_split, 1)

            def weights_low(n, raw, hi, lo):
                dve.wait_ge(w_hi, n)
                low(lo[:], raw, hi[:]).then_inc(w_lo, 1)

            def cx_low(b):
                dve.wait_ge(cx_hi, b + 1)
                s = slice(b * T, (b + 1) * T)
                low(cxl[:, :, s], chunked(XQ[b % 2]), cxh[:, :, s]).then_inc(cx_split, 1)

            def keys_low(g, blk):
                src, half = block_of(blk)
                dve.wait_ge(xk_hi, g * NKV + blk + 1)
                at = (slice(None), slice(4 * half, 4 * half + 4), slice(src * T, (src + 1) * T))
                low(kl[at], chunked(KV_BANK["k", blk]), kh[at]).then_inc(xk_split, 1)

            def values_low(g, blk):
                src, half = block_of(blk)
                dve.wait_ge(xv_hi, g * NKV + blk + 1)
                at = (slice(None), slice(4 * half, 4 * half + 4), src)
                low(vl[at], chunked(KV_BANK["t", blk]), vh[at]).then_inc(xv_split, 1)

            def kv_step(g, kind, blk):
                if kind != "v":
                    {"k": keys_low, "t": values_low}[kind](g, blk)

            def queries_low(g, h, j):
                dve.wait_ge(xq_hi, g * NQ + 2 * h + j + 1)
                low(xql[:, h % 2, j, :], XQ[j][:], xqh[:, h % 2, j, :]).then_inc(xq_split, 1)

            def cross_max(g, u):
                dve.wait_ge(xs_done, g * NU + u + 1)
                if u >= 2:
                    dve.wait_ge(xexp_done, g * NU + u - 1)
                link(dve.tensor_reduce(xmax[:, u % 2, 0, :], SC[:, u % 2, :].rearrange("p (j k) -> p j k", j=2),
                                       AX_X, ALU.max))
                dve.tensor_scalar(xmax[:, u % 2, 1, :], xmax[:, u % 2, 0, :], -XSCALE, None, ALU.mult)\
                   .then_inc(xmax_ready, 1)

            def cross_norm(g, u):
                dve.wait_ge(xexp_done, g * NU + u + 1)
                link(dve.reciprocal(xsum[:, u % 2, 1, :], xsum[:, u % 2, 0, :]))
                for j in range(2):
                    last = dve.tensor_scalar(xp[:, u % 2, j, :], xp[:, u % 2, j, :], xsum[:, u % 2, 1, j:j + 1], None,
                                             ALU.mult)
                last.then_inc(xp_normed, 1)

            def cross_pt_low(g, u):
                dve.wait_ge(xpt_hi, g * NU + u + 1)
                low(xptl[:], XT[:].rearrange("p (c n) -> p c n", c=2), xpth[:]).then_inc(xpt_split, 1)

            def cross_o_low(g, u):
                dve.wait_ge(xo_hi, g * NU + u + 1)
                low(xol[:], XO[:, 0:2 * T], xoh[:]).then_inc(xo_split, 1)

            def cross_add(g, u):
                dve.wait_ge(xy_ready, g * NU + u + 1)
                dve.tensor_tensor(y[:, u % B, :], XY[u % 2][:], y[:, u % B, :], ALU.add).then_inc(xy_added, 1)

            def tile_stats(b, added, count):
                dve.wait_ge(added, count)
                return dve.bn_stats(stats[:, b, :], y[:, b, :])

            def moments(first, n):
                for b in range(first, first + n):
                    last = dve.bn_aggr(meanvar[:, b, :], stats[:, b, :])
                link(last)

            def scales(first, n):
                return rsqrt(n, meanvar[:, first:first + n, 1])

            def normalize(b, scale, done):
                dve.tensor_scalar(y[:, b, :], y[:, b, :], meanvar[:, b, 0:1], scale,
                                  ALU.subtract, ALU.mult).then_inc(done, 1)

            def x2_low(b):
                dve.wait_ge(x2_hi, b + 1)
                s = slice(b * T, (b + 1) * T)
                low(x1l[:, :, s], chunked(FX[b % 2]), x1h[:, :, s]).then_inc(x2_split, 1)

            def dve_units(g, last):
                for u in range(NU):
                    if u + 1 < NU:
                        cross_max(g, u + 1)
                    cross_pt_low(g, u)
                    if u + 1 < NU:
                        cross_norm(g, u + 1)
                    if u >= LATE:
                        if not last:
                            for kind, blk in KV_STEPS[u]:
                                kv_step(g + 1, kind, blk)
                    elif (u + AHEAD) % 2 == 1:
                        queries_low(g, (u + AHEAD) // 4, (u + AHEAD) % 4 // 2)
                    if u >= 1:
                        cross_add(g, u - 1)
                    if last and u > NU - B:
                        done = u - 1 - (NU - B)
                        if done < HB:
                            ins = tile_stats(done, xy_added, g * NU + u)
                        if done == HB - 1:
                            link(ins)
                            moments(0, HB)
                        elif done == HB:
                            rsqrt_guess(HB, meanvar[:, 0:HB, 1])
                            rsqrt_steps(HB, (2,))
                        elif done == HB + 1:
                            scale = rsqrt_steps(HB, (1, 0))
                            normalize(0, scale[:, 0:1], x2_normed)
                        elif done == HB + 2:
                            normalize(1, scale[:, 1:2], x2_normed)
                            normalize(2, scale[:, 2:3], x2_normed)
                    cross_o_low(g, u)
                if last:
                    x2_low(0)
                    normalize(3, scale[:, 3:4], x2_normed)
                    x2_low(1)
                cross_add(g, NU - 1)

            def rest_of_projections(g):
                queries_low(g, 0, 0)
                kv_step(g, "t", 2)
                queries_low(g, 0, 1)
                kv_step(g, "k", 3)
                cross_max(g, 0)
                cross_norm(g, 0)
                kv_step(g, "t", 3)

            def dve_group(g):
                links[0], chain[0] = chain_base + g * 2 * NU, 0
                dve_units(g, last=False)
                rest_of_projections(g + 1)

            x_low(0)
            for c in range(C):
                dve.wait_ge(wq_hi, c + 1)
                low(wql[:, c, :], wq_raw[:, c, :], wqh[:, c, :]).then_inc(wq_split, 1)
            weights_low(1, wkv_raw, wkvh, wkvl)
            dve.wait_ge(consts_in, 32)
            rope_q(0)
            rope_k(0)
            dve.wait_ge(q_hi, 1)
            dve.wait_ge(roped_q, 1)
            low(qs[:, :, 1, :, :], roped[:, 0:H, :].unsqueeze(2).to_broadcast([P, H, 2, HD]), qs[:, :, 0, :, :])\
               .then_inc(q_lo, 1)
            dve.wait_ge(k_hi, 1)
            dve.wait_ge(roped_k, 1)
            low(ks[:, :, :, 1, :], roped[:, H:, :].unsqueeze(2).to_broadcast([P, KV, 4, HD]), ks[:, :, :, 0, :])\
               .then_inc(k_lo, 1)
            stack_copy(0)
            x_low(1)
            maxima(0)
            dve.wait_ge(xres_in, 16)
            for b in range(B):
                n = UN * b
                if b >= 1:
                    set_attn(n - 1)
                maxima(n + 1)
                if b >= 2:
                    layer_norm(b - 2)
                if b + 1 == B:
                    cx_low(0)
                    cx_low(1)
                if b == 0:
                    weights_low(3, wo_raw, woh, wol)

                set_attn(n)
                if b >= 2:
                    norm_low(b - 2)
                if b + 1 == B:
                    cx_low(2)
                maxima(n + 2)
                if b >= 1:
                    attn_low(b - 1)
                if b + 1 < B:
                    rope_q(b + 1)
                    rope_k(b + 1)
                else:
                    cx_low(3)

                set_attn(n + 1)
                if b >= 1:
                    add_residual(b - 1)
                if b + 1 == B:
                    cx_low(4)
                    cx_low(5)
                maxima(n + 3)
                if b + 1 < B:
                    stack_copy(b + 1)
                else:
                    cx_low(6)

                set_attn(n + 2)
                if b + 1 == B:
                    cx_low(7)
                if b + 1 < B:
                    maxima(n + 4)
                if b >= 1:
                    tile_moments(b - 1)
                if b + 2 < B:
                    x_low(b + 2)
            layer_norm(B - 2)
            kv_step(0, "k", 0)
            set_attn(UN * B - 1)
            norm_low(B - 2)
            attn_low(B - 1)
            kv_step(0, "k", 1)
            add_residual(B - 1)
            tile_moments(B - 1)
            kv_step(0, "t", 0)
            layer_norm(B - 1)
            kv_step(0, "t", 1)
            norm_low(B - 1)
            kv_step(0, "k", 2)
            dve.wait_ge(y_set, B)
            rest_of_projections(0)
            chain_base = chain[0]
            loop(dve, 0, XG - 1, dve_group)
            links[0], chain[0] = chain_base + (XG - 1) * 2 * NU, 0
            dve_units(XG - 1, last=True)

            def expert_rows(half):
                t = slice(half * HB, (half + 1) * HB)
                dve.wait_ge(ag_copied, (half + 1) * HB)
                for b in range(B)[t]:
                    last = dve.max(top[:, b, :], lowg[:, b, ER:])
                link(last)
                dve.tensor_tensor(share[:, 0, t], top[:, t, 1], top[:, t, 0], ALU.subtract).then_inc(top_ready, 1)
                for b in range(B)[t]:
                    last = dve.max_index(topi[:, b, :], top[:, b, :], lowg[:, b, ER:])
                link(last)
                link(dve.tensor_copy(topf[:, t], topi[:, t, 0:TOPK]))
                dve.wait_ge(top_exp, half + 1)
                link(dve.tensor_scalar(share[:, 2, t], share[:, 1, t], 1.0, 1.0 / SCALING, ALU.add, ALU.mult))
                link(dve.reciprocal(share[:, 2, t], share[:, 2, t]))
                dve.tensor_tensor(share[:, 3, t], share[:, 1, t], share[:, 2, t], ALU.mult)
                iota = consts[:, C_IOTA:C_IOTA + E].unsqueeze(1).to_broadcast([P, HB, E])
                for i in range(TOPK):
                    last = dve.tensor_tensor(gates[:, i, t], iota, topf[:, t, i].unsqueeze(2).to_broadcast([P, HB, E]),
                                             ALU.is_equal)
                link(last)
                for i in range(TOPK):
                    last = dve.tensor_tensor(gates[:, i, t], gates[:, i, t],
                                             share[:, 2 + i, t].unsqueeze(2).to_broadcast([P, HB, E]), ALU.mult)
                link(last)
                link(dve.tensor_tensor(gates[:, 0, t], gates[:, 0, t], gates[:, 1, t], ALU.add))
                dve.tensor_tensor(wlow[:, t, :].rearrange("p b (e r) -> p b e r", e=E),
                                  lowg[:, t, 0:ER].rearrange("p b (e r) -> p b e r", e=E),
                                  gates[:, 0, t, :].unsqueeze(3).to_broadcast([P, HB, E, R]), ALU.mult)\
                   .then_inc(wlow_set, 1)

            def lw_low(b):
                dve.wait_ge(lw_hi, b + 1)
                low(lwl[:, b % 2, :], FX[b % 2][:, 0:P], lwh[:, b % 2, :]).then_inc(lw_split, 1)

            def add_residual_2(b):
                dve.wait_ge(ff_ready, b + 1)
                dve.wait_ge(x2_kept, b + 1)
                dve.tensor_tensor(y[:, b, :], FY[b % 4], y[:, b, :], ALU.add).then_inc(ff_added, 1)

            def last_norm(first, n):
                scale = scales(first, n)
                for i in range(n):
                    normalize(first + i, scale[:, i:i + 1], out_set)

            tile_stats(4, xy_added, XG * NU - 3)
            tile_stats(5, xy_added, XG * NU - 2)
            x2_low(2)
            tile_stats(6, xy_added, XG * NU - 1)
            link(tile_stats(7, xy_added, XG * NU))
            x2_low(3)
            moments(HB, HB)
            scale = scales(HB, HB)
            for b in range(HB, B):
                normalize(b, scale[:, b - HB:b - HB + 1], x2_normed)
            expert_rows(0)
            for b in range(HB, B):
                x2_low(b)
            lw_low(0)
            lw_low(1)
            add_residual_2(0)
            lw_low(2)
            add_residual_2(1)
            lw_low(3)
            tile_stats(0, ff_added, 1)
            tile_stats(1, ff_added, 2)
            expert_rows(1)
            add_residual_2(2)
            tile_stats(2, ff_added, 3)
            add_residual_2(3)
            link(tile_stats(3, ff_added, 4))
            moments(0, HB)
            scale = scales(0, HB)
            lw_low(HB)
            lw_low(HB + 1)
            normalize(0, scale[:, 0:1], out_set)
            normalize(1, scale[:, 1:2], out_set)
            add_residual_2(4)
            lw_low(6)
            add_residual_2(5)
            lw_low(7)
            tile_stats(4, ff_added, 5)
            normalize(2, scale[:, 2:3], out_set)
            add_residual_2(6)
            tile_stats(5, ff_added, 6)
            normalize(3, scale[:, 3:4], out_set)
            add_residual_2(7)
            tile_stats(6, ff_added, 7)
            link(tile_stats(7, ff_added, 8))
            moments(HB, HB)
            last_norm(HB, HB)


_NAMES = ["x", "ctx_4096", "L0_attn_Wq", "L0_attn_Wk", "L0_attn_Wv", "L0_attn_Wo", "L0_xattn_Wq", "L0_xattn_Wk",
          "L0_xattn_Wv", "L0_xattn_Wo", "L0_ffn_gate_w", "L0_ffn_base_w", "L0_ffn_base_b", "L0_ffn_lora_A",
          "L0_ffn_lora_B"]


def _tables(np):
    inv = (1.0 / np.float32(500000.0) ** (np.arange(0, HD, 2, dtype=np.float32) / np.float32(HD))).astype(np.float32)
    angle = np.arange(T, dtype=np.float32)[:, None] * inv[None, :]
    cos, sin = np.cos(angle), np.sin(angle)
    iota = np.broadcast_to(np.arange(E, dtype=np.float32), (T, E))
    table = np.concatenate([cos, cos, sin, -sin, iota], axis=1).astype(np.float32)
    row = np.arange(T)
    mask = np.where(row[None, :] > row[:, None], np.float32(-1e30), np.float32(0.0)).astype(np.float32)
    return np.ascontiguousarray(table), np.ascontiguousarray(mask)


def kernel(**inputs):
    import numpy as np
    import concourse.bacc as bacc
    from concourse.bass_utils import run_bass_kernel_spmd

    nc = bacc.Bacc("TRN2", target_bir_lowering=False, num_devices=1)
    arrays, args = {}, []
    table, mask = _tables(np)
    for name, a in [(n, inputs[n]) for n in _NAMES] + [("table", table), ("mask", mask)]:
        a = np.ascontiguousarray(a)
        arrays[f"in_{name}"] = a
        args.append(nc.dram_tensor(f"in_{name}", a.shape, F32, kind="ExternalInput").ap())
    o = nc.dram_tensor("out_0", (B, T, D), F32, kind="ExternalOutput").ap()
    post_ln_decoder(nc, *args, o)
    r = run_bass_kernel_spmd(nc, [arrays], core_ids=[0])
    return r.results[0]["out_0"]
```

```python
from contextlib import ExitStack

import concourse.bass as bass
from concourse import mybir

F32 = mybir.dt.float32
F32R = mybir.dt.float32r
BF16 = mybir.dt.bfloat16
I32 = mybir.dt.int32
U32 = mybir.dt.uint32
ALU = mybir.AluOpType
ACT = mybir.ActivationFunctionType
AX_X = mybir.AxisListType.X

P = 128
B, T, D = 8, 128, 512
C = D // P
H, KV, HD = 32, 8, 16
GS = H // KV
HALF = HD // 2
KD = KV * HD
UN = 4
UH = H // UN
VW = HD + 2
XH, XG, XD = 32, 4, 128
XHG = XH // XG
PAIRS = XHG // 2
XSCALE = float(XD) ** -0.5
KEYS = 2 * T
E, R, TOPK = 8, 16, 2
ER = E * R
SCALING = 2.0
EPS = 1e-5
GUESS = float(0x5F3759DF - (3 << 23) + (1 << 23) - (1 << 31))

C_COS, C_SIN, C_NSIN, C_IOTA = 0, HD, HD + HALF, HD + 2 * HALF
C_N = C_IOTA + E


def post_ln_decoder(nc, x, context, sa_wq, sa_wk, sa_wv, sa_wo, xa_wq, xa_wk, xa_wv, xa_wo,
                    gate_w, base_w, base_b, lora_a, lora_b, table, mask, out):
    with ExitStack() as ctx:
        def sbuf(name, shape, dt=F32, scope=ctx):
            return scope.enter_context(nc.sbuf_tensor(name, shape, dt))

        def sem(name):
            return ctx.enter_context(nc.semaphore(name))

        bank = [ctx.enter_context(nc.psum_tensor(f"bank{i}", [P, 512], F32)) for i in range(6)]
        score_banks = ctx.enter_context(nc.psum_tensor("score_banks", [P, 2, 512], F32))

        y = sbuf("y", [P, B, D])
        x1h = sbuf("x1h", [P, C, B * T], F32R)
        x1l = sbuf("x1l", [P, C, B * T], F32R)
        ident = sbuf("ident", [P, P])
        identb = sbuf("identb", [P, P], BF16)
        consts = sbuf("consts", [P, C_N])
        one = sbuf("one", [P, 1])
        maskb = sbuf("maskb", [P, P], BF16)
        maskf = sbuf("maskf", [P, P])
        stats = sbuf("stats", [P, B, 6])
        meanvar = sbuf("meanvar", [P, B, 2])
        newton = sbuf("newton", [P, 5, B])

        xwq_raw = sbuf("xwq_raw", [P, C, 2 * XD])
        xwo_raw = sbuf("xwo_raw", [P, 2, D])
        xwkv_raw = sbuf("xwkv_raw", [P, C, 2 * XD])
        xwkvh = sbuf("xwkvh", [P, C, 2 * XD], F32R)
        xwkvl = sbuf("xwkvl", [P, C, 2 * XD], F32R)
        cx_raw = sbuf("cx_raw", [P, 2, D])
        vfm = sbuf("vfm", [P, 2, 4 * T])

        pa = ExitStack()
        wqh = sbuf("wqh", [P, C, D], F32R, pa)
        wql = sbuf("wql", [P, C, D], F32R, pa)
        wkvh = sbuf("wkvh", [P, C, 2 * KD], F32R, pa)
        wkvl = sbuf("wkvl", [P, C, 2 * KD], F32R, pa)
        wraw = sbuf("wraw", [P, C * (2 * D + 2 * KD)], F32, pa)
        wq_raw = wraw[:, 0:C * D].rearrange("p (c n) -> p c n", c=C)
        wkv_raw = wraw[:, C * D:C * (D + 2 * KD)].rearrange("p (c n) -> p c n", c=C)
        wo_raw = wraw[:, C * (D + 2 * KD):].rearrange("p (c n) -> p c n", c=C)
        xin = sbuf("xin", [P, D], F32, pa)
        xth = sbuf("xth", [P, C, T], F32R, pa)
        xtl = sbuf("xtl", [P, C, T], F32R, pa)
        rot1 = sbuf("rot1", [P, H + KV, HD], F32, pa)
        rot2 = sbuf("rot2", [P, H + KV, HD], F32, pa)
        roped = sbuf("roped", [P, H + KV, HD], F32, pa)
        qs = sbuf("qs", [P, H, 2, 2, HD], F32R, pa)
        ks = sbuf("ks", [P, KV, 4, 2, HD], F32R, pa)
        vnext = sbuf("vnext", [P, KV, HD], F32, pa)
        qt = sbuf("qt", [P, H // 2, T], F32R, pa)
        kt = sbuf("kt", [P, KV, T], F32R, pa)
        woh = sbuf("woh", [P, C, D], F32R, pa)
        wol = sbuf("wol", [P, C, D], F32R, pa)
        vaug = sbuf("vaug", [P, KV, VW], F32, pa)
        probs = sbuf("probs", [P, 2, UH, T], F32, pa)
        pt = sbuf("pt", [P, UH, T], F32, pa)
        nmax = sbuf("nmax", [P, 2, 2, UH], F32, pa)
        rsum = sbuf("rsum", [P, UH], F32, pa)
        attn = sbuf("attn", [P, D], F32, pa)
        ath = sbuf("ath", [P, C, T], F32R, pa)
        atl = sbuf("atl", [P, C, T], F32R, pa)
        xpre = sbuf("xpre", [P, D], F32, pa)
        xnorm = sbuf("xnorm", [P, D], F32, pa)
        pa.close()

        pb = ExitStack()
        cxh = sbuf("cxh", [P, C, B * T], F32R, pb)
        cxl = sbuf("cxl", [P, C, B * T], F32R, pb)
        kh = sbuf("kh", [P, B, KEYS], F32R, pb)
        kl = sbuf("kl", [P, B, KEYS], F32R, pb)
        vh = sbuf("vh", [P, B, 2, XD], F32R, pb)
        vl = sbuf("vl", [P, B, 2, XD], F32R, pb)
        xwq = sbuf("xwq", [P, 2, 2, C, 2 * XD], F32R, pb)
        xwqh, xwql = xwq[:, :, 0], xwq[:, :, 1]
        xwoh = sbuf("xwoh", [P, 2, 2, D], F32R, pb)
        xwol = sbuf("xwol", [P, 2, 2, D], F32R, pb)
        xqh = sbuf("xqh", [P, 2, 2, 4 * T], F32R, pb)
        xql = sbuf("xql", [P, 2, 2, 4 * T], F32R, pb)
        xp = sbuf("xp", [P, 2, 2, KEYS], F32, pb)
        xpth = sbuf("xpth", [P, 2, 2 * T], F32R, pb)
        xptl = sbuf("xptl", [P, 2, 2 * T], F32R, pb)
        xoh = sbuf("xoh", [P, 2 * T], F32R, pb)
        xol = sbuf("xol", [P, 2 * T], F32R, pb)
        xmax = sbuf("xmax", [P, 2, 2, 2], F32, pb)
        xsum = sbuf("xsum", [P, 2, 2, 2], F32, pb)
        pb.close()

        pc = ExitStack()
        gate_raw = sbuf("gate_raw", [E, D], F32, pc)
        bias = sbuf("bias", [P, D], F32, pc)
        bwh = sbuf("bwh", [P, C, D], F32R, pc)
        bwl = sbuf("bwl", [P, C, D], F32R, pc)
        agh = sbuf("agh", [P, C, ER + E], F32R, pc)
        agl = sbuf("agl", [P, C, ER + E], F32R, pc)
        lbh = sbuf("lbh", [P, D], F32R, pc)
        lbl = sbuf("lbl", [P, D], F32R, pc)
        lwh = sbuf("lwh", [P, 2, P], F32R, pc)
        lwl = sbuf("lwl", [P, 2, P], F32R, pc)
        lowg = sbuf("lowg", [P, B, ER + E], F32, pc)
        wlow = sbuf("wlow", [P, B, ER], F32, pc)
        top = sbuf("top", [P, B, 8], F32, pc)
        topi = sbuf("topi", [P, B, 8], U32, pc)
        topf = sbuf("topf", [P, B, TOPK], F32, pc)
        share = sbuf("share", [P, 4, B], F32, pc)
        gates = sbuf("gates", [P, TOPK, B, E], F32, pc)
        pc.close()
        base_raw = (xwq_raw[:].rearrange("p c n -> p (c n)"), xwo_raw[:].rearrange("p c n -> p (c n)"))
        lora_raw = xwkv_raw[:].rearrange("p c n -> p (c n)")
        la_raw, lb_raw = lora_raw[:, 0:D], lora_raw[:, D:2 * D]

        consts_in = sem("consts_in")
        ident_made = sem("ident_made")
        wq_in, wkv_in, wo_in = [sem(f"wq_in{c}") for c in range(C)], sem("wkv_in"), sem("wo_in")
        w_hi, w_lo, wq_hi, wq_split = sem("w_hi"), sem("w_lo"), sem("wq_hi"), sem("wq_split")
        x_in, xres_in = sem("x_in"), sem("xres_in")
        xt_ready, xt_hi, xt_split = sem("xt_ready"), sem("xt_hi"), sem("xt_split")
        q_ready, kv_ready = sem("q_ready"), sem("kv_ready")
        roped_q, roped_k, q_hi, k_hi, q_lo, k_lo = (sem(n) for n in ("roped_q", "roped_k", "q_hi", "k_hi", "q_lo", "k_lo"))
        v_copied, v_set = sem("v_copied"), sem("v_set")
        stack_ready, stack_act, stack_dve = sem("stack_ready"), sem("stack_act"), sem("stack_dve")
        scores_ready, max_ready, exp_done = sem("scores_ready"), sem("max_ready"), sem("exp_done")
        pt_ready, pt_copied = sem("pt_ready"), sem("pt_copied")
        pv_ready, attn_set = sem("pv_ready"), sem("attn_set")
        at_ready, at_hi, at_split = sem("at_ready"), sem("at_hi"), sem("at_split")
        proj_ready, y_added, normed, y_set = sem("proj_ready"), sem("y_added"), sem("normed"), sem("y_set")
        x1_ready, x1_split = sem("x1_ready"), sem("x1_split")
        dve_chain = sem("dve_chain")
        xwq_in, xwo_in, xwkv_in = sem("xwq_in"), sem("xwo_in"), sem("xwkv_in")
        xw_hi, xwq_split, xwo_split, xwkv_split = sem("xw_hi"), sem("xwq_split"), sem("xwo_split"), sem("xwkv_split")
        cx_in = (sem("cx_in0"), sem("cx_in1"))
        cx_ready, cx_hi, cx_split = sem("cx_ready"), sem("cx_hi"), sem("cx_split")
        k_done, v_done, xk_hi, xk_split = sem("k_done"), sem("v_done"), sem("xk_hi"), sem("xk_split")
        vfm_copied, vt_ready, xv_hi, xv_split = sem("vfm_copied"), sem("vt_ready"), sem("xv_hi"), sem("xv_split")
        xq_done, xq_hi, xq_split = sem("xq_done"), sem("xq_hi"), sem("xq_split")
        xs_done, xmax_ready, xexp_done, xp_normed = sem("xs_done"), sem("xmax_ready"), sem("xexp_done"), sem("xp_normed")
        xpt_ready, xpt_hi, xpt_split = sem("xpt_ready"), sem("xpt_hi"), sem("xpt_split")
        xo_ready, xo_hi, xo_split = sem("xo_ready"), sem("xo_hi"), sem("xo_split")
        xy_ready, xy_added = sem("xy_ready"), sem("xy_added")
        base_in, lora_in, gate_in, bias_in = sem("base_in"), sem("lora_in"), sem("gate_in"), sem("bias_in")
        fw_ready, fw_kept, fw_hi, fw_split = sem("fw_ready"), sem("fw_kept"), sem("fw_hi"), sem("fw_split")
        x2_normed, x2_ready, x2_hi, x2_split, x2_kept = (sem(n) for n in ("x2_normed", "x2_ready", "x2_hi", "x2_split", "x2_kept"))
        ag_ready, ag_copied = sem("ag_ready"), sem("ag_copied")
        top_ready, top_exp, wlow_set = sem("top_ready"), sem("top_exp"), sem("wlow_set")
        lw_ready, lw_hi, lw_split = sem("lw_ready"), sem("lw_hi"), sem("lw_split")
        ff_ready, ff_added, out_set = sem("ff_ready"), sem("ff_added"), sem("out_set")
        stored = sem("stored")
        block = ctx.enter_context(nc.Block())

        TM, QB, KVB, CT, TP = bank[0], bank[1], bank[2], bank[3], (bank[4], bank[5])
        SC, STACK = score_banks, (QB, KVB, TM)

        XQ, XT, XO, XY = (bank[1], bank[2]), bank[0], bank[3], (bank[4], bank[5])

        FX, FG, FY = (XQ[1], XQ[0]), (XT, XO), (SC[:, 0, :], SC[:, 1, :], bank[4][:], bank[5][:])

        NU = PAIRS * B
        NQ = 4 * PAIRS
        NKV = 4
        AHEAD = 5
        NF = C + 3
        HB = B // 2
        LATE = 2 * NQ - AHEAD
        KV_STEPS = {LATE: (("k", 0),), LATE + 1: (("v", 0),), LATE + 2: (("k", 1), ("t", 0)), LATE + 3: (("v", 1),),
                    LATE + 4: (("t", 1), ("k", 2))}
        KV_BANK = {("k", 0): XQ[0], ("k", 1): XQ[0], ("k", 2): XQ[0], ("k", 3): XQ[0],
                   ("v", 0): XQ[1], ("v", 1): XQ[0], ("v", 2): XQ[1], ("v", 3): XQ[1],
                   ("t", 0): XQ[1], ("t", 1): XQ[1], ("t", 2): XT, ("t", 3): XO}
        FW_STEPS = {LATE: (0,), LATE + 1: (1,), LATE + 2: (2, 3), LATE + 3: (4, 5), LATE + 4: (6,)}

        def before(b, n):
            return isinstance(b, int) and b < n

        def batches(eng, body):
            body(0, 0)
            body(1, 1)
            with eng.Fori(2, B - 2) as b:
                body(b, 2)
            body(B - 2, B - 2)
            body(B - 1, B - 1)

        def unit(b, k):
            return (b + k // UN, k % UN) if k // UN else (b, k)

        def block_of(blk):
            return blk % 2, blk // 2

        def loop(eng, first, end, body):
            with eng.Fori(first, end) as i:
                body(i)

        def chunked(ap):
            return ap[:, :].rearrange("p (c n) -> p c n", c=C)

        def y_tile(b):
            return y[:, bass.ds(b, 1), :].rearrange("p o n -> p (o n)")

        def tile(ap, b):
            return ap[bass.ds(b, 1), :, :].rearrange("o t n -> (o t) n")

        @block.sync
        def _(sp):
            sp.dma_start(xin[:], tile(x, 0)).then_inc(x_in, 16)
            for c in range(C):
                sp.dma_start(wq_raw[:, c, :], sa_wq[c * P:(c + 1) * P, :]).then_inc(wq_in[c], 16)
            sp.dma_start(consts[:], table).then_inc(consts_in, 16)
            sp.dma_start(maskf[:], mask).then_inc(consts_in, 16)
            sp.dma_start(wkv_raw[:, :, 0:KD], sa_wk.rearrange("(c p) n -> p c n", p=P)).then_inc(wkv_in, 16)
            sp.dma_start(wkv_raw[:, :, KD:], sa_wv.rearrange("(c p) n -> p c n", p=P)).then_inc(wkv_in, 16)
            sp.dma_start(wo_raw, sa_wo.rearrange("(c p) n -> p c n", p=P)).then_inc(wo_in, 16)
            sp.dma_start(y[:], x.rearrange("b t n -> t b n")).then_inc(xres_in, 16)

            def load_x(b):
                sp.wait_ge(xt_ready, b)
                sp.dma_start(xin[:], tile(x, b)).then_inc(x_in, 16)

            loop(sp, 1, B, load_x)

            def load_pair(pair):
                sp.dma_start(xwq_raw[:], xa_wq.rearrange("(c p) n -> p c n", p=P)[:, :, bass.ds(pair * 2 * XD, 2 * XD)])\
                  .then_inc(xwq_in, 16)
                sp.dma_start(xwo_raw[:], xa_wo.rearrange("(h d) n -> d h n", d=XD)[:, bass.ds(pair * 2, 2), :])\
                  .then_inc(xwo_in, 16)

            def load_kv(g):
                for j, w in enumerate((xa_wk, xa_wv)):
                    sp.dma_start(xwkv_raw[:, :, j * XD:(j + 1) * XD],
                                 w.rearrange("(c p) n -> p c n", p=P)[:, :, bass.ds(g * XD, XD)]).then_inc(xwkv_in, 16)

            load_kv(0)
            load_pair(0)
            for b in range(B):
                if b >= 2:
                    sp.wait_ge(cx_ready, b - 1)
                sp.dma_start(cx_raw[:, b % 2, :], tile(context, b)).then_inc(cx_in[b % 2], 16)

            def pair_loads(g, pairs):
                for p in pairs:
                    sp.wait_ge(xwo_split, g * PAIRS + p)
                    load_pair(g * PAIRS + p)

            def sp_group(g):
                sp.wait_ge(xwkv_split, g + 1)
                load_kv(g + 1)
                pair_loads(g, range(1, PAIRS + 1))

            loop(sp, 0, XG - 1, sp_group)
            sp.wait_ge(xwkv_split, XG)
            sp.dma_start(la_raw, lora_a.rearrange("e r n -> (e r) n")).then_inc(lora_in, 16)
            for c in range(C):
                sp.dma_start(lb_raw[:, c * ER:(c + 1) * ER].rearrange("p (e r) -> p e r", e=E),
                             lora_b[:, c * P:(c + 1) * P, :].rearrange("e p r -> p e r")).then_inc(lora_in, 16)
            sp.wait_ge(v_done, XG * NKV)
            sp.dma_start(gate_raw[:], gate_w).then_inc(gate_in, 16)
            sp.dma_start(bias[:], base_b.rearrange("(o n) -> o n", o=1).to_broadcast([P, D])).then_inc(bias_in, 16)
            pair_loads(XG - 1, range(1, PAIRS))
            sp.wait_ge(xwo_split, XG * PAIRS)
            for i, raw in enumerate(base_raw):
                sp.dma_start(raw.rearrange("p (c n) -> p c n", c=2),
                             base_w[2 * i * P:2 * (i + 1) * P, :].rearrange("(c p) n -> p c n", p=P)).then_inc(base_in, 16)
            for b in range(B):
                sp.wait_ge(out_set, b + 1)
                sp.dma_start(tile(out, b), y[:, b, :]).then_inc(stored, 16)
            sp.wait_ge(stored, 16 * B)

        @block.gpsimd
        def _(pool):
            pool.memset(ident[:], 0.0).then_inc(ident_made, 1)
            pool.memset(vaug[:], 0.0).then_inc(ident_made, 1)
            pool.memset(one[:], 1.0).then_inc(ident_made, 1)
            pool.wait_ge(ident_made, 3)
            pool.affine_select(out=ident[:], in_=ident[:], compare_op=ALU.not_equal, fill=1.0, base=0,
                               pattern=[[-1, P]], channel_multiplier=1).then_inc(ident_made, 1)
            pool.memset(vaug[:, :, HD:HD + 1], 1.0).then_inc(ident_made, 1)
            pool.wait_ge(ident_made, 5)
            pool.tensor_copy(identb[:], ident[:]).then_inc(ident_made, 1)

            def low_parts(b):
                pool.wait_ge(q_hi, b + 1)
                pool.tensor_tensor(qs[:, :, 1, :, :], roped[:, 0:H, :].unsqueeze(2).to_broadcast([P, H, 2, HD]),
                                   qs[:, :, 0, :, :].bitcast(F32), ALU.subtract).then_inc(q_lo, 1)
                pool.wait_ge(k_hi, b + 1)
                pool.tensor_tensor(ks[:, :, :, 1, :], roped[:, H:, :].unsqueeze(2).to_broadcast([P, KV, 4, HD]),
                                   ks[:, :, :, 0, :].bitcast(F32), ALU.subtract).then_inc(k_lo, 1)

            def set_v(b):
                if not before(b, 1):
                    pool.wait_ge(pv_ready, UN * b)
                pool.wait_ge(v_copied, b + 1)
                pool.tensor_tensor(vaug[:, :, 0:HD], vnext[:], one[:].unsqueeze(2).to_broadcast([P, KV, HD]), ALU.mult).then_inc(v_set, 1)

            def keep_norm(b):
                pool.wait_ge(normed, b + 1)
                pool.tensor_tensor(y_tile(b), xnorm[:], one[:].to_broadcast([P, D]), ALU.mult).then_inc(y_set, 1)

            def split(raw, hi, lo, done):
                pool.tensor_tensor(hi, raw, one[:].unsqueeze(2).to_broadcast(raw.shape), ALU.mult).then_inc(xw_hi, 1)
                hi_count[0] += 1
                pool.wait_ge(xw_hi, hi_base[0] + hi_count[0])
                pool.tensor_tensor(lo, raw, hi.bitcast(F32), ALU.subtract).then_inc(done, 1)

            hi_base, hi_count = [0], [0]

            def split_kv(g):
                pool.wait_ge(xwkv_in, 32 * g + 32)
                split(xwkv_raw[:], xwkvh[:], xwkvl[:], xwkv_split)

            def split_pair(g, p, free=None, between=None):
                pair = g * PAIRS + p
                if free:
                    pool.wait_ge(xq_done, free[0] * NQ + 4 * (free[1] + 1))
                pool.wait_ge(xwq_in, 16 * pair + 16)
                split(xwq_raw[:], xwqh[:, p % 2], xwql[:, p % 2], xwq_split)
                if between:
                    between()
                    pool.wait_ge(x1_split, B)
                if free:
                    pool.wait_ge(xy_ready, free[0] * NU + B * (free[1] + 1))
                pool.wait_ge(xwo_in, 16 * pair + 16)
                split(xwo_raw[:], xwoh[:, p % 2], xwol[:, p % 2], xwo_split)

            def pool_group(g):
                hi_base[0], hi_count[0] = 5 + g * 9, 0
                pool.wait_ge(v_done, g * NKV + NKV)
                split_kv(g + 1)
                for p in (2, 3):
                    split_pair(g, p, (g, p - 2))
                for p in (0, 1):
                    split_pair(g + 1, p, (g, p + 2))

            set_v(0)

            def pool_batch(b, at):
                if at + 1 < B:
                    low_parts(b + 1)
                    set_v(b + 1)
                if at == B - 1:
                    split_kv(0)
                if at >= 1:
                    keep_norm(b - 1)

            batches(pool, pool_batch)
            pool.wait_ge(scores_ready, UN * B)
            split_pair(0, 0, between=lambda: keep_norm(B - 1))
            split_pair(0, 1)
            loop(pool, 0, XG - 1, pool_group)
            hi_base[0], hi_count[0] = 5 + (XG - 1) * 9, 0
            for p in (2, 3):
                split_pair(XG - 1, p, (XG - 1, p - 2))

            for i in range(NF):
                whole = vfm[:, i % 2, :]
                pool.wait_ge(fw_hi, i + 1)
                pool.wait_ge(fw_kept, i + 1)
                if i < C:
                    o, w, hi = bwl[:, i, :], whole, bwh[:, i, :]
                elif i == C:
                    o, w, hi = lbl[:], whole, lbh[:]
                elif i == C + 1:
                    o, w, hi = agl[:, :, 0:ER], whole.rearrange("p (c n) -> p c n", c=C), agh[:, :, 0:ER]
                else:
                    o, w, hi = agl[:, :, ER:], whole[:, 0:C * E].rearrange("p (c e) -> p c e", c=C), agh[:, :, ER:]
                pool.tensor_tensor(o, w, hi.bitcast(F32), ALU.subtract).then_inc(fw_split, 1)

            pool.wait_ge(bias_in, 16)
            for b in range(B):
                pool.wait_ge(x2_ready, b + 1)
                pool.tensor_tensor(y[:, b, :], y[:, b, :], bias[:], ALU.add).then_inc(x2_kept, 1)

        @block.tensor
        def _(pe):
            def three_passes(o, pairs, n):
                last = None
                for i, ((lh, ll), (rh, rl)) in enumerate(pairs):
                    pe.matmul(o, ll, rh, start=(i == 0), stop=False)
                    pe.matmul(o, lh, rl, start=False, stop=False)
                    last = pe.matmul(o, lh, rh, start=False, stop=(i == n - 1))
                return last

            def transpose4(dst, srcs):
                for j, s in enumerate(srcs):
                    last = pe.transpose(dst[:, j * P:(j + 1) * P], s, ident[:])
                return last

            def x_transpose(b):
                pe.wait_ge(x_in, 16 * (b + 1))
                if not before(b, 1):
                    pe.wait_ge(stack_act, 3 * b - 2)
                transpose4(QB, [xin[:, c * P:(c + 1) * P] for c in range(C)]).then_inc(xt_ready, 1)

            def project_q(b):
                pe.wait_ge(xt_split, b + 1)
                for c in range(C):
                    if before(b, 1):
                        pe.wait_ge(wq_split, c + 1)
                    pe.matmul(QB[:], xtl[:, c, :], wqh[:, c, :], start=(c == 0), stop=False)
                    pe.matmul(QB[:], xth[:, c, :], wql[:, c, :], start=False, stop=False)
                    last = pe.matmul(QB[:], xth[:, c, :], wqh[:, c, :], start=False, stop=(c == C - 1))
                last.then_inc(q_ready, 1)

            def project_kv(b):
                if not before(b, 1):
                    pe.wait_ge(stack_act, 3 * b - 1)
                three_passes(KVB[:, 0:2 * KD],
                             [((xth[:, c, :], xtl[:, c, :]), (wkvh[:, c, :], wkvl[:, c, :])) for c in range(C)],
                             C).then_inc(kv_ready, 1)

            def stack_transpose(b, groups):
                qf = qs[:].bitcast(F32).rearrange("p (j h) a e d -> p j (h a e d)", h=2)
                kf = ks[:].bitcast(F32).rearrange("p g a e d -> p g (a e d)")
                blocks = [qf[:, j, :] for j in range(H // 2)] + [kf[:, g, :] for g in range(KV)]
                for g in groups:
                    if g == 0:
                        pe.wait_ge(q_lo, b + 1)
                    if g == 1:
                        pe.wait_ge(roped_k, b + 1)
                    if g == 2 and before(b, 2) and b == 1:
                        pe.wait_ge(stack_act, 3)
                    if g == 2 and not before(b, 2):
                        pe.wait_ge(y_added, b - 1)
                    if g == 4:
                        pe.wait_ge(k_lo, b + 1)
                    if g >= 3:
                        pe.wait_ge(stack_dve, 3 * b + g - 2)
                    transpose4(STACK[g % 3], blocks[4 * g:4 * g + 4]).then_inc(stack_ready, 1)

            def scores(b, k):
                b, k = unit(b, k)
                n = UN * b + k
                if k == 0:
                    pe.wait_ge(stack_act, 3 * b + 2)
                    pe.wait_ge(stack_dve, 3 * b + 3)
                if k == 2:
                    pe.wait_ge(stack_act, 3 * b + 3)
                if not before(n, 1):
                    pe.wait_ge(exp_done, n)
                for odd in range(2):
                    pe.matmul(SC[:, odd, :], identb[:], maskb[:].unsqueeze(1).to_broadcast([P, 4, T]),
                              start=True, stop=False, skip_group_check=True)
                for i in range(UH // 2):
                    for odd in range(2):
                        h = UH * k + 2 * i + odd
                        rows = slice(64 * odd, 64 * odd + 64)
                        last = pe.matmul(SC[:, odd, i * T:(i + 1) * T], qt[rows, h // 2, :], kt[rows, h // GS, :],
                                         start=False, stop=True, skip_group_check=True)
                last.then_inc(scores_ready, 1)

            def probs_transpose(b, k):
                n = UN * b + k
                pe.wait_ge(exp_done, n + 1)
                for g in range(2):
                    if not before(n, 1):
                        pe.wait_ge(pt_copied, 2 * n - 1 + g)
                    transpose4(TP[g], [probs[:, k % 2, 4 * g + j, :] for j in range(4)]).then_inc(pt_ready, 1)

            def weigh_values(b, k):
                n = UN * b + k
                pe.wait_ge(pt_copied, 2 * n + 2)
                if k == 0:
                    pe.wait_ge(v_set, b + 1)
                if not before(n, 1):
                    pe.wait_ge(attn_set, n)
                for s in range(UH):
                    h = UH * k + 2 * (s % 4) + s // 4
                    last = pe.matmul(CT[:, s * VW:(s + 1) * VW], pt[:, s, :], vaug[:, h // GS, :],
                                     start=True, stop=True)
                last.then_inc(pv_ready, 1)

            def attn_transpose(b):
                pe.wait_ge(attn_set, UN * (b + 1))
                if before(b, 1):
                    pe.wait_ge(stack_act, 6)
                else:
                    pe.wait_ge(x1_split, b)
                transpose4(TM, [attn[:, c * P:(c + 1) * P] for c in range(C)]).then_inc(at_ready, 1)

            def project_out(b):
                pe.wait_ge(at_split, b + 1)
                three_passes(TM[:], [((ath[:, c, :], atl[:, c, :]), (woh[:, c, :], wol[:, c, :])) for c in range(C)],
                             C).then_inc(proj_ready, 1)

            def norm_transpose(b):
                pe.wait_ge(normed, b + 1)
                if not isinstance(b, int) or b + 2 < B:
                    pe.wait_ge(stack_act, 3 * b + 9)
                transpose4(TM, [xnorm[:, c * P:(c + 1) * P] for c in range(C)]).then_inc(x1_ready, 1)

            def cx_transpose(b):
                pe.wait_ge(cx_in[b % 2], 16 * (b // 2 + 1))
                if b < 2:
                    pe.wait_ge(stack_act, 3 * B - 2 + b)
                else:
                    pe.wait_ge(cx_split, b - 1)
                transpose4(XQ[b % 2], [cx_raw[:, b % 2, c * P:(c + 1) * P] for c in range(C)]).then_inc(cx_ready, 1)

            def passes(lh, ll, rh, rl):
                return [(ll, rh), (lh, rl), (lh, rh)]

            def run(o, ops, first=True, last=True):
                for i, (l, r) in enumerate(ops):
                    mm = pe.matmul(o, l, r, start=(first and i == 0), stop=(last and i == len(ops) - 1),
                                   skip_group_check=True)
                return mm

            def project_block(g, blk, j, bank_):
                src, half = block_of(blk)
                sh, sl = ((cxh, cxl), (x1h, x1l))[src]
                cols, toks = slice(j * XD, (j + 1) * XD), slice(half * 4 * T, (half + 1) * 4 * T)
                ops = []
                for c in range(C):
                    ops += passes(xwkvh[:, c, cols], xwkvl[:, c, cols], sh[:, c, toks], sl[:, c, toks])
                return run(bank_[:], ops)

            def kv_step(g, kind, blk):
                n, q = g * NKV, g * NQ
                if (kind, blk) == ("k", 0):
                    pe.wait_ge(xwkv_split, g + 1)
                if (kind, blk) in (("k", 0), ("v", 0)):
                    j = "kv".index(kind)
                    if before(g, 1):
                        pe.wait_ge(cx_split, B - 1 + j)
                    else:
                        pe.wait_ge(xq_split, q - 1 + j)
                elif kind == "k":
                    pe.wait_ge(*{1: (xk_split, n + 1), 2: (vfm_copied, n + 2), 3: (xq_split, q + 1)}[blk])
                elif kind == "v":
                    pe.wait_ge(*{1: (xk_split, n + 2), 2: (xv_split, n + 2), 3: (xq_split, q + 2)}[blk])
                else:
                    pe.wait_ge(vfm_copied, n + blk + 1)
                    if blk % 2 == 1:
                        pe.wait_ge(xv_split, n + blk)
                    if blk == 2 and before(g, 1):
                        pe.wait_ge(x1_split, B)
                if kind == "t":
                    transpose4(KV_BANK[kind, blk], [vfm[:, blk % 2, t * T:(t + 1) * T] for t in range(4)])\
                        .then_inc(vt_ready, 1)
                elif kind == "k":
                    project_block(g, blk, 0, KV_BANK[kind, blk]).then_inc(k_done, 1)
                else:
                    project_block(g, blk, 1, KV_BANK[kind, blk]).then_inc(v_done, 1)

            def project_queries(g, part):
                h, quarter = part // 4, part % 4
                j = quarter // 2
                toks = slice((h % 2) * 4 * T, (h % 2 + 1) * 4 * T)
                w = (h // 2) % 2
                if quarter == 0 and h % 2 == 0:
                    pe.wait_ge(xwq_split, g * PAIRS + h // 2 + 1)
                if quarter % 2 == 0:
                    if h >= 2:
                        pe.wait_ge(xq_split, g * NQ + 2 * (h - 1) + j + 1)
                    else:
                        pe.wait_ge((xk_split, vfm_copied)[j], g * NKV + 3 + h)
                ops = []
                for c in range(C):
                    cols = slice(j * XD, (j + 1) * XD)
                    ops += passes(xwqh[:, w, c, cols], xwql[:, w, c, cols], x1h[:, c, toks], x1l[:, c, toks])
                n = len(ops) // 2
                if quarter % 2 == 0:
                    run(XQ[j][:], ops[:n], last=False)
                else:
                    run(XQ[j][:], ops[n:], first=False).then_inc(xq_done, 1)

            def cross_scores(g, u):
                b, h = u % B, u // 4
                toks = slice((u % 4) * T, (u % 4 + 1) * T)
                if u % 4 == 0:
                    pe.wait_ge(xq_split, g * NQ + 2 * h + 2)
                if u in (0, 4):
                    pe.wait_ge(xk_split, g * NKV + (2 if u == 0 else NKV))
                if u >= 2:
                    pe.wait_ge(xexp_done, g * NU + u - 1)
                for j in range(2):
                    mm = run(SC[:, u % 2, j * KEYS:(j + 1) * KEYS],
                             passes(xqh[:, h % 2, j, toks], xql[:, h % 2, j, toks], kh[:, b, :], kl[:, b, :]))
                mm.then_inc(xs_done, 1)

            def cross_transpose(g, u):
                pe.wait_ge(xp_normed, g * NU + u + 1)
                if u >= 1:
                    pe.wait_ge(xpt_split, g * NU + u)
                else:
                    pe.wait_ge(xv_split, g * NKV + 3)
                transpose4(XT, [xp[:, u % 2, j, c * T:(c + 1) * T] for c in range(2) for j in range(2)])\
                    .then_inc(xpt_ready, 1)

            def cross_values(g, u):
                pe.wait_ge(xpt_split, g * NU + u + 1)
                if u >= 1:
                    pe.wait_ge(xo_split, g * NU + u)
                else:
                    pe.wait_ge(xv_split, g * NKV + NKV)
                ops = []
                for c in range(2):
                    ops += passes(vh[:, u % B, c, :], vl[:, u % B, c, :], xpth[:, c, :], xptl[:, c, :])
                run(XO[:, 0:2 * T], ops).then_inc(xo_ready, 1)

            def cross_out(g, u):
                w = (u // B) % 2
                pe.wait_ge(xo_split, g * NU + u + 1)
                if u % B == 0:
                    pe.wait_ge(xwo_split, g * PAIRS + u // B + 1)
                if u >= 2:
                    pe.wait_ge(xy_added, g * NU + u - 1)
                ops = []
                for j in range(2):
                    cols = slice(j * T, (j + 1) * T)
                    ops += passes(xoh[:, cols], xol[:, cols], xwoh[:, w, j, :], xwol[:, w, j, :])
                run(XY[u % 2][:], ops).then_inc(xy_ready, 1)

            def weights_transpose(i):
                if i < 2:
                    pe.wait_ge(xq_split, XG * NQ - 1 + i)
                else:
                    pe.wait_ge(fw_hi, i - 1)
                if i == 0:
                    pe.wait_ge(base_in, 32)
                if i == C:
                    pe.wait_ge(lora_in, 16 * (C + 1))
                if i < C:
                    srcs = [base_raw[oc // 2][:, (oc % 2) * D + i * P:(oc % 2) * D + (i + 1) * P] for oc in range(C)]
                elif i < C + 2:
                    srcs = [(lb_raw, la_raw)[i - C][:, c * P:(c + 1) * P] for c in range(C)]
                if i < C + 2:
                    transpose4(XQ[i % 2], srcs).then_inc(fw_ready, 1)
                    return
                pe.wait_ge(gate_in, 16)
                for c in range(C):
                    mm = pe.transpose(XQ[0][:, c * E:(c + 1) * E], gate_raw[:, c * P:(c + 1) * P], ident[0:E, 0:E])
                mm.then_inc(fw_ready, 1)

            def x2_transpose(b):
                pe.wait_ge(x2_normed, b + 1)
                if b >= 2:
                    pe.wait_ge(x2_split, b - 1)
                else:
                    pe.wait_ge(fw_hi, NF - 1 + b)
                transpose4(FX[b % 2], [y[:, b, c * P:(c + 1) * P] for c in range(C)]).then_inc(x2_ready, 1)

            def pe_units(g, last):
                for u in range(NU):
                    if u + 1 < NU:
                        cross_scores(g, u + 1)
                    cross_transpose(g, u)
                    if u < LATE:
                        project_queries(g, u + AHEAD)
                    elif last:
                        for i in FW_STEPS[u]:
                            weights_transpose(i)
                        if u == NU - 1:
                            x2_transpose(0)
                    else:
                        for kind, blk in KV_STEPS[u]:
                            kv_step(g + 1, kind, blk)
                    if u >= 1:
                        cross_out(g, u - 1)
                    cross_values(g, u)

            def rest_of_projections(g):
                project_queries(g, 0)
                project_queries(g, 1)
                kv_step(g, "t", 2)
                project_queries(g, 2)
                project_queries(g, 3)
                kv_step(g, "k", 3)
                cross_scores(g, 0)
                kv_step(g, "v", 3)
                project_queries(g, 4)
                kv_step(g, "t", 3)

            def pe_group(g):
                pe_units(g, last=False)
                kv_step(g + 1, "v", 2)
                cross_out(g, NU - 1)
                rest_of_projections(g + 1)
                pe.wait_ge(xy_added, g * NU + NU)

            pe.wait_ge(ident_made, 6)
            x_transpose(0)
            project_q(0)
            pe.wait_ge(w_lo, 1)
            project_kv(0)
            stack_transpose(0, range(5))
            x_transpose(1)
            stack_transpose(0, (5,))
            scores(0, 0)
            project_q(1)

            def pe_batch(b, at):
                scores(b, 1)
                probs_transpose(b, 0)
                if at + 1 < B:
                    if at >= 1:
                        project_q(b + 1)
                else:
                    cx_transpose(0)
                    cx_transpose(1)
                weigh_values(b, 0)
                if at >= 2:
                    norm_transpose(b - 2)
                if at + 1 == B:
                    cx_transpose(2)

                scores(b, 2)
                probs_transpose(b, 1)
                if at >= 1:
                    attn_transpose(b - 1)
                if at + 1 < B:
                    project_kv(b + 1)
                else:
                    cx_transpose(3)
                if at == 1:
                    pe.wait_ge(w_lo, 2)
                if at >= 1:
                    project_out(b - 1)
                if at + 1 == B:
                    cx_transpose(4)
                    cx_transpose(5)
                weigh_values(b, 1)

                scores(b, 3)
                probs_transpose(b, 2)
                if at + 1 < B:
                    stack_transpose(b + 1, range(5))
                else:
                    cx_transpose(6)
                    cx_transpose(7)
                weigh_values(b, 2)

                if at + 1 < B:
                    scores(b, 4)
                probs_transpose(b, 3)
                if at + 1 < B:
                    stack_transpose(b + 1, (5,))
                if at + 2 < B:
                    x_transpose(b + 2)
                if at + 1 == B:
                    kv_step(0, "k", 0)
                weigh_values(b, 3)

            batches(pe, pe_batch)
            norm_transpose(B - 2)
            kv_step(0, "v", 0)
            attn_transpose(B - 1)
            kv_step(0, "k", 1)
            project_out(B - 1)
            kv_step(0, "t", 0)
            kv_step(0, "v", 1)
            kv_step(0, "t", 1)
            norm_transpose(B - 1)
            kv_step(0, "k", 2)
            kv_step(0, "v", 2)
            rest_of_projections(0)
            loop(pe, 0, XG - 1, pe_group)
            pe_units(XG - 1, last=True)

            def tile_passes(b, wh, wl):
                toks = slice(b * T, (b + 1) * T)
                ops = []
                for c in range(C):
                    ops += passes(x1h[:, c, toks], x1l[:, c, toks], wh[:, c, :], wl[:, c, :])
                return ops

            def low_and_gate(b):
                pe.wait_ge(x2_split, b + 1)
                if b == 0:
                    pe.wait_ge(fw_split, NF)
                if b >= 2:
                    pe.wait_ge(ag_copied, b - 1)
                run(FG[b % 2][:, 0:ER + E], tile_passes(b, agh, agl)).then_inc(ag_ready, 1)

            def base(b):
                if b >= 4:
                    pe.wait_ge(ff_added, b - 3)
                elif b >= 2:
                    pe.wait_ge(xy_added, XG * NU - 3 + b)
                run(FY[b % 4], tile_passes(b, bwh, bwl), last=False)

            def low_transpose(b):
                pe.wait_ge(wlow_set, b // HB + 1)
                if b >= 2:
                    pe.wait_ge(lw_split, b - 1)
                pe.transpose(FX[b % 2][:, 0:P], wlow[:, b, :], ident[:]).then_inc(lw_ready, 1)

            def lora(b):
                pe.wait_ge(lw_split, b + 1)
                run(FY[b % 4], passes(lwh[:, b % 2, :], lwl[:, b % 2, :], lbh[:], lbl[:]), first=False)\
                    .then_inc(ff_ready, 1)

            def rows_of(tiles):
                for b in tiles:
                    low_and_gate(b)
                    if b + 2 in tiles:
                        x2_transpose(b + 2)

            x2_transpose(1)
            cross_out(XG - 1, NU - 1)
            rows_of(range(HB))
            for b in range(HB - 1):
                base(b)
            x2_transpose(HB)
            x2_transpose(HB + 1)
            base(HB - 1)
            rows_of(range(HB, B))
            pe.wait_ge(x2_split, B)
            low_transpose(0)
            low_transpose(1)
            lora(0)
            low_transpose(2)
            lora(1)
            low_transpose(3)
            base(4)
            lora(2)
            base(5)
            lora(3)
            base(6)
            low_transpose(4)
            low_transpose(5)
            base(7)
            for b in range(HB, B):
                lora(b)
                if b + 2 < B:
                    low_transpose(b + 2)

        @block.scalar
        def _(act):
            def copy(o, i):
                return act.activation(o, i, ACT.Copy)

            def split_weights(n, raw, hi, loaded, count):
                act.wait_ge(loaded, count)
                copy(hi[:], raw).then_inc(w_hi, 1)

            def x_high(b):
                act.wait_ge(xt_ready, b + 1)
                copy(xth[:], chunked(QB)).then_inc(xt_hi, 1)

            def stack_high(b):
                act.wait_ge(roped_q, b + 1)
                copy(qs[:, :, 0, :, :], roped[:, 0:H, :].unsqueeze(2).to_broadcast([P, H, 2, HD])).then_inc(q_hi, 1)
                act.wait_ge(roped_k, b + 1)
                copy(ks[:, :, :, 0, :], roped[:, H:, :].unsqueeze(2).to_broadcast([P, KV, 4, HD])).then_inc(k_hi, 1)

            def copy_v(b):
                act.wait_ge(kv_ready, b + 1)
                if not before(b, 1):
                    act.wait_ge(v_set, b)
                copy(vnext[:], KVB[:, KD:2 * KD].rearrange("p (g d) -> p g d", g=KV)).then_inc(v_copied, 1)

            def stack_copy(b, groups):
                for g in groups:
                    dst = {3: qt[:, 12:16, :], 4: kt[:, 0:4, :], 5: kt[:, 4:8, :]}[g]
                    act.wait_ge(stack_ready, 6 * b + g + 1)
                    copy(dst, chunked(STACK[g % 3])).then_inc(stack_act, 1)

            def exponentials(b, k):
                b, k = unit(b, k)
                n = UN * b + k
                act.wait_ge(max_ready, n + 1)
                if not before(n, 2):
                    act.wait_ge(pt_ready, 2 * (n - 1))
                for s in range(UH):
                    last = act.activation(probs[:, k % 2, s, :], SC[:, s // 4, (s % 4) * T:(s % 4 + 1) * T], ACT.Exp,
                                          bias=nmax[:, k % 2, 1, s:s + 1], scale=HD ** -0.5)
                last.then_inc(exp_done, 1)

            def pt_copy(b, k):
                n = UN * b + k
                for g in range(2):
                    act.wait_ge(pt_ready, 2 * n + g + 1)
                    copy(pt[:, 4 * g:4 * g + 4, :], chunked(TP[g])).then_inc(pt_copied, 1)

            def attn_high(b):
                act.wait_ge(at_ready, b + 1)
                copy(ath[:], chunked(TM)).then_inc(at_hi, 1)

            def cx_high(b):
                act.wait_ge(cx_ready, b + 1)
                copy(cxh[:, :, b * T:(b + 1) * T], chunked(XQ[b % 2])).then_inc(cx_hi, 1)

            def keys_high(g, blk):
                src, half = block_of(blk)
                act.wait_ge(k_done, g * NKV + blk + 1)
                copy(kh[:, 4 * half:4 * half + 4, src * T:(src + 1) * T], chunked(KV_BANK["k", blk])).then_inc(xk_hi, 1)

            def values_copy(g, blk):
                act.wait_ge(v_done, g * NKV + blk + 1)
                if blk >= 2:
                    act.wait_ge(vt_ready, g * NKV + blk - 1)
                copy(vfm[:, blk % 2, :], KV_BANK["v", blk][:]).then_inc(vfm_copied, 1)

            def values_high(g, blk):
                src, half = block_of(blk)
                act.wait_ge(vt_ready, g * NKV + blk + 1)
                copy(vh[:, 4 * half:4 * half + 4, src, :], chunked(KV_BANK["t", blk])).then_inc(xv_hi, 1)

            def kv_step(g, kind, blk):
                {"k": keys_high, "v": values_copy, "t": values_high}[kind](g, blk)

            def queries_high(g, h, j):
                act.wait_ge(xq_done, g * NQ + 2 * h + j + 1)
                copy(xqh[:, h % 2, j, :], XQ[j][:]).then_inc(xq_hi, 1)

            def cross_exp(g, u):
                act.wait_ge(xmax_ready, g * NU + u + 1)
                if u >= 2:
                    act.wait_ge(xpt_ready, g * NU + u - 1)
                for j in range(2):
                    last = act.activation(xp[:, u % 2, j, :], SC[:, u % 2, j * KEYS:(j + 1) * KEYS], ACT.Exp,
                                          bias=xmax[:, u % 2, 1, j:j + 1], scale=XSCALE,
                                          accum_out=xsum[:, u % 2, 0, j:j + 1])
                last.then_inc(xexp_done, 1)

            def cross_pt_high(g, u):
                act.wait_ge(xpt_ready, g * NU + u + 1)
                copy(xpth[:], XT[:].rearrange("p (c n) -> p c n", c=2)).then_inc(xpt_hi, 1)

            def cross_o_high(g, u):
                act.wait_ge(xo_ready, g * NU + u + 1)
                copy(xoh[:], XO[:, 0:2 * T]).then_inc(xo_hi, 1)

            def weights_high(i):
                act.wait_ge(fw_ready, i + 1)
                if i >= 2:
                    act.wait_ge(fw_split, i - 1)
                wide = C * E if i == C + 2 else D
                copy(vfm[:, i % 2, 0:wide], XQ[i % 2][:, 0:wide]).then_inc(fw_kept, 1)
                if i < C:
                    copy(bwh[:, i, :], XQ[i % 2][:]).then_inc(fw_hi, 1)
                elif i == C:
                    copy(lbh[:], XQ[0][:]).then_inc(fw_hi, 1)
                elif i == C + 1:
                    copy(agh[:, :, 0:ER], chunked(XQ[1])).then_inc(fw_hi, 1)
                else:
                    copy(agh[:, :, ER:], XQ[0][:, 0:C * E].rearrange("p (c e) -> p c e", c=C)).then_inc(fw_hi, 1)

            def x2_high(b):
                act.wait_ge(x2_ready, b + 1)
                copy(x1h[:, :, b * T:(b + 1) * T], chunked(FX[b % 2])).then_inc(x2_hi, 1)

            def act_units(g, last):
                for u in range(NU):
                    cross_pt_high(g, u)
                    if u + 1 < NU:
                        cross_exp(g, u + 1)
                    if u >= LATE:
                        if last:
                            for i in FW_STEPS[u]:
                                weights_high(i)
                            if u == NU - 1:
                                x2_high(0)
                        else:
                            for kind, blk in KV_STEPS[u]:
                                kv_step(g + 1, kind, blk)
                    elif (u + AHEAD) % 2 == 1:
                        queries_high(g, (u + AHEAD) // 4, (u + AHEAD) % 4 // 2)
                    cross_o_high(g, u)

            def rest_of_projections(g):
                kv_step(g, "v", 2)
                queries_high(g, 0, 0)
                kv_step(g, "t", 2)
                queries_high(g, 0, 1)
                kv_step(g, "k", 3)
                cross_exp(g, 0)
                kv_step(g, "v", 3)
                kv_step(g, "t", 3)

            def act_group(g):
                act_units(g, last=False)
                rest_of_projections(g + 1)

            x_high(0)
            for c in range(C):
                act.wait_ge(wq_in[c], 16)
                copy(wqh[:, c, :], wq_raw[:, c, :]).then_inc(wq_hi, 1)
            split_weights(1, wkv_raw, wkvh, wkv_in, 32)
            act.wait_ge(consts_in, 32)
            copy(maskb[:], maskf[:]).then_inc(w_hi, 1)
            copy_v(0)
            stack_high(0)
            split_weights(2, wo_raw, woh, wo_in, 16)
            stack_copy(0, (3, 4))
            x_high(1)
            stack_copy(0, (5,))
            exponentials(0, 0)

            def act_batch(b, at):
                pt_copy(b, 0)
                if at + 1 == B:
                    cx_high(0)
                exponentials(b, 1)
                if at + 1 == B:
                    cx_high(1)
                if at + 1 == B:
                    cx_high(2)

                pt_copy(b, 1)
                if at >= 1:
                    attn_high(b - 1)
                if at + 1 == B:
                    cx_high(3)
                exponentials(b, 2)
                if at + 1 < B:
                    copy_v(b + 1)
                    stack_high(b + 1)
                else:
                    cx_high(4)
                    cx_high(5)

                pt_copy(b, 2)
                exponentials(b, 3)
                if at + 1 < B:
                    stack_copy(b + 1, (3, 4))
                else:
                    cx_high(6)
                    cx_high(7)

                pt_copy(b, 3)
                if at + 1 < B:
                    exponentials(b, 4)
                    stack_copy(b + 1, (5,))
                if at + 2 < B:
                    x_high(b + 2)

            batches(act, act_batch)
            kv_step(0, "k", 0)
            kv_step(0, "v", 0)
            attn_high(B - 1)
            kv_step(0, "k", 1)
            kv_step(0, "t", 0)
            kv_step(0, "v", 1)
            kv_step(0, "t", 1)
            kv_step(0, "k", 2)
            rest_of_projections(0)
            loop(act, 0, XG - 1, act_group)
            act_units(XG - 1, last=True)

            def gates_of(half):
                act.wait_ge(top_ready, half + 1)
                s = slice(half * HB, (half + 1) * HB)
                act.activation(share[:, 1, s], share[:, 0, s], ACT.Exp).then_inc(top_exp, 1)

            for half in range(2):
                tiles = range(half * HB, (half + 1) * HB)
                if half == 1:
                    x2_high(tiles[0])
                x2_high(tiles[1])
                for b in tiles:
                    act.wait_ge(ag_ready, b + 1)
                    copy(lowg[:, b, :], FG[b % 2][:, 0:ER + E]).then_inc(ag_copied, 1)
                    if b + 2 in tiles:
                        x2_high(b + 2)
                if half == 0:
                    gates_of(half)
            for b in range(B):
                if b == HB:
                    gates_of(1)
                act.wait_ge(lw_ready, b + 1)
                if b >= 2:
                    act.wait_ge(ff_ready, b - 1)
                copy(lwh[:, b % 2, :], FX[b % 2][:, 0:P]).then_inc(lw_hi, 1)

        @block.vector
        def _(dve):
            chain, links = [0], [0]

            def link(ins):
                chain[0] += 1
                ins.then_inc(dve_chain, 1)
                dve.wait_ge(dve_chain, links[0] + chain[0])

            def low(o, whole, high):
                return dve.tensor_tensor(o, whole, high.bitcast(F32), ALU.subtract)

            def x_low(b):
                dve.wait_ge(xt_hi, b + 1)
                low(xtl[:], chunked(QB), xth[:]).then_inc(xt_split, 1)

            def rope(b, src, lo, hi, ready, done, others):
                heads = hi - lo
                v = src.rearrange("p (h d) -> p h d", h=heads)
                cos = consts[:, C_COS:C_COS + HD].unsqueeze(1).to_broadcast([P, heads, HD])
                nsin = consts[:, C_NSIN:C_NSIN + HALF].unsqueeze(1).to_broadcast([P, heads, HALF])
                sin = consts[:, C_SIN:C_SIN + HALF].unsqueeze(1).to_broadcast([P, heads, HALF])
                dve.wait_ge(ready, b + 1)
                for s in others:
                    if not before(b, 1):
                        dve.wait_ge(s, b)
                dve.tensor_tensor(rot1[:, lo:hi, :], v, cos, ALU.mult)
                dve.tensor_tensor(rot2[:, lo:hi, 0:HALF], v[:, :, HALF:], nsin, ALU.mult)
                link(dve.tensor_tensor(rot2[:, lo:hi, HALF:], v[:, :, 0:HALF], sin, ALU.mult))
                dve.tensor_tensor(roped[:, lo:hi, :], rot1[:, lo:hi, :], rot2[:, lo:hi, :], ALU.add).then_inc(done, 1)

            def rope_q(b):
                rope(b, QB[:], 0, H, q_ready, roped_q, (q_lo,))

            def rope_k(b):
                dve.wait_ge(v_copied, b + 1)
                rope(b, KVB[:, 0:KD], H, H + KV, kv_ready, roped_k, (k_lo,))

            def stack_copy(b):
                for g in range(3):
                    dve.wait_ge(stack_ready, 6 * b + g + 1)
                    dve.tensor_copy(qt[:, 4 * g:4 * g + 4, :], chunked(STACK[g])).then_inc(stack_dve, 1)

            def maxima(b, k):
                b, k = unit(b, k)
                n = UN * b + k
                dve.wait_ge(scores_ready, n + 1)
                if not before(n, 2):
                    dve.wait_ge(exp_done, n - 1)
                link(dve.tensor_reduce(nmax[:, k % 2, 0, :].rearrange("p (o i) -> p o i", o=2),
                                       SC[:].rearrange("p o (i t) -> p o i t", i=4), AX_X, ALU.max))
                dve.tensor_scalar(nmax[:, k % 2, 1, :], nmax[:, k % 2, 0, :], -HD ** -0.5, None,
                                  ALU.mult).then_inc(max_ready, 1)

            def set_attn(b, k):
                n = UN * b + k
                dve.wait_ge(pv_ready, n + 1)
                pv = CT[:, 0:UH * VW].rearrange("p (s v) -> p s v", s=UH)
                link(dve.reciprocal(rsum[:], pv[:, :, HD]))
                for odd in range(2):
                    o = attn[:, k * UH * HD:(k + 1) * UH * HD].rearrange("p (i o d) -> p o i d", o=2, d=HD)[:, odd]
                    last = dve.tensor_tensor(o, pv[:, 4 * odd:4 * odd + 4, 0:HD],
                                             rsum[:, 4 * odd:4 * odd + 4].unsqueeze(2).to_broadcast([P, 4, HD]), ALU.mult)
                last.then_inc(attn_set, 1)

            def attn_low(b):
                dve.wait_ge(at_hi, b + 1)
                low(atl[:], chunked(TM), ath[:]).then_inc(at_split, 1)

            def add_residual(b):
                dve.wait_ge(proj_ready, b + 1)
                dve.tensor_tensor(xpre[:], TM[:], y_tile(b), ALU.add).then_inc(y_added, 1)

            def rsqrt_guess(n, var):
                a, r = newton[:, 3, 0:n], newton[:, 4, 0:n]
                for i, s in enumerate((4.0, 16.0, 64.0)):
                    last = dve.tensor_scalar(newton[:, i, 0:n], var, EPS, s, ALU.add, ALU.mult)
                link(last)
                link(dve.tensor_scalar(a.bitcast(I32), newton[:, 0, 0:n].bitcast(I32), 1, None, ALU.logical_shift_right))
                link(dve.tensor_scalar(r.bitcast(I32), a.bitcast(I32), -1.0, GUESS, ALU.mult, ALU.add))

            def rsqrt_steps(n, steps):
                a, r = newton[:, 3, 0:n], newton[:, 4, 0:n]
                for i in steps:
                    if n == 1:
                        link(dve.scalar_tensor_tensor(a, r, newton[:, i, 0:1], r, ALU.mult, ALU.mult))
                    else:
                        link(dve.tensor_tensor(a, r, r, ALU.mult))
                        link(dve.tensor_tensor(a, a, newton[:, i, 0:n], ALU.mult))
                    link(dve.scalar_tensor_tensor(r, a, -3.0, r, ALU.add, ALU.mult))
                return r

            def rsqrt(n, var):
                rsqrt_guess(n, var)
                return rsqrt_steps(n, (2, 1, 0))

            def row_stats(b):
                dve.wait_ge(y_added, b + 1)
                link(dve.bn_stats(stats[:, 0, :], xpre[:]))

            def row_moments():
                link(dve.bn_aggr(meanvar[:, 0, :], stats[:, 0, :]))
                rsqrt_guess(1, meanvar[:, 0, 1:2])

            def layer_norm(b):
                r = rsqrt_steps(1, (2, 1, 0))
                if not before(b, 1):
                    dve.wait_ge(x1_ready, b)
                    dve.wait_ge(y_set, b)
                dve.tensor_scalar(xnorm[:], xpre[:], meanvar[:, 0, 0:1], r, ALU.subtract, ALU.mult).then_inc(normed, 1)

            def norm_split(b):
                dve.wait_ge(x1_ready, b + 1)
                at = (slice(None), slice(None), bass.ds(b * T, T))
                link(dve.tensor_tensor(x1h[at], chunked(TM), one[:].unsqueeze(2).to_broadcast([P, C, T]), ALU.mult))
                low(x1l[at], chunked(TM), x1h[at]).then_inc(x1_split, 1)

            def weights_low(n, raw, hi, lo):
                dve.wait_ge(w_hi, n)
                low(lo[:], raw, hi[:]).then_inc(w_lo, 1)

            def cx_low(b):
                dve.wait_ge(cx_hi, b + 1)
                s = slice(b * T, (b + 1) * T)
                low(cxl[:, :, s], chunked(XQ[b % 2]), cxh[:, :, s]).then_inc(cx_split, 1)

            def keys_low(g, blk):
                src, half = block_of(blk)
                dve.wait_ge(xk_hi, g * NKV + blk + 1)
                at = (slice(None), slice(4 * half, 4 * half + 4), slice(src * T, (src + 1) * T))
                low(kl[at], chunked(KV_BANK["k", blk]), kh[at]).then_inc(xk_split, 1)

            def values_low(g, blk):
                src, half = block_of(blk)
                dve.wait_ge(xv_hi, g * NKV + blk + 1)
                at = (slice(None), slice(4 * half, 4 * half + 4), src)
                low(vl[at], chunked(KV_BANK["t", blk]), vh[at]).then_inc(xv_split, 1)

            def kv_step(g, kind, blk):
                if kind != "v":
                    {"k": keys_low, "t": values_low}[kind](g, blk)

            def queries_low(g, h, j):
                dve.wait_ge(xq_hi, g * NQ + 2 * h + j + 1)
                low(xql[:, h % 2, j, :], XQ[j][:], xqh[:, h % 2, j, :]).then_inc(xq_split, 1)

            def cross_max(g, u):
                dve.wait_ge(xs_done, g * NU + u + 1)
                if u >= 2:
                    dve.wait_ge(xexp_done, g * NU + u - 1)
                link(dve.tensor_reduce(xmax[:, u % 2, 0, :], SC[:, u % 2, :].rearrange("p (j k) -> p j k", j=2),
                                       AX_X, ALU.max))
                dve.tensor_scalar(xmax[:, u % 2, 1, :], xmax[:, u % 2, 0, :], -XSCALE, None, ALU.mult)\
                   .then_inc(xmax_ready, 1)

            def cross_norm(g, u):
                dve.wait_ge(xexp_done, g * NU + u + 1)
                link(dve.reciprocal(xsum[:, u % 2, 1, :], xsum[:, u % 2, 0, :]))
                for j in range(2):
                    last = dve.tensor_scalar(xp[:, u % 2, j, :], xp[:, u % 2, j, :], xsum[:, u % 2, 1, j:j + 1], None,
                                             ALU.mult)
                last.then_inc(xp_normed, 1)

            def cross_pt_low(g, u):
                dve.wait_ge(xpt_hi, g * NU + u + 1)
                low(xptl[:], XT[:].rearrange("p (c n) -> p c n", c=2), xpth[:]).then_inc(xpt_split, 1)

            def cross_o_low(g, u):
                dve.wait_ge(xo_hi, g * NU + u + 1)
                low(xol[:], XO[:, 0:2 * T], xoh[:]).then_inc(xo_split, 1)

            def cross_add(g, u):
                dve.wait_ge(xy_ready, g * NU + u + 1)
                dve.tensor_tensor(y[:, u % B, :], XY[u % 2][:], y[:, u % B, :], ALU.add).then_inc(xy_added, 1)

            def tile_stats(b, added, count):
                dve.wait_ge(added, count)
                return dve.bn_stats(stats[:, b, :], y[:, b, :])

            def moments(first, n):
                for b in range(first, first + n):
                    last = dve.bn_aggr(meanvar[:, b, :], stats[:, b, :])
                link(last)

            def scales(first, n):
                return rsqrt(n, meanvar[:, first:first + n, 1])

            def normalize(b, scale, done):
                dve.tensor_scalar(y[:, b, :], y[:, b, :], meanvar[:, b, 0:1], scale,
                                  ALU.subtract, ALU.mult).then_inc(done, 1)

            def x2_low(b):
                dve.wait_ge(x2_hi, b + 1)
                s = slice(b * T, (b + 1) * T)
                low(x1l[:, :, s], chunked(FX[b % 2]), x1h[:, :, s]).then_inc(x2_split, 1)

            def dve_units(g, last):
                for u in range(NU):
                    if u + 1 < NU:
                        cross_max(g, u + 1)
                    cross_pt_low(g, u)
                    if u + 1 < NU:
                        cross_norm(g, u + 1)
                    if u >= LATE:
                        if not last:
                            for kind, blk in KV_STEPS[u]:
                                kv_step(g + 1, kind, blk)
                    elif (u + AHEAD) % 2 == 1:
                        queries_low(g, (u + AHEAD) // 4, (u + AHEAD) % 4 // 2)
                    if u >= 1:
                        cross_add(g, u - 1)
                    if last and u > NU - B:
                        done = u - 1 - (NU - B)
                        if done < HB:
                            ins = tile_stats(done, xy_added, g * NU + u)
                        if done == HB - 1:
                            link(ins)
                            moments(0, HB)
                        elif done == HB:
                            rsqrt_guess(HB, meanvar[:, 0:HB, 1])
                            rsqrt_steps(HB, (2,))
                        elif done == HB + 1:
                            scale = rsqrt_steps(HB, (1, 0))
                            normalize(0, scale[:, 0:1], x2_normed)
                        elif done == HB + 2:
                            normalize(1, scale[:, 1:2], x2_normed)
                            normalize(2, scale[:, 2:3], x2_normed)
                    cross_o_low(g, u)
                if last:
                    x2_low(0)
                    normalize(3, scale[:, 3:4], x2_normed)
                    x2_low(1)
                cross_add(g, NU - 1)

            def rest_of_projections(g):
                queries_low(g, 0, 0)
                kv_step(g, "t", 2)
                queries_low(g, 0, 1)
                kv_step(g, "k", 3)
                cross_max(g, 0)
                cross_norm(g, 0)
                kv_step(g, "t", 3)

            def dve_group(g):
                links[0], chain[0] = chain_base + g * 2 * NU, 0
                dve_units(g, last=False)
                rest_of_projections(g + 1)

            x_low(0)
            for c in range(C):
                dve.wait_ge(wq_hi, c + 1)
                low(wql[:, c, :], wq_raw[:, c, :], wqh[:, c, :]).then_inc(wq_split, 1)
            weights_low(1, wkv_raw, wkvh, wkvl)
            dve.wait_ge(consts_in, 32)
            rope_q(0)
            rope_k(0)
            dve.wait_ge(q_hi, 1)
            dve.wait_ge(roped_q, 1)
            low(qs[:, :, 1, :, :], roped[:, 0:H, :].unsqueeze(2).to_broadcast([P, H, 2, HD]), qs[:, :, 0, :, :])\
               .then_inc(q_lo, 1)
            dve.wait_ge(k_hi, 1)
            dve.wait_ge(roped_k, 1)
            low(ks[:, :, :, 1, :], roped[:, H:, :].unsqueeze(2).to_broadcast([P, KV, 4, HD]), ks[:, :, :, 0, :])\
               .then_inc(k_lo, 1)
            stack_copy(0)
            x_low(1)
            maxima(0, 0)
            dve.wait_ge(xres_in, 16)

            LINKS = 4 * 2 + 2 + 2 + 9 + 1
            loop_base = [0]

            def dve_batch(b, at):
                if at == 2:
                    links[0], chain[0] = loop_base[0] + (b - 2) * LINKS, 0
                if at >= 1:
                    set_attn(b - 1, UN - 1)
                maxima(b, 1)
                if at >= 2:
                    layer_norm(b - 2)
                if at + 1 == B:
                    cx_low(0)
                    cx_low(1)
                if at == 0:
                    weights_low(3, wo_raw, woh, wol)

                if at >= 2:
                    norm_split(b - 2)
                if at + 1 == B:
                    cx_low(2)
                maxima(b, 2)
                if at >= 1:
                    attn_low(b - 1)
                set_attn(b, 0)
                if at + 1 < B:
                    rope_q(b + 1)
                    rope_k(b + 1)
                else:
                    cx_low(3)

                set_attn(b, 1)
                if at >= 1:
                    add_residual(b - 1)
                if at + 1 == B:
                    cx_low(4)
                    cx_low(5)
                maxima(b, 3)
                if at + 1 < B:
                    stack_copy(b + 1)
                else:
                    cx_low(6)

                set_attn(b, 2)
                if at + 1 == B:
                    cx_low(7)
                if at + 1 < B:
                    maxima(b, 4)
                if at >= 1:
                    row_stats(b - 1)
                if at + 2 < B:
                    x_low(b + 2)
                if at >= 1:
                    row_moments()
                if at == 1:
                    loop_base[0] = chain[0]
                if at == 2:
                    assert chain[0] == LINKS
                    links[0], chain[0] = 0, loop_base[0] + (B - 4) * LINKS

            batches(dve, dve_batch)
            layer_norm(B - 2)
            kv_step(0, "k", 0)
            set_attn(B - 1, UN - 1)
            norm_split(B - 2)
            attn_low(B - 1)
            kv_step(0, "k", 1)
            add_residual(B - 1)
            row_stats(B - 1)
            row_moments()
            kv_step(0, "t", 0)
            layer_norm(B - 1)
            kv_step(0, "t", 1)
            norm_split(B - 1)
            kv_step(0, "k", 2)
            dve.wait_ge(y_set, B)
            rest_of_projections(0)
            chain_base = chain[0]
            loop(dve, 0, XG - 1, dve_group)
            links[0], chain[0] = chain_base + (XG - 1) * 2 * NU, 0
            dve_units(XG - 1, last=True)

            def expert_rows(half):
                t = slice(half * HB, (half + 1) * HB)
                dve.wait_ge(ag_copied, (half + 1) * HB)
                for b in range(B)[t]:
                    last = dve.max(top[:, b, :], lowg[:, b, ER:])
                link(last)
                dve.tensor_tensor(share[:, 0, t], top[:, t, 1], top[:, t, 0], ALU.subtract).then_inc(top_ready, 1)
                for b in range(B)[t]:
                    last = dve.max_index(topi[:, b, :], top[:, b, :], lowg[:, b, ER:])
                link(last)
                link(dve.tensor_copy(topf[:, t], topi[:, t, 0:TOPK]))
                dve.wait_ge(top_exp, half + 1)
                link(dve.tensor_scalar(share[:, 2, t], share[:, 1, t], 1.0, 1.0 / SCALING, ALU.add, ALU.mult))
                link(dve.reciprocal(share[:, 2, t], share[:, 2, t]))
                dve.tensor_tensor(share[:, 3, t], share[:, 1, t], share[:, 2, t], ALU.mult)
                iota = consts[:, C_IOTA:C_IOTA + E].unsqueeze(1).to_broadcast([P, HB, E])
                for i in range(TOPK):
                    last = dve.tensor_tensor(gates[:, i, t], iota, topf[:, t, i].unsqueeze(2).to_broadcast([P, HB, E]),
                                             ALU.is_equal)
                link(last)
                for i in range(TOPK):
                    last = dve.tensor_tensor(gates[:, i, t], gates[:, i, t],
                                             share[:, 2 + i, t].unsqueeze(2).to_broadcast([P, HB, E]), ALU.mult)
                link(last)
                link(dve.tensor_tensor(gates[:, 0, t], gates[:, 0, t], gates[:, 1, t], ALU.add))
                dve.tensor_tensor(wlow[:, t, :].rearrange("p b (e r) -> p b e r", e=E),
                                  lowg[:, t, 0:ER].rearrange("p b (e r) -> p b e r", e=E),
                                  gates[:, 0, t, :].unsqueeze(3).to_broadcast([P, HB, E, R]), ALU.mult)\
                   .then_inc(wlow_set, 1)

            def lw_low(b):
                dve.wait_ge(lw_hi, b + 1)
                low(lwl[:, b % 2, :], FX[b % 2][:, 0:P], lwh[:, b % 2, :]).then_inc(lw_split, 1)

            def add_residual_2(b):
                dve.wait_ge(ff_ready, b + 1)
                dve.wait_ge(x2_kept, b + 1)
                dve.tensor_tensor(y[:, b, :], FY[b % 4], y[:, b, :], ALU.add).then_inc(ff_added, 1)

            def last_norm(first, n):
                scale = scales(first, n)
                for i in range(n):
                    normalize(first + i, scale[:, i:i + 1], out_set)

            tile_stats(4, xy_added, XG * NU - 3)
            tile_stats(5, xy_added, XG * NU - 2)
            x2_low(2)
            tile_stats(6, xy_added, XG * NU - 1)
            link(tile_stats(7, xy_added, XG * NU))
            x2_low(3)
            moments(HB, HB)
            scale = scales(HB, HB)
            for b in range(HB, B):
                normalize(b, scale[:, b - HB:b - HB + 1], x2_normed)
            expert_rows(0)
            for b in range(HB, B):
                x2_low(b)
            lw_low(0)
            lw_low(1)
            add_residual_2(0)
            lw_low(2)
            add_residual_2(1)
            lw_low(3)
            tile_stats(0, ff_added, 1)
            tile_stats(1, ff_added, 2)
            expert_rows(1)
            add_residual_2(2)
            tile_stats(2, ff_added, 3)
            add_residual_2(3)
            link(tile_stats(3, ff_added, 4))
            moments(0, HB)
            scale = scales(0, HB)
            lw_low(HB)
            lw_low(HB + 1)
            normalize(0, scale[:, 0:1], out_set)
            normalize(1, scale[:, 1:2], out_set)
            add_residual_2(4)
            lw_low(6)
            add_residual_2(5)
            lw_low(7)
            tile_stats(4, ff_added, 5)
            normalize(2, scale[:, 2:3], out_set)
            add_residual_2(6)
            tile_stats(5, ff_added, 6)
            normalize(3, scale[:, 3:4], out_set)
            add_residual_2(7)
            tile_stats(6, ff_added, 7)
            link(tile_stats(7, ff_added, 8))
            moments(HB, HB)
            last_norm(HB, HB)


_NAMES = ["x", "ctx_4096", "L0_attn_Wq", "L0_attn_Wk", "L0_attn_Wv", "L0_attn_Wo", "L0_xattn_Wq", "L0_xattn_Wk",
          "L0_xattn_Wv", "L0_xattn_Wo", "L0_ffn_gate_w", "L0_ffn_base_w", "L0_ffn_base_b", "L0_ffn_lora_A",
          "L0_ffn_lora_B"]


def _tables(np):
    inv = (1.0 / np.float32(500000.0) ** (np.arange(0, HD, 2, dtype=np.float32) / np.float32(HD))).astype(np.float32)
    angle = np.arange(T, dtype=np.float32)[:, None] * inv[None, :]
    cos, sin = np.cos(angle), np.sin(angle)
    iota = np.broadcast_to(np.arange(E, dtype=np.float32), (T, E))
    table = np.concatenate([cos, cos, sin, -sin, iota], axis=1).astype(np.float32)
    row = np.arange(T)
    mask = np.where(row[None, :] > row[:, None], np.float32(-1e30), np.float32(0.0)).astype(np.float32)
    return np.ascontiguousarray(table), np.ascontiguousarray(mask)


def kernel(**inputs):
    import numpy as np
    import concourse.bacc as bacc
    from concourse.bass_utils import run_bass_kernel_spmd

    nc = bacc.Bacc("TRN2", target_bir_lowering=False, num_devices=1)
    arrays, args = {}, []
    table, mask = _tables(np)
    for name, a in [(n, inputs[n]) for n in _NAMES] + [("table", table), ("mask", mask)]:
        a = np.ascontiguousarray(a)
        arrays[f"in_{name}"] = a
        args.append(nc.dram_tensor(f"in_{name}", a.shape, F32, kind="ExternalInput").ap())
    o = nc.dram_tensor("out_0", (B, T, D), F32, kind="ExternalOutput").ap()
    post_ln_decoder(nc, *args, o)
    r = run_bass_kernel_spmd(nc, [arrays], core_ids=[0])
    return r.results[0]["out_0"]
```
